# Optimizing a Trainium2 kernel written in Bass

```python
import numpy as np
import jax
import jax.numpy as jnp

def _softmax(x, axis=-1):
    return jax.nn.softmax(x, axis=axis)

def _gelu(x):
    return jax.nn.gelu(x, approximate=True)

def _silu(x):
    return jax.nn.silu(x)

def _sigmoid(x):
    return jax.nn.sigmoid(x)

def _layernorm(x, axis=-1, eps=1e-05):
    m = jnp.mean(x, axis=axis, keepdims=True)
    v = jnp.var(x, axis=axis, keepdims=True)
    return (x - m) / jnp.sqrt(v + eps)

def _scatter_add(tgt, idx, src, axis=0):
    return tgt.at[idx].add(src)

def _segment_sum(src, seg, n):
    return jax.ops.segment_sum(src, seg, n)
kernel_name = 'mk_flamingo_gated_d1_seqx_r2_c07e27'

def setup_inputs(seed: int=0):
    np.random.seed(seed)
    _w = jnp.asarray

    def _rec_inputs():
        import jax
        import jax.numpy as jnp
        _rk = jax.random.key(seed)
        x = -0.0002928 + 1 * jax.random.normal(jax.random.fold_in(_rk, 1), (32, 100, 512), jnp.float32)
        _lenS = 100 - jax.random.randint(jax.random.fold_in(_rk, 7), (32,), 0, max(1, 100 // 4) + 1, jnp.int32)
        _lenS2 = 722 - jax.random.randint(jax.random.fold_in(_rk, 8), (32,), 0, max(1, 722 // 4) + 1, jnp.int32)
        _ctx_1024P = jax.random.normal(jax.random.fold_in(_rk, 11), (32, 16, 512), jnp.float32)
        _ctx_1024c = jax.random.dirichlet(jax.random.fold_in(_rk, 511), 0.3 * jnp.ones((16,), jnp.float32), (32, 722))
        _ctx_1024t = jnp.einsum('bsk,bkd->bsd', _ctx_1024c, _ctx_1024P)
        _ctx_1024t = _ctx_1024t * jax.lax.rsqrt(jnp.mean(jnp.square(_ctx_1024t)) + 1e-12) * 0.953939
        ctx_1024 = -1.39393e-06 + 0.999914 * (_ctx_1024t + 0.3 * jax.random.normal(jax.random.fold_in(_rk, 611), (32, 722, 512), jnp.float32))
        _g = jax.random.normal(jax.random.fold_in(_rk, 9001), (2, 1), jnp.float32)
        _g = jnp.sign(_g) * jnp.maximum(jnp.abs(_g), 1.0) + (_g == 0) * 1.0
        g_xattn = _g[0]
        g_ffn = _g[1]
        return (x, ctx_1024, g_xattn, g_ffn)
    x, ctx_1024, g_xattn, g_ffn = _rec_inputs()

    def _L0_xattn_setup():
        import jax, jax.numpy as jnp
        import numpy as np
        B, S, DIM, H = (2, 1024, 512, 16)
        HD = DIM // H
        key = jax.random.key(seed)
        ks = jax.random.split(key, 11)
        s = 0.02
        return {'q': jax.random.normal(ks[0], (B, S, DIM), jnp.float32), 'k': jax.random.normal(ks[1], (B, S, DIM), jnp.float32), 'v': jax.random.normal(ks[2], (B, S, DIM), jnp.float32), 'wq': jax.random.normal(ks[3], (DIM, DIM), jnp.float32) * s, 'bq': jax.random.normal(ks[4], (DIM,), jnp.float32) * s, 'wk': jax.random.normal(ks[5], (DIM, DIM), jnp.float32) * s, 'bk': jax.random.normal(ks[6], (DIM,), jnp.float32) * s, 'wv': jax.random.normal(ks[7], (DIM, DIM), jnp.float32) * s, 'bv': jax.random.normal(ks[8], (DIM,), jnp.float32) * s, 'wo': jax.random.normal(ks[9], (DIM, DIM), jnp.float32) * s, 'bo': jax.random.normal(ks[10], (DIM,), jnp.float32) * s}
    _L0_xattn_all = _L0_xattn_setup()
    _L0_xattn_in = {k: v for k, v in _L0_xattn_all.items() if k in ('wq', 'bq', 'wk', 'bk', 'wv', 'bv', 'wo', 'bo')}
    del _L0_xattn_all

    def _L0_ffn_setup():
        import jax, jax.numpy as jnp
        import numpy as np
        B, N, C, H, REG = (1, 2309, 512, 16, 5)
        D = C // H
        key = jax.random.key(seed)
        k0, k1, k2, k3 = jax.random.split(key, 4)
        x = jax.random.normal(k0, (B, N, C), dtype=jnp.float32)
        g_info = jax.random.normal(k1, (12, 2, C), dtype=jnp.float32)
        W_qkv = jax.random.normal(k2, (C, 3 * C), dtype=jnp.float32) * 0.02
        W_proj = jax.random.normal(k3, (C, C), dtype=jnp.float32) * 0.02
        b_proj = jnp.zeros((C,), dtype=jnp.float32)
        return {'x': x, 'g_info': g_info, 'W_qkv': W_qkv, 'W_proj': W_proj, 'b_proj': b_proj}
    _L0_ffn_all = _L0_ffn_setup()
    _L0_ffn_in = {k: v for k, v in _L0_ffn_all.items() if k in ('g_info', 'W_qkv', 'W_proj', 'b_proj')}
    del _L0_ffn_all
    return {'x': x, 'ctx_1024': ctx_1024, 'g_xattn': g_xattn, 'g_ffn': g_ffn, 'L0_xattn_wq': _L0_xattn_in['wq'], 'L0_xattn_bq': _L0_xattn_in['bq'], 'L0_xattn_wk': _L0_xattn_in['wk'], 'L0_xattn_bk': _L0_xattn_in['bk'], 'L0_xattn_wv': _L0_xattn_in['wv'], 'L0_xattn_bv': _L0_xattn_in['bv'], 'L0_xattn_wo': _L0_xattn_in['wo'], 'L0_xattn_bo': _L0_xattn_in['bo'], 'L0_ffn_g_info': _L0_ffn_in['g_info'], 'L0_ffn_W_qkv': _L0_ffn_in['W_qkv'], 'L0_ffn_W_proj': _L0_ffn_in['W_proj'], 'L0_ffn_b_proj': _L0_ffn_in['b_proj']}

def reference(x, ctx_1024, g_xattn, g_ffn, L0_xattn_wq, L0_xattn_bq, L0_xattn_wk, L0_xattn_bk, L0_xattn_wv, L0_xattn_bv, L0_xattn_wo, L0_xattn_bo, L0_ffn_g_info, L0_ffn_W_qkv, L0_ffn_W_proj, L0_ffn_b_proj):
    import jax
    import jax.numpy as jnp

    def _L0_xattn_ref(q, k, v, wq, bq, wk, bk, wv, bv, wo, bo):
        import jax, jax.numpy as jnp
        import numpy as np
        B, S, DIM, H = (2, 1024, 512, 16)
        HD = DIM // H
        b, s, _ = k.shape
        qh = (q @ wq + bq).reshape(b, -1, H, HD).transpose(0, 2, 1, 3)
        kh = (k @ wk + bk).reshape(b, -1, H, HD).transpose(0, 2, 1, 3)
        vh = (v @ wv + bv).reshape(b, -1, H, HD).transpose(0, 2, 1, 3)
        scores = jax.nn.softmax(jnp.einsum('bhqd,bhkd->bhqk', qh, kh), axis=-1)
        attn = jnp.einsum('bhqk,bhkd->bhqd', scores, vh)
        concat = attn.transpose(0, 2, 1, 3).reshape(b, -1, H * HD)
        return concat @ wo + bo

    def _L0_ffn_ref(x, g_info, W_qkv, W_proj, b_proj):
        import jax, jax.numpy as jnp
        import numpy as np
        B, N, C, H, REG = (1, 2309, 512, 16, 5)
        D = C // H
        Bx, Nx, Cx = x.shape
        scale = D ** (-0.5)
        qkv = (x @ W_qkv).reshape(Bx, Nx, 3, H, D)
        q, k, v = (qkv[:, :, 0], qkv[:, :, 1], qkv[:, :, 2])
        g_layer = g_info[0].reshape(-1, H, D)
        q_g = g_layer[0]
        q_pure = q[:, REG:]
        q_n = q_pure / jnp.linalg.norm(q_pure, axis=-1, keepdims=True)
        qg_n = q_g / jnp.linalg.norm(q_g, axis=-1, keepdims=True)
        sim = (qg_n[None, None] * q_n).sum(-1).mean(-1)
        sim = (sim - sim.min()) / (sim.max() - sim.min())
        pos = sim > 0.9
        logits = jnp.einsum('bqhd,bkhd->bhqk', q * scale, k)

        def masked_attn(tok_mask):
            key_mask = jnp.concatenate([jnp.ones((Bx, REG), bool), tok_mask], axis=1)
            l = jnp.where(key_mask[:, None, None, :], logits, -jnp.inf)
            a = jax.nn.softmax(l, axis=-1)
            return jnp.einsum('bhqk,bkhd->bqhd', a, v)
        x_pos = masked_attn(pos)
        x_neg = masked_attn(~pos)
        reg_out = (x_pos[:, :REG] + x_neg[:, :REG]) * 0.5
        tok_out = jnp.where(pos[:, :, None, None], x_pos[:, REG:], x_neg[:, REG:])
        out = jnp.concatenate([reg_out, tok_out], axis=1).reshape(Bx, Nx, Cx)
        return out @ W_proj + b_proj
    x = x + jnp.tanh(g_xattn[0]) * _L0_xattn_ref(_layernorm(x, axis=-1), ctx_1024, ctx_1024, L0_xattn_wq, L0_xattn_bq, L0_xattn_wk, L0_xattn_bk, L0_xattn_wv, L0_xattn_bv, L0_xattn_wo, L0_xattn_bo)
    x = x + jnp.tanh(g_ffn[0]) * _L0_ffn_ref(_layernorm(x, axis=-1), L0_ffn_g_info, L0_ffn_W_qkv, L0_ffn_W_proj, L0_ffn_b_proj)
    return x

_drawn_inputs = setup_inputs


def setup_inputs(seed=0):
    import zlib

    import numpy as np

    out = dict(_drawn_inputs(seed))
    spreads = {'L0_ffn_b_proj': (0.0, 0.1)}
    factors = {'L0_xattn_bq': 31.881,
     'L0_xattn_bk': 64.0,
     'L0_xattn_bv': 8.0,
     'L0_xattn_bo': 3.616,
     'L0_ffn_g_info': 64.0}
    for name, (base, spread) in spreads.items():
        noise = np.random.default_rng([zlib.crc32(name.encode()), seed]).standard_normal(out[name].shape)
        drawn = base * np.exp(spread * noise) if base else spread * noise
        out[name] = jnp.asarray(drawn.astype(out[name].dtype))
    for name, factor in factors.items():
        out[name] = (out[name] * factor).astype(out[name].dtype)
    return out
```

```python
from contextlib import ExitStack

import numpy as np

import concourse.bass as bass
from concourse import mybir

F32 = mybir.dt.float32
F32R = mybir.dt.float32r
ALU = mybir.AluOpType
ACT = mybir.ActivationFunctionType
AX = mybir.AxisListType

P = 128
B, S, D = 32, 100, 512
C = 722
H, HD = 16, 32
KT = D // P
HPT = P // HD
REG = 5
ROWS = B * S
EPS = 1e-5
LOGIT_SCALE = HD ** -0.5
THRESHOLD = 0.9
MASKED = -1e30


class Tally:

    def __init__(self, sem, base=0):
        self.sem, self.base, self.n = sem, base, 0

    def done(self, instruction):
        instruction.then_inc(self.sem, 1)
        self.n += 1

    def wait(self, engine, back=0):
        engine.wait_ge(self.sem, self.base + (self.n - back))


class Memory:
    def __init__(self, nc, ctx, prefix):
        self.nc, self.ctx, self.prefix = nc, ctx, prefix

    def sb(self, name, shape, dt=F32):
        return self.ctx.enter_context(self.nc.sbuf_tensor(self.prefix + name, shape, dt))

    def ps(self, name, shape):
        return self.ctx.enter_context(self.nc.psum_tensor(self.prefix + name, shape, F32))

    def sem(self, name):
        return self.ctx.enter_context(self.nc.semaphore(self.prefix + name))


def f32(ap):
    return ap.bitcast(F32)


def repeated(ap, dim, times):
    shape = list(ap.shape)
    shape[dim] = times
    return ap.broadcast_to(shape)


def row_of(vector, partitions):
    return repeated(vector.rearrange("(a n) -> a n", a=1), 0, partitions)


def three_products(pe, out, left_hi, left_lo, right_hi, right_lo, first, last):
    pe.matmul(out, left_hi, right_hi, start=first, stop=False)
    pe.matmul(out, left_hi, right_lo, start=False, stop=False)
    return pe.matmul(out, left_lo, right_hi, start=False, stop=last)


GB = 4
GROUPS = B // GB
GS = GB * S


def stage_queries(nc, x, wq, bq, ident_dram, q_parts):
    with ExitStack() as ctx:
        m = Memory(nc, ctx, "q_")
        ident = m.sb("ident", [P, P])
        w_raw = m.sb("w_raw", [P, KT, D])
        w_hi, w_lo = m.sb("w_hi", [P, KT, D], F32R), m.sb("w_lo", [P, KT, D], F32R)
        bias = m.sb("bias", [P, KT])
        eps = m.sb("eps", [P, 1])
        rows = m.sb("rows", [S, GB, D])
        stats, moments = m.sb("stats", [S, GB, 6]), m.sb("moments", [S, GB, 2])
        std, rstd = m.sb("std", [S, GB]), m.sb("rstd", [S, GB])
        normed = m.sb("normed", [S, GB, D])
        xt_hi, xt_lo = m.sb("xt_hi", [P, KT, GS], F32R), m.sb("xt_lo", [P, KT, GS], F32R)
        q_hi, q_lo = m.sb("q_hi", [P, KT, GS], F32R), m.sb("q_lo", [P, KT, GS], F32R)
        bank = [m.ps(f"bank{i}", [P, 512]) for i in range(8)]
        turned, product = bank[:4], bank[4:]

        loaded, w_split, rows_in = m.sem("loaded"), m.sem("w_split"), m.sem("rows_in")
        eps_set, stats_seen = m.sem("eps_set"), m.sem("stats_seen")
        dve_step, act_std = m.sem("dve_step"), m.sem("act_std")
        normed_ready, turned_ready = m.sem("normed_ready"), m.sem("turned_ready")
        xt_hi_ready, xt_lo_ready = m.sem("xt_hi_ready"), m.sem("xt_lo_ready")
        product_ready = m.sem("product_ready")
        q_hi_ready, q_lo_ready, stored = m.sem("q_hi_ready"), m.sem("q_lo_ready"), m.sem("stored")

        block = ctx.enter_context(nc.Block())
        x_groups = x.rearrange("(g r) s d -> g s r d", r=GB)

        @block.sync
        def _(sp):
            sp.dma_start(rows[:], x_groups[0]).then_inc(rows_in, 16)
            sp.dma_start(w_raw[:], wq.rearrange("(k p) n -> p k n", p=P)).then_inc(loaded, 16)
            sp.dma_start(bias[:], bq.rearrange("(k p) -> p k", p=P), allow_slow_non_contiguous=True).then_inc(loaded, 16)
            sp.dma_start(ident[:], ident_dram).then_inc(loaded, 16)

            def store(g):
                sp.wait_ge(q_hi_ready, g * KT + KT)
                sp.wait_ge(q_lo_ready, g * KT + KT)
                for part, t in enumerate((q_hi, q_lo)):
                    dst = q_parts[part].rearrange("(k p) n -> p k n", p=P)
                    sp.dma_start(dst[:, :, bass.ds(g * GS, GS)], f32(t[:])).then_inc(stored, 16)

            with sp.Fori(0, GROUPS - 1) as g:
                sp.wait_ge(normed_ready, g + 1)
                sp.dma_start(rows[:], x_groups[g + 1]).then_inc(rows_in, 16)
                store(g)
            store(GROUPS - 1)
            sp.wait_ge(stored, 32 * GROUPS)

        @block.vector
        def _(dve):
            dve.memset(eps[:], EPS).then_inc(eps_set, 1)
            dve.wait_ge(loaded, 48)
            dve.wait_ge(w_split, 1)
            dve.tensor_tensor(w_lo[:], w_raw[:], w_hi[:], ALU.subtract).then_inc(w_split, 1)
            STEPS = GB + GB + 1

            def normalise(g):
                step = Tally(dve_step, g * STEPS)
                dve.wait_ge(rows_in, g * 16 + 16)
                for r in range(GB):
                    step.done(dve.bn_stats(stats[:, r, :], rows[:, r, :]))
                step.wait(dve)
                dve.sem_inc(stats_seen, 1)
                for r in range(GB):
                    step.done(dve.bn_aggr(moments[:, r, :], stats[:, r, :]))
                dve.wait_ge(act_std, g + 1)
                step.done(dve.reciprocal(rstd[:], std[:]))
                step.wait(dve)
                for r in range(GB):
                    last = dve.tensor_scalar(normed[:, r, :], rows[:, r, :], moments[:, r, 0:1],
                                             rstd[:, r:r + 1], ALU.subtract, ALU.mult)
                last.then_inc(normed_ready, 1)

            def split_rows(g):
                for k in range(KT):
                    dve.wait_ge(xt_hi_ready, g * KT + k + 1)
                    dve.tensor_tensor(xt_lo[:, k, :], turned[k][:, 0:GS], xt_hi[:, k, :],
                                      ALU.subtract).then_inc(xt_lo_ready, 1)

            def split_queries(g):
                for k in range(KT):
                    dve.wait_ge(q_hi_ready, g * KT + k + 1)
                    dve.scalar_tensor_tensor(q_lo[:, k, :], product[k][:, 0:GS], bias[:, k:k + 1],
                                             q_hi[:, k, :], ALU.add, ALU.subtract).then_inc(q_lo_ready, 1)

            normalise(0)
            split_rows(0)
            with dve.Fori(0, GROUPS - 1) as g:
                normalise(g + 1)
                split_queries(g)
                split_rows(g + 1)
            split_queries(GROUPS - 1)

        @block.scalar
        def _(act):
            act.wait_ge(loaded, 48)
            act.activation(w_hi[:], w_raw[:], ACT.Copy).then_inc(w_split, 1)
            act.wait_ge(eps_set, 1)

            def roots(g):
                act.wait_ge(dve_step, g * (2 * GB + 1) + 2 * GB)
                act.activation(std[:], moments[:, :, 1], ACT.Sqrt, bias=eps[0:S, :]).then_inc(act_std, 1)

            def split_rows(g):
                for k in range(KT):
                    act.wait_ge(turned_ready, g * KT + k + 1)
                    act.activation(xt_hi[:, k, :], turned[k][:, 0:GS], ACT.Copy).then_inc(xt_hi_ready, 1)

            def split_queries(g, stores_before):
                for k in range(KT):
                    act.wait_ge(product_ready, g * KT + k + 1)
                    if k == 0 and stores_before:
                        act.wait_ge(stored, g * 32)
                    act.activation(q_hi[:, k, :], product[k][:, 0:GS], ACT.Identity,
                                   bias=bias[:, k:k + 1]).then_inc(q_hi_ready, 1)

            roots(0)
            split_rows(0)
            roots(1)
            split_queries(0, False)
            split_rows(1)
            with act.Fori(1, GROUPS - 1) as g:
                roots(g + 1)
                split_queries(g, True)
                split_rows(g + 1)
            split_queries(GROUPS - 1, True)

        @block.tensor
        def _(pe):
            pe.wait_ge(loaded, 48)

            def turn(g):
                pe.wait_ge(normed_ready, g + 1)
                for k in range(KT):
                    for r in range(GB):
                        last = pe.transpose(turned[k][:, r * S:(r + 1) * S],
                                            normed[:, r, k * P:(k + 1) * P], ident[0:S, 0:S])
                    last.then_inc(turned_ready, 1)

            def project(g):
                pe.wait_ge(xt_lo_ready, g * KT + KT)
                for n in range(KT):
                    for k in range(KT):
                        cols = slice(n * P, (n + 1) * P)
                        last = three_products(pe, product[n][:, 0:GS], w_hi[:, k, cols], w_lo[:, k, cols],
                                              xt_hi[:, k, :], xt_lo[:, k, :], k == 0, k == KT - 1)
                    last.then_inc(product_ready, 1)

            turn(0)
            pe.wait_ge(w_split, 2)
            project(0)
            turn(1)
            with pe.Fori(1, GROUPS - 1) as g:
                pe.wait_ge(q_lo_ready, g * KT)
                project(g)
                turn(g + 1)
            pe.wait_ge(q_lo_ready, (GROUPS - 1) * KT)
            project(GROUPS - 1)


CT = -(-C // P)
CPAD = CT * P
C_LAST = C - (CT - 1) * P
HALF = (C // 2 + 1) // 2 * 2
HALVES = (slice(0, HALF), slice(HALF, C))
MAX_HALVES = (slice(0, HALF), slice(C - HALF, C))
STACK = 3 * HD
SROWS = STACK + HPT
VW = 2 * HD + 2
HG = 4
PR = 4

V_PARTS, K_PARTS = 4, 2
V_HELD = 3
PARTS = {"values": V_PARTS, "keys": K_PARTS}


def front_plan():
    plan, peaks = [], 0
    parts = [(t, p) for t in range(CT) for p in range(V_PARTS)]
    spread = len(parts) - V_HELD
    for n, (t, p) in enumerate(parts[:spread]):
        plan.append(("values", t, p))
        while peaks < H and peaks * spread < n * H:
            plan.append(("peak", peaks, 0))
            peaks += 1
            if peaks % HPT == 2 and peaks > HPT:
                plan.append(("shift", peaks // HPT - 1, 0))
    plan += [("peak", n, 0) for n in range(peaks, H)]
    held = [("values", t, p) for t, p in parts[spread:]]
    return plan + held[:1] + [("scores", 0, 0)] + held[1:2] + [("shift", KT - 1, 0)] + held[2:]


FIRST_TURNS = [("turn", t, 0) for t in range(CT)]
FIRST_KEYS = [("keys", n, p) for n in range(2 * KT) for p in range(K_PARTS)]
TURNS_AFTER = {0: (0,), 1: (1,), 2: (2, 3), 3: (4,), 4: (5,)}
KEYS_AFTER = {4: ((0, 0),), 5: ((0, 1),), 6: ((1, 0),), 7: ((1, 1), (2, 0)), 8: ((2, 1),), 9: ((3, 0),),
              10: ((3, 1), (4, 0)), 11: ((4, 1),), 12: ((5, 0),), 13: ((5, 1), (6, 0)), 14: ((6, 1),),
              15: ((7, 0), (7, 1))}


def batch_plan(with_next):
    plan = front_plan()
    for h in range(H + 2):
        if 0 < h < H:
            plan.append(("scores", h, 0))
        if with_next:
            plan += [("turn", t, 0) for t in TURNS_AFTER.get(h, ())]
            plan += [("keys", n, p) for n, p in KEYS_AFTER.get(h, ())]
        if h >= 2:
            plan.append(("mix", h - 2, 0))
    return plan


A_USES = CT + CT + 2 * KT
A_FIRST = CT + 2 * KT


def work_use(kind, index, b):
    if kind == "values":
        return index, A_FIRST + b * A_USES + index
    at = index if kind == "turn" else CT + index
    return (at, at) if b is None else (CT + at, A_FIRST + b * A_USES + CT + at)


def stage_cross(nc, context, wk, bk, wv, bv, ident_dram, neg_ident_dram, q_parts, attn):
    with ExitStack() as ctx:
        m = Memory(nc, ctx, "c_")
        ident = m.sb("ident", [P, P])
        neg_ident = m.sb("neg_ident", [HPT, HPT])
        rows = m.sb("rows", [P, CT, D])
        wk_hi, wk_lo = m.sb("wk_hi", [P, KT, D], F32R), m.sb("wk_lo", [P, KT, D], F32R)
        wv_hi, wv_lo = m.sb("wv_hi", [P, KT, D], F32R), m.sb("wv_lo", [P, KT, D], F32R)
        key_bias = m.sb("key_bias", [P, KT])
        value_bias = m.sb("value_bias", [S, D])
        ct_hi, ct_lo = m.sb("ct_hi", [P, KT, C], F32R), m.sb("ct_lo", [P, KT, C], F32R)
        k_hi = [m.sb(f"k_hi{i}", [P, C], F32R) for i in range(2)]
        k_lo = [m.sb(f"k_lo{i}", [P, C], F32R) for i in range(2)]
        k_stack = m.sb("k_stack", [SROWS, H, CPAD], F32R)
        q_stack = m.sb("q_stack", [SROWS, H, S], F32R)
        v = m.sb("v", [P, CT, H, VW], F32R)
        peak = m.sb("peak", [S, H])
        prob = [m.sb(f"prob{i}", [P, CT, S]) for i in range(2)]
        p_hi = [m.sb(f"p_hi{i}", [P, CT, S], F32R) for i in range(PR)]
        p_lo = [m.sb(f"p_lo{i}", [P, CT, S], F32R) for i in range(PR)]
        mixed = m.sb("mixed", [S, H, VW])
        joined = m.sb("joined", [S, H, HD])
        inv_sum = m.sb("inv_sum", [S, H])
        out_rows = m.sb("out_rows", [S, H, HD])
        raw_w = rows[:, 0:KT, :]

        work = [m.ps(f"work{i}", [P, 512]) for i in range(2)]
        pair = [m.ps(f"pair{i}", [P, 2, 512]) for i in range(2)]
        mix = [m.ps(f"mix{i}", [P, 512]) for i in range(2)]
        shift_bank = mix[0][:, 384:384 + S]

        consts_in, w_in, w_hi_done, w_lo_done = m.sem("consts_in"), m.sem("w_in"), m.sem("w_hi_done"), m.sem("w_lo_done")
        cleared = m.sem("cleared")
        rows_in = m.sem("rows_in")
        q_in = [m.sem(f"q_in{half}") for half in range(2)]
        k_in = [m.sem(f"k_in{n}") for n in range(KT)]
        work_full, work_hi, work_lo = m.sem("work_full"), m.sem("work_hi"), m.sem("work_lo")
        peak_full, peak_done = m.sem("peak_full"), m.sem("peak_done")
        shift_full, shift_done = m.sem("shift_full"), m.sem("shift_done")
        scores_full, exp_hi_done, exp_done = m.sem("scores_full"), m.sem("exp_hi_done"), m.sem("exp_done")
        p_lo_done, mix_done = m.sem("p_lo_done"), m.sem("mix_done")
        mixed_done, finish, out_ready, stored = m.sem("mixed_done"), m.sem("finish"), m.sem("out_ready"), m.sem("stored")

        block = ctx.enter_context(nc.Block())

        def c_rows(t):
            return P if t < CT - 1 else C_LAST

        def stack_queries(engine, b, half):
            heads = slice(half * H // 2, (half + 1) * H // 2)
            for n, part in enumerate((0, 0, 1)):
                src = q_parts[part].rearrange("(h d) n -> d h n", d=HD)[:, heads, bass.ds(b * S, S)]
                engine.dma_start(f32(q_stack[n * HD:(n + 1) * HD, heads, :]), src).then_inc(q_in[half], 16)

        @block.sync
        def _(sp):
            sp.dma_start(ident[:], ident_dram).then_inc(consts_in, 16)
            sp.dma_start(neg_ident[:], neg_ident_dram).then_inc(consts_in, 16)
            sp.dma_start(key_bias[:], bk.rearrange("(k p) -> p k", p=P), allow_slow_non_contiguous=True).then_inc(consts_in, 16)
            sp.dma_start(value_bias[:], row_of(bv, S)).then_inc(consts_in, 16)
            sp.dma_start(raw_w, wk.rearrange("(k p) n -> p k n", p=P)).then_inc(w_in, 16)
            sp.wait_ge(w_hi_done, 1)
            sp.wait_ge(w_lo_done, 1)
            sp.dma_start(raw_w, wv.rearrange("(k p) n -> p k n", p=P)).then_inc(w_in, 16)
            sp.wait_ge(w_hi_done, 2)
            sp.wait_ge(w_lo_done, 2)

            def load_rows(b):
                whole = (CT - 1) * P
                sp.dma_start(rows[:, 0:CT - 1, :], context[b, 0:whole, :].rearrange("(t p) d -> p t d", p=P)
                             ).then_inc(rows_in, 16)
                sp.dma_start(rows[0:C_LAST, CT - 1, :], context[b, whole:C, :]).then_inc(rows_in, 16)

            def stack_keys(n):
                for j in range(HPT):
                    for place, part in enumerate((k_hi, k_lo, k_hi)):
                        sp.dma_start(f32(k_stack[place * HD:(place + 1) * HD, n * HPT + j, 0:C]),
                                     f32(part[n % 2][j * HD:(j + 1) * HD, :])).then_inc(k_in[n], 16)

            load_rows(0)
            sp.wait_ge(cleared, 2)
            for half in range(2):
                stack_queries(sp, 0, half)
            for n in range(KT):
                sp.wait_ge(work_lo, CT + 2 * n + 2)
                stack_keys(n)

            with sp.Fori(0, B - 1) as b:
                sp.wait_ge(work_full, A_FIRST - 2 * KT + b * A_USES)
                load_rows(b + 1)
                for n in range(KT):
                    use = work_use("keys", 2 * n + 1, b)[1]
                    sp.wait_ge(work_lo, use + 1)
                    stack_keys(n)
                sp.wait_ge(out_ready, b + 1)
                sp.dma_start(attn[bass.ds(b * S, S), :], out_rows[:]).then_inc(stored, 16)
            sp.wait_ge(out_ready, B)
            sp.dma_start(attn[(B - 1) * S:B * S, :], out_rows[:]).then_inc(stored, 16)
            sp.wait_ge(stored, 16 * B)

        @block.gpsimd
        def _(pool):
            fills = [(k_stack[:, :, C:CPAD], 0.0), (k_stack[STACK:SROWS, :, 0:C], 1.0),
                     (v[:, CT - 1, :, :], 0.0), (v[0:C_LAST, CT - 1, :, 2 * HD:2 * HD + 1], 1.0),
                     (v[:, 0:CT - 1, :, 2 * HD + 1:VW], 0.0), (v[:, 0:CT - 1, :, 2 * HD:2 * HD + 1], 1.0)]
            for n, (part, value) in enumerate(fills):
                if n:
                    pool.wait_ge(cleared, n)
                pool.memset(f32(part), value).then_inc(cleared, 1)

        @block.scalar
        def _(act):
            for n, w in enumerate((wk_hi, wv_hi)):
                act.wait_ge(w_in, 16 * n + 16)
                act.activation(w[:], raw_w, ACT.Copy).then_inc(w_hi_done, 1)
            act.wait_ge(consts_in, 64)
            act.wait_ge(cleared, 6)

            def emit(kind, i, part, b, with_next=False):
                if part < PARTS.get(kind, 1) - 1:
                    return
                if kind in ("values", "turn", "keys"):
                    local, use = work_use(kind, i, b)
                    bank = work[local % 2]
                    act.wait_ge(work_full, use + 1)
                    if kind == "values":
                        r = c_rows(i)
                        ins = act.activation(v[0:r, i, :, 0:HD],
                                             bank[0:r, :].rearrange("p (h d) -> p h d", d=HD), ACT.Copy)
                    elif kind == "turn":
                        r = c_rows(i)
                        ins = act.activation(ct_hi[:, :, i * P:i * P + r],
                                             bank[:, 0:KT * r].rearrange("p (k c) -> p k c", k=KT), ACT.Copy)
                    else:
                        n, half = divmod(i, 2)
                        if half == 0 and not (b is None and n < 2):
                            before = (n + 2) % KT
                            times = 0 if b is None else b + 1
                            act.wait_ge(k_in[before], (times + (1 if n >= 2 else 0)) * 16 * 3 * HPT)
                        cols = HALVES[half]
                        ins = act.activation(k_hi[n % 2][:, cols], bank[:, 0:cols.stop - cols.start],
                                             ACT.Identity, bias=key_bias[:, n:n + 1])
                    ins.then_inc(work_hi, 1)
                elif kind == "scores":
                    act.wait_ge(scores_full, b * H + i + 1)
                    logits = pair[i % 2][:, :, 0:CT // 2 * S]
                    if i >= PR:
                        act.wait_ge(mix_done, b * H + i - PR + 1)
                    act.activation(p_hi[i % PR][:, :, :].rearrange("p (a t) s -> p a (t s)", a=2), logits,
                                   ACT.Exp).then_inc(exp_hi_done, 1)
                    if i >= 2:
                        act.wait_ge(p_lo_done, b * H + i - 1)
                    act.activation(prob[i % 2][:, :, :].rearrange("p (a t) s -> p a (t s)", a=2), logits,
                                   ACT.Exp).then_inc(exp_done, 1)
                    if with_next and i % (H // 2) == H // 2 - 1:
                        stack_queries(act, b + 1, i // (H // 2))

            for kind, i, part in FIRST_TURNS + FIRST_KEYS:
                emit(kind, i, part, None)
            with act.Fori(0, B - 1) as b:
                for kind, i, part in batch_plan(True):
                    emit(kind, i, part, b, True)
            for kind, i, part in batch_plan(False):
                emit(kind, i, part, B - 1)

        @block.vector
        def _(dve):
            for n, (hi, lo) in enumerate(((wk_hi, wk_lo), (wv_hi, wv_lo))):
                dve.wait_ge(w_hi_done, n + 1)
                dve.tensor_tensor(lo[:], raw_w, hi[:], ALU.subtract).then_inc(w_lo_done, 1)
            dve.wait_ge(consts_in, 64)
            dve.wait_ge(cleared, 6)
            FINISH = 3

            def emit(kind, i, part, b):
                if part < PARTS.get(kind, 1) - 1:
                    return
                if kind in ("values", "turn", "keys"):
                    local, use = work_use(kind, i, b)
                    bank = work[local % 2]
                    dve.wait_ge(work_hi, use + 1)
                    if kind == "values":
                        r = c_rows(i)
                        ins = dve.tensor_tensor(v[0:r, i, :, HD:2 * HD],
                                                bank[0:r, :].rearrange("p (h d) -> p h d", d=HD),
                                                v[0:r, i, :, 0:HD], ALU.subtract)
                    elif kind == "turn":
                        r = c_rows(i)
                        cols = slice(i * P, i * P + r)
                        ins = dve.tensor_tensor(ct_lo[:, :, cols],
                                                bank[:, 0:KT * r].rearrange("p (k c) -> p k c", k=KT),
                                                ct_hi[:, :, cols], ALU.subtract)
                    else:
                        n, half = divmod(i, 2)
                        cols = HALVES[half]
                        ins = dve.scalar_tensor_tensor(k_lo[n % 2][:, cols], bank[:, 0:cols.stop - cols.start],
                                                       key_bias[:, n:n + 1], k_hi[n % 2][:, cols],
                                                       ALU.add, ALU.subtract)
                    ins.then_inc(work_lo, 1)
                elif kind == "peak":
                    dve.wait_ge(peak_full, b * H + i + 1)
                    dve.tensor_reduce(peak[:, i:i + 1], pair[i % 2][0:S, :, 0:HALF], AX.XY, ALU.max
                                      ).then_inc(peak_done, 1)
                elif kind == "shift":
                    dve.wait_ge(shift_full, b * KT + i + 1)
                    dve.tensor_tensor(q_stack[STACK:SROWS, i * HPT:(i + 1) * HPT, :],
                                      repeated(shift_bank[0:HPT, :].unsqueeze(1), 1, HPT),
                                      repeated(neg_ident[:].unsqueeze(2), 2, S), ALU.mult
                                      ).then_inc(shift_done, 1)
                elif kind == "scores":
                    dve.wait_ge(exp_done, b * H + i + 1)
                    if i >= PR:
                        dve.wait_ge(mix_done, b * H + i - PR + 1)
                    dve.tensor_tensor(p_lo[i % PR][:], prob[i % 2][:], p_hi[i % PR][:], ALU.subtract
                                      ).then_inc(p_lo_done, 1)
                elif kind == "mix" and i % HG == HG - 1:
                    g = i // HG
                    dve.wait_ge(mix_done, b * H + i + 1)
                    dve.tensor_copy(mixed[:, g * HG:(g + 1) * HG, :],
                                    mix[g % 2][0:S, 0:HG * VW].rearrange("p (h w) -> p h w", w=VW)
                                    ).then_inc(mixed_done, 1)

            def finish_rows(b, stored_before):
                step = Tally(finish, b * FINISH)
                dve.wait_ge(mixed_done, b * (H // HG) + H // HG)
                step.done(dve.tensor_tensor(joined[:], mixed[:, :, 0:HD], mixed[:, :, HD:2 * HD], ALU.add))
                step.done(dve.reciprocal(inv_sum[:], mixed[:, :, 2 * HD]))
                step.wait(dve)
                if stored_before:
                    dve.wait_ge(stored, b * 16)
                step.done(dve.tensor_tensor(out_rows[:], joined[:], repeated(inv_sum[:].unsqueeze(2), 2, HD),
                                            ALU.mult))
                step.wait(dve)
                dve.tensor_tensor(out_rows[:], out_rows[:],
                                  value_bias[:].rearrange("p (h d) -> p h d", d=HD), ALU.add
                                  ).then_inc(out_ready, 1)

            for kind, i, part in FIRST_TURNS + FIRST_KEYS:
                emit(kind, i, part, None)
            for kind, i, part in batch_plan(True):
                emit(kind, i, part, 0)
            finish_rows(0, False)
            with dve.Fori(1, B - 1) as b:
                for kind, i, part in batch_plan(True):
                    emit(kind, i, part, b)
                finish_rows(b, True)
            for kind, i, part in batch_plan(False):
                emit(kind, i, part, B - 1)
            finish_rows(B - 1, True)

        @block.tensor
        def _(pe):
            pe.wait_ge(consts_in, 64)
            pe.wait_ge(w_lo_done, 2)
            pe.wait_ge(cleared, 6)

            def emit(kind, i, part, b):
                if kind in ("values", "turn", "keys"):
                    local, use = work_use(kind, i, b)
                    bank = work[local % 2]
                    if part == 0 and not (b is None and local < 2):
                        pe.wait_ge(work_lo, use - 1)
                        pe.wait_ge(work_hi, use - 1)
                    if kind == "turn":
                        if i == 0:
                            pe.wait_ge(rows_in, 32 if b is None else b * 32 + 64)
                        r = c_rows(i)
                        for k in range(KT):
                            last = pe.transpose(bank[:, k * r:(k + 1) * r], rows[0:r, i, k * P:(k + 1) * P],
                                                ident[0:r, 0:r])
                    elif kind == "keys":
                        n, half = divmod(i, 2)
                        cols = HALVES[half]
                        if n == 0 and part == 0:
                            tile_end = -(-cols.stop // P)
                            pe.wait_ge(work_lo, work_use("turn", tile_end - 1, b)[1] + 1)
                        for k in range(part * KT // K_PARTS, (part + 1) * KT // K_PARTS):
                            wcols = slice(n * P, (n + 1) * P)
                            last = three_products(pe, bank[:, 0:cols.stop - cols.start], wk_hi[:, k, wcols],
                                                  wk_lo[:, k, wcols], ct_hi[:, k, cols], ct_lo[:, k, cols],
                                                  k == 0, k == KT - 1)
                    else:
                        r = c_rows(i)
                        cols = slice(i * P, i * P + r)
                        for k in range(part * KT // V_PARTS, (part + 1) * KT // V_PARTS):
                            last = three_products(pe, bank[0:r, :], ct_hi[:, k, cols], ct_lo[:, k, cols],
                                                  wv_hi[:, k, :], wv_lo[:, k, :], k == 0, k == KT - 1)
                    if part == PARTS.get(kind, 1) - 1:
                        last.then_inc(work_full, 1)
                elif kind == "peak":
                    if i % (H // 2) == 0:
                        pe.wait_ge(q_in[i // (H // 2)], b * 48 + 48)
                    if i % HPT == 0:
                        pe.wait_ge(k_in[i // HPT], (b + 1) * 16 * 3 * HPT)
                    if i >= 2:
                        pe.wait_ge(peak_done, b * H + i - 1)
                    for bank, cols in enumerate(MAX_HALVES):
                        last = pe.matmul(pair[i % 2][0:S, bank, 0:HALF], q_stack[0:STACK, i, :],
                                         k_stack[0:STACK, i, cols], start=True, stop=True)
                    last.then_inc(peak_full, 1)
                elif kind == "shift":
                    pe.wait_ge(peak_done, b * H + (i + 1) * HPT)
                    if i >= 1:
                        pe.wait_ge(shift_done, b * KT + i)
                    pe.transpose(shift_bank[0:HPT, :], peak[:, i * HPT:(i + 1) * HPT], ident[0:S, 0:S]
                                 ).then_inc(shift_full, 1)
                elif kind == "scores":
                    if i % HPT == 0:
                        pe.wait_ge(shift_done, b * KT + i // HPT + 1)
                    if i < 2:
                        pe.wait_ge(peak_done, b * H + H - 1 + i)
                    else:
                        pe.wait_ge(exp_done, b * H + i - 1)
                    for t in range(CT):
                        col = t % (CT // 2) * S
                        last = pe.matmul(pair[i % 2][:, t // (CT // 2), col:col + S],
                                         k_stack[:, i, t * P:(t + 1) * P], q_stack[:, i, :],
                                         start=True, stop=True)
                    last.then_inc(scores_full, 1)
                elif kind == "mix":
                    g, at = divmod(i, HG)
                    if i == 0:
                        pe.wait_ge(shift_done, b * KT + KT)
                        pe.wait_ge(work_lo, work_use("values", CT - 1, b)[1] + 1)
                    if at == 0 and g >= 2:
                        pe.wait_ge(mixed_done, b * (H // HG) + g - 1)
                    pe.wait_ge(p_lo_done, b * H + i + 1)
                    for t in range(CT):
                        for p in (p_hi, p_lo):
                            last = pe.matmul(mix[g % 2][0:S, at * VW:(at + 1) * VW], p[i % PR][:, t, :],
                                             v[:, t, i, :], start=(t == 0 and p is p_hi),
                                             stop=(t == CT - 1 and p is p_lo))
                    last.then_inc(mix_done, 1)

            for kind, i, part in FIRST_TURNS + FIRST_KEYS:
                emit(kind, i, part, None)
            with pe.Fori(0, B - 1) as b:
                for kind, i, part in batch_plan(True):
                    emit(kind, i, part, b)
            for kind, i, part in batch_plan(False):
                emit(kind, i, part, B - 1)


TILES = ROWS // P
X1_STEPS = 4
SIM_STEPS = 6


def stage_rows(nc, x, attn, g_xattn, wo, bo, g_info, w_qkv, ident_dram, x1_dram, qkv_dram, sim_dram):
    with ExitStack() as ctx:
        m = Memory(nc, ctx, "r_")
        ident = m.sb("ident", [P, P])
        raw = [m.sb(f"raw{i}", [P, KT, D]) for i in range(2)]
        w_hi = [m.sb(f"w_hi{i}", [P, KT, D], F32R) for i in range(4)]
        w_lo = [m.sb(f"w_lo{i}", [P, KT, D], F32R) for i in range(4)]
        gate, gate_bias = m.sb("gate", [P, 1]), m.sb("gate_bias", [P, D])
        guide, guide_sq = m.sb("guide", [P, D]), m.sb("guide_sq", [P, D])
        guide_norm = m.sb("guide_norm", [P, 3, H])
        eps = m.sb("eps", [P, 1])
        a_rows, x_rows = m.sb("a_rows", [P, D]), m.sb("x_rows", [P, D])
        at_hi, at_lo = m.sb("at_hi", [P, KT, P], F32R), m.sb("at_lo", [P, KT, P], F32R)
        x1, normed = m.sb("x1", [P, D]), m.sb("normed", [P, D])
        nt_hi, nt_lo = m.sb("nt_hi", [P, KT, P], F32R), m.sb("nt_lo", [P, KT, P], F32R)
        stats, moments, std, rstd = m.sb("stats", [P, 6]), m.sb("moments", [P, 2]), m.sb("std", [P, 1]), m.sb("rstd", [P, 1])
        qkv = m.sb("qkv", [P, 3, D])
        q_sq, q_dot = m.sb("q_sq", [P, D]), m.sb("q_dot", [P, D])
        sq_sum, dot_sum = m.sb("sq_sum", [P, H]), m.sb("dot_sum", [P, H])
        q_norm, cosine = m.sb("q_norm", [P, 2, H]), m.sb("cosine", [P, H])
        sim = m.sb("sim", [P, 1])
        turned_a, turned_x, mixed = m.ps("turned_a", [P, KT, P]), m.ps("turned_x", [P, KT, P]), m.ps("mixed", [P, D])
        product = [m.ps(f"product{i}", [P, D]) for i in range(3)]

        consts_in, w_hi_done, w_lo_done = m.sem("consts_in"), m.sem("w_hi_done"), m.sem("w_lo_done")
        w_in = [m.sem(f"w_in{i}") for i in range(2)]
        set_up, act_setup, stats_seen = m.sem("set_up"), m.sem("act_setup"), m.sem("stats_seen")
        a_in, x_in = m.sem("a_in"), m.sem("x_in")
        a_turned, a_hi, a_lo, a_mixed = m.sem("a_turned"), m.sem("a_hi"), m.sem("a_lo"), m.sem("a_mixed")
        x1_ready, x1_step, act_std, normed_ready = m.sem("x1_ready"), m.sem("x1_step"), m.sem("act_std"), m.sem("normed_ready")
        n_turned, n_hi, n_lo = m.sem("n_turned"), m.sem("n_hi"), m.sem("n_lo")
        q_full, kv_full, q_out, kv_out = m.sem("q_full"), m.sem("kv_full"), m.sem("q_out"), m.sem("kv_out")
        q_sq_done, q_root, sim_step, sim_ready = m.sem("q_sq_done"), m.sem("q_root"), m.sem("sim_step"), m.sem("sim_ready")
        x1_stored, qkv_stored, sim_stored = m.sem("x1_stored"), m.sem("qkv_stored"), m.sem("sim_stored")

        block = ctx.enter_context(nc.Block())

        @block.sync
        def _(sp):
            sp.dma_start(ident[:], ident_dram).then_inc(consts_in, 16)
            sp.dma_start(gate[:], row_of(g_xattn, P)).then_inc(consts_in, 16)
            sp.dma_start(gate_bias[:], row_of(bo, P)).then_inc(consts_in, 16)
            sp.dma_start(guide[:], repeated(g_info[0, 0:1, :], 0, P)).then_inc(consts_in, 16)
            for n in range(4):
                if n >= 2:
                    sp.wait_ge(w_hi_done, n - 1)
                    sp.wait_ge(w_lo_done, n - 1)
                src = wo if n == 0 else w_qkv[:, (n - 1) * D:n * D]
                sp.dma_start(raw[n % 2][:], src.rearrange("(k p) n -> p k n", p=P)).then_inc(w_in[n % 2], 16)
                if n == 1:
                    sp.dma_start(a_rows[:], attn[0:P, :]).then_inc(a_in, 16)
                    sp.dma_start(x_rows[:], x[0:P, :]).then_inc(x_in, 16)

            def load(t):
                sp.wait_ge(a_turned, t)
                sp.dma_start(a_rows[:], attn[bass.ds(t * P, P), :]).then_inc(a_in, 16)
                sp.wait_ge(x1_ready, t)
                sp.dma_start(x_rows[:], x[bass.ds(t * P, P), :]).then_inc(x_in, 16)

            def store_x1(t):
                sp.wait_ge(x1_ready, t + 1)
                sp.dma_start(x1_dram[bass.ds(t * P, P), :], x1[:]).then_inc(x1_stored, 16)

            def store_qkv(t):
                sp.wait_ge(sim_ready, t + 1)
                sp.dma_start(sim_dram[bass.ds(t * P, P), :], sim[:]).then_inc(sim_stored, 16)
                sp.wait_ge(q_out, t + 1)
                sp.wait_ge(kv_out, 2 * t + 2)
                sp.dma_start(qkv_dram[bass.ds(t * P, P), :], qkv[:].rearrange("p a n -> p (a n)")
                             ).then_inc(qkv_stored, 16)

            store_x1(0)
            load(1)
            with sp.Fori(0, TILES - 2) as t:
                store_x1(t + 1)
                load(t + 2)
                store_qkv(t)
            store_x1(TILES - 1)
            store_qkv(TILES - 2)
            store_qkv(TILES - 1)
            sp.wait_ge(x1_stored, 16 * TILES)
            sp.wait_ge(qkv_stored, 16 * TILES)
            sp.wait_ge(sim_stored, 16 * TILES)

        @block.scalar
        def _(act):
            for n in range(4):
                act.wait_ge(w_in[n % 2], 16 * (n // 2) + 16)
                act.activation(w_hi[n][:], raw[n % 2][:], ACT.Copy).then_inc(w_hi_done, 1)
            act.wait_ge(consts_in, 64)
            act.activation(gate[:], gate[:], ACT.Tanh).then_inc(act_setup, 1)
            act.wait_ge(set_up, 2)
            act.activation(guide_norm[:, 1, :], guide_norm[:, 0, :], ACT.Sqrt).then_inc(act_setup, 1)

            def split_attn(t):
                act.wait_ge(a_turned, t + 1)
                act.activation(at_hi[:], turned_a[:], ACT.Copy).then_inc(a_hi, 1)

            def root(t):
                act.wait_ge(x1_step, t * X1_STEPS + X1_STEPS - 1)
                act.activation(std[:], moments[:, 1:2], ACT.Sqrt, bias=eps[:]).then_inc(act_std, 1)

            def split_normed(t):
                act.wait_ge(n_turned, t + 1)
                act.activation(nt_hi[:], turned_x[:], ACT.Copy).then_inc(n_hi, 1)

            def queries(t, stored_before):
                act.wait_ge(q_full, t + 1)
                if stored_before:
                    act.wait_ge(qkv_stored, 16 * t)
                    act.wait_ge(sim_ready, t)
                act.activation(q_sq[:], product[0][:], ACT.Square).then_inc(q_sq_done, 1)
                act.activation(qkv[:, 0, :], product[0][:], ACT.Copy).then_inc(q_out, 1)

            def keys_values(t):
                for n in (1, 2):
                    act.wait_ge(kv_full, 2 * t + n)
                    act.activation(qkv[:, n, :], product[n][:], ACT.Copy).then_inc(kv_out, 1)

            def query_root(t):
                act.wait_ge(sim_step, t * SIM_STEPS + 2)
                act.activation(q_norm[:, 0, :], sq_sum[:], ACT.Sqrt).then_inc(q_root, 1)

            def body(t, stored_before):
                split_normed(t)
                split_attn(t + 1)
                queries(t, stored_before)
                root(t + 1)
                query_root(t)
                keys_values(t)

            split_attn(0)
            root(0)
            body(0, False)
            with act.Fori(1, TILES - 1) as t:
                body(t, True)
            split_normed(TILES - 1)
            queries(TILES - 1, True)
            query_root(TILES - 1)
            keys_values(TILES - 1)

        @block.vector
        def _(dve):
            for n in range(4):
                dve.wait_ge(w_hi_done, n + 1)
                dve.tensor_tensor(w_lo[n][:], raw[n % 2][:], w_hi[n][:], ALU.subtract).then_inc(w_lo_done, 1)
            dve.wait_ge(consts_in, 64)
            by_head = guide[:].rearrange("p (h d) -> p h d", d=HD)
            step = Tally(set_up)
            step.done(dve.memset(eps[:], EPS))
            dve.tensor_tensor(guide_sq[:], guide[:], guide[:], ALU.mult).then_inc(sim_step, 1)
            dve.wait_ge(sim_step, 1)
            step.done(dve.tensor_reduce(guide_norm[:, 0, :], guide_sq[:].rearrange("p (h d) -> p h d", d=HD),
                                        AX.X, ALU.add))
            dve.wait_ge(act_setup, 2)
            step.done(dve.reciprocal(guide_norm[:, 2, :], guide_norm[:, 1, :]))
            step.wait(dve)
            step.done(dve.tensor_tensor(by_head, by_head, repeated(guide_norm[:, 2, :].unsqueeze(2), 2, HD), ALU.mult))
            step.done(dve.tensor_scalar(gate_bias[:], gate_bias[:], gate[:], None, ALU.mult))
            step.wait(dve)

            def split_attn(t):
                dve.wait_ge(a_hi, t + 1)
                dve.tensor_tensor(at_lo[:], turned_a[:], at_hi[:], ALU.subtract).then_inc(a_lo, 1)

            def residual(t, stored_before):
                step = Tally(x1_step, t * X1_STEPS)
                dve.wait_ge(a_mixed, t + 1)
                dve.wait_ge(x_in, t * 16 + 16)
                if stored_before:
                    dve.wait_ge(x1_stored, 16 * t)
                step.done(dve.scalar_tensor_tensor(x1[:], mixed[:], gate[:], x_rows[:], ALU.mult, ALU.add))
                step.wait(dve)
                dve.tensor_tensor(x1[:], x1[:], gate_bias[:], ALU.add).then_inc(x1_ready, 1)
                dve.wait_ge(x1_ready, t + 1)
                step.done(dve.bn_stats(stats[:], x1[:]))
                step.wait(dve)
                dve.sem_inc(stats_seen, 1)
                step.done(dve.bn_aggr(moments[:], stats[:]))
                dve.wait_ge(act_std, t + 1)
                step.done(dve.reciprocal(rstd[:], std[:]))
                step.wait(dve)
                if stored_before:
                    dve.wait_ge(n_turned, t)
                dve.tensor_scalar(normed[:], x1[:], moments[:, 0:1], rstd[:], ALU.subtract, ALU.mult
                                  ).then_inc(normed_ready, 1)

            def split_normed(t):
                dve.wait_ge(n_hi, t + 1)
                dve.tensor_tensor(nt_lo[:], turned_x[:], nt_hi[:], ALU.subtract).then_inc(n_lo, 1)

            def query_sums(t):
                step = Tally(sim_step, t * SIM_STEPS + 1)
                dve.wait_ge(q_sq_done, t + 1)
                step.done(dve.tensor_reduce(sq_sum[:], q_sq[:].rearrange("p (h d) -> p h d", d=HD), AX.X, ALU.add))
                dve.wait_ge(q_out, t + 1)
                step.done(dve.tensor_tensor(q_dot[:], qkv[:, 0, :], guide[:], ALU.mult))
                step.wait(dve)
                step.done(dve.tensor_reduce(dot_sum[:], q_dot[:].rearrange("p (h d) -> p h d", d=HD), AX.X, ALU.add))
                return step

            def similarity(t, step, stored_before):
                dve.wait_ge(q_root, t + 1)
                step.done(dve.reciprocal(q_norm[:, 1, :], q_norm[:, 0, :]))
                step.wait(dve)
                step.done(dve.tensor_tensor(cosine[:], dot_sum[:], q_norm[:, 1, :], ALU.mult))
                step.wait(dve)
                step.done(dve.tensor_scalar(cosine[:], cosine[:], 1.0 / H, None, ALU.mult))
                step.wait(dve)
                if stored_before:
                    dve.wait_ge(sim_stored, 16 * t)
                dve.tensor_reduce(sim[:], cosine[:], AX.X, ALU.add).then_inc(sim_ready, 1)

            def body(t, stored_before):
                split_normed(t)
                split_attn(t + 1)
                step = query_sums(t)
                residual(t + 1, True)
                similarity(t, step, stored_before)

            split_attn(0)
            residual(0, False)
            body(0, False)
            with dve.Fori(1, TILES - 1) as t:
                body(t, True)
            split_normed(TILES - 1)
            similarity(TILES - 1, query_sums(TILES - 1), True)

        @block.tensor
        def _(pe):
            pe.wait_ge(consts_in, 64)

            def turn_attn(t):
                pe.wait_ge(a_in, t * 16 + 16)
                for k in range(KT):
                    last = pe.transpose(turned_a[:, k, :], a_rows[:, k * P:(k + 1) * P], ident[:])
                last.then_inc(a_turned, 1)

            def mix_attn(t):
                pe.wait_ge(a_lo, t + 1)
                for k in range(KT):
                    last = three_products(pe, mixed[:], at_hi[:, k, :], at_lo[:, k, :], w_hi[0][:, k, :],
                                          w_lo[0][:, k, :], k == 0, k == KT - 1)
                last.then_inc(a_mixed, 1)

            def turn_normed(t):
                pe.wait_ge(normed_ready, t + 1)
                for k in range(KT):
                    last = pe.transpose(turned_x[:, k, :], normed[:, k * P:(k + 1) * P], ident[:])
                last.then_inc(n_turned, 1)

            def project(n):
                for k in range(KT):
                    last = three_products(pe, product[n][:], nt_hi[:, k, :], nt_lo[:, k, :], w_hi[n + 1][:, k, :],
                                          w_lo[n + 1][:, k, :], k == 0, k == KT - 1)
                last.then_inc(q_full if n == 0 else kv_full, 1)

            def project_all(t, follows, attn_between):
                pe.wait_ge(n_lo, t + 1)
                if follows:
                    pe.wait_ge(q_out, t)
                project(0)
                if attn_between:
                    mix_attn(t + 1)
                if follows:
                    pe.wait_ge(kv_out, 2 * t)
                project(1)
                project(2)

            def body(t, follows):
                turn_normed(t)
                turn_attn(t + 1)
                project_all(t, follows, True)

            turn_attn(0)
            pe.wait_ge(w_lo_done, 4)
            mix_attn(0)
            body(0, False)
            with pe.Fori(1, TILES - 1) as t:
                body(t, True)
            turn_normed(TILES - 1)
            project_all(TILES - 1, True, False)


QR = S + REG


def stage_self(nc, qkv_dram, sim_dram, x1_dram, class_dram, g_ffn, w_proj, b_proj, ident_dram, fold_dram, out):
    with ExitStack() as ctx:
        m = Memory(nc, ctx, "s_")
        ident, fold = m.sb("ident", [P, P]), m.sb("fold", [QR, S])
        raw = m.sb("raw", [P, KT, D])
        w_hi, w_lo = m.sb("w_hi", [P, KT, D], F32R), m.sb("w_lo", [P, KT, D], F32R)
        gate, gate_bias = m.sb("gate", [P, 1]), m.sb("gate_bias", [S, D])
        sim = m.sb("sim", [B, S])
        ends, ends_row, ends_all = m.sb("ends", [B, 2]), m.sb("ends_row", [1, 2]), m.sb("ends_all", [B, 2])
        low_high = m.sb("low_high", [1, 2])
        ones = m.sb("ones", [1, B])
        spread = m.sb("spread", [B, 2])
        classes = m.sb("classes", [B, QR])
        qk = m.sb("qk", [QR, 2, D])
        values = m.sb("values", [S, D])
        x1 = m.sb("x1", [S, D])
        key_class, query_class = m.sb("key_class", [QR, S]), m.sb("query_class", [QR, 1])
        mask = m.sb("mask", [QR, S])
        qt, kt = m.sb("qt", [P, KT, QR]), m.sb("kt", [P, KT, S])
        logits = m.sb("logits", [QR, HPT, KT, S])
        prob = m.sb("prob", [QR, HPT, KT, S])
        top, total, inv = m.sb("top", [QR, H]), m.sb("total", [QR, H]), m.sb("inv", [QR, H])
        pt = m.sb("pt", [S, H, QR])
        mixed = m.sb("mixed", [QR, D])
        ot_hi, ot_lo = m.sb("ot_hi", [P, KT, S], F32R), m.sb("ot_lo", [P, KT, S], F32R)
        y = m.sb("y", [S, D])
        scores = m.ps("scores", [P, HPT, 512])
        turned = [m.ps(f"turned{i}", [P, 512]) for i in range(2)]
        mix_bank, proj_bank = m.ps("mix_bank", [P, 512]), m.ps("proj_bank", [P, 512])

        consts_in, w_split, act_setup = m.sem("consts_in"), m.sem("w_split"), m.sem("act_setup")
        sim_in, ends_step, ends_turned = m.sem("sim_in"), m.sem("ends_step"), m.sem("ends_turned")
        class_ready, class_stored = m.sem("class_ready"), m.sem("class_stored")
        qk_in, v_in, class_in, x1_in = m.sem("qk_in"), m.sem("v_in"), m.sem("class_in"), m.sem("x1_in")
        q_turned, k_turned, qt_done, kt_done = m.sem("q_turned"), m.sem("k_turned"), m.sem("qt_done"), m.sem("kt_done")
        scored, mask_done, logit_step, exp_done, inv_done = (
            m.sem("scored"), m.sem("mask_done"), m.sem("logit_step"), m.sem("exp_done"), m.sem("inv_done"))
        p_turned, pt_act, pt_dve = m.sem("p_turned"), m.sem("pt_act"), m.sem("pt_dve")
        mix_full, mixed_done = m.sem("mix_full"), m.sem("mixed_done")
        o_turned, ot_hi_done, ot_lo_done = m.sem("o_turned"), m.sem("ot_hi_done"), m.sem("ot_lo_done")
        proj_full, y_step, y_ready, stored = m.sem("proj_full"), m.sem("y_step"), m.sem("y_ready"), m.sem("stored")

        block = ctx.enter_context(nc.Block())
        LOGIT_STEPS = 3

        @block.sync
        def _(sp):
            sp.dma_start(sim[:], sim_dram.rearrange("(b s) a -> b (s a)", s=S)).then_inc(sim_in, 16)
            sp.dma_start(ident[:], ident_dram).then_inc(consts_in, 16)
            sp.dma_start(fold[:], fold_dram).then_inc(consts_in, 16)
            sp.dma_start(gate[:], row_of(g_ffn, P)).then_inc(consts_in, 16)
            sp.dma_start(gate_bias[:], row_of(b_proj, S)).then_inc(consts_in, 16)
            sp.dma_start(raw[:], w_proj.rearrange("(k p) n -> p k n", p=P)).then_inc(consts_in, 16)

            def load_qk(b):
                src = qkv_dram[bass.ds(b * S, S), 0:2 * D].rearrange("s (a n) -> s a n", a=2)
                sp.dma_start(qk[0:S, :, :], src).then_inc(qk_in, 16)
                sp.dma_start(qk[S:QR, 0, :], qkv_dram[bass.ds(b * S, REG), 0:D]).then_inc(qk_in, 16)

            def load_classes(b):
                sp.dma_start(key_class[:], repeated(class_dram[bass.ds(b, 1), 0:S], 0, QR)).then_inc(class_in, 16)
                sp.dma_start(query_class[:], class_dram[bass.ds(b, 1), :].rearrange("a (q c) -> (a q) c", c=1),
                             allow_slow_non_contiguous=True).then_inc(class_in, 16)

            def load_values(b):
                sp.dma_start(values[:], qkv_dram[bass.ds(b * S, S), 2 * D:3 * D]).then_inc(v_in, 16)

            def load_x1(b):
                sp.dma_start(x1[:], x1_dram[bass.ds(b * S, S), :]).then_inc(x1_in, 16)

            load_qk(0)
            load_values(0)
            load_x1(0)
            sp.wait_ge(class_ready, 1)
            sp.dma_start(class_dram, classes[:]).then_inc(class_stored, 16)
            sp.wait_ge(class_stored, 16)
            load_classes(0)
            sp.wait_ge(k_turned, 1)
            load_qk(1)
            sp.wait_ge(mask_done, 1)
            load_classes(1)

            def finish(b):
                sp.wait_ge(y_ready, b + 1)
                sp.dma_start(out[bass.ds(b * S, S), :], y[:]).then_inc(stored, 16)

            with sp.Fori(0, B - 2) as b:
                sp.wait_ge(k_turned, b + 2)
                load_qk(b + 2)
                sp.wait_ge(mix_full, b + 1)
                load_values(b + 1)
                sp.wait_ge(mask_done, b + 2)
                load_classes(b + 2)
                finish(b)
                load_x1(b + 1)
            sp.wait_ge(mix_full, B - 1)
            load_values(B - 1)
            finish(B - 2)
            load_x1(B - 1)
            finish(B - 1)
            sp.wait_ge(stored, 16 * B)

        def turn_use(b, n):
            return turned[n % 2]

        @block.scalar
        def _(act):
            act.wait_ge(consts_in, 80)
            act.activation(w_hi[:], raw[:], ACT.Copy).then_inc(w_split, 1)
            act.activation(gate[:], gate[:], ACT.Tanh).then_inc(act_setup, 1)

            def queries(b):
                act.wait_ge(q_turned, b + 1)
                act.activation(qt[:], turned[0][:, 0:KT * QR].rearrange("p (k s) -> p k s", k=KT), ACT.Copy,
                               scale=LOGIT_SCALE).then_inc(qt_done, 1)

            def exponentials(b):
                act.wait_ge(logit_step, b * LOGIT_STEPS + LOGIT_STEPS)
                act.activation(prob[:].rearrange("p a m s -> p (a m s)"),
                               logits[:].rearrange("p a m s -> p (a m s)"), ACT.Exp).then_inc(exp_done, 1)

            def turn_back(b):
                for n in (0, 2):
                    act.wait_ge(p_turned, b * HPT + n + 1)
                    act.activation(pt[:, n * HPT:(n + 1) * HPT, :],
                                   turned[n % 2][0:S, 0:HPT * QR].rearrange("p (j q) -> p j q", j=HPT), ACT.Copy
                                   ).then_inc(pt_act, 1)

            def mix_parts(b):
                act.wait_ge(o_turned, b + 1)
                act.activation(ot_hi[:], turned[0][:, 0:KT * S].rearrange("p (k s) -> p k s", k=KT), ACT.Copy
                               ).then_inc(ot_hi_done, 1)

            queries(0)
            exponentials(0)
            with act.Fori(0, B - 1) as b:
                turn_back(b)
                queries(b + 1)
                mix_parts(b)
                exponentials(b + 1)
            turn_back(B - 1)
            mix_parts(B - 1)

        @block.vector
        def _(dve):
            step = Tally(ends_step)
            dve.wait_ge(sim_in, 16)
            step.done(dve.memset(ones[:], 1.0))
            step.done(dve.tensor_reduce(ends[:, 0:1], sim[:, REG:S], AX.X, ALU.min))
            step.done(dve.tensor_reduce(ends[:, 1:2], sim[:, REG:S], AX.X, ALU.max))
            dve.wait_ge(ends_turned, 1)
            step.done(dve.tensor_reduce(low_high[:, 0:1], mix_bank[0:1, 0:B], AX.X, ALU.min))
            step.done(dve.tensor_reduce(low_high[:, 1:2], mix_bank[0:1, B:2 * B], AX.X, ALU.max))
            dve.wait_ge(ends_turned, 2)
            step.done(dve.tensor_copy(ends_all[:], proj_bank[0:B, 0:2]))
            step.wait(dve)
            step.done(dve.tensor_tensor(spread[:, 0:1], ends_all[:, 1:2], ends_all[:, 0:1], ALU.subtract))
            step.done(dve.memset(classes[:, S:QR], 0.0))
            step.wait(dve)
            step.done(dve.reciprocal(spread[:, 1:2], spread[:, 0:1]))
            step.wait(dve)
            step.done(dve.tensor_scalar(sim[:], sim[:], ends_all[:, 0:1], spread[:, 1:2], ALU.subtract, ALU.mult))
            step.wait(dve)
            step.done(dve.tensor_scalar(classes[:, 0:S], sim[:], THRESHOLD, None, ALU.is_gt))
            step.wait(dve)
            dve.memset(classes[:, 0:REG], 1.0).then_inc(class_ready, 1)
            dve.wait_ge(consts_in, 80)
            dve.wait_ge(w_split, 1)
            dve.tensor_tensor(w_lo[:], raw[:], w_hi[:], ALU.subtract).then_inc(w_split, 1)
            dve.wait_ge(act_setup, 1)
            step.done(dve.tensor_scalar(gate_bias[:], gate_bias[:], gate[0:S, :], None, ALU.mult))
            step.done(dve.memset(mask[:, 0:REG], 0.0))
            step.wait(dve)

            def keys(b):
                dve.wait_ge(k_turned, b + 1)
                dve.tensor_copy(kt[:], turned[1][:, 0:KT * S].rearrange("p (k s) -> p k s", k=KT)
                                ).then_inc(kt_done, 1)

            def make_mask(b):
                dve.wait_ge(class_in, 32 * b + 32)
                dve.tensor_scalar(mask[:, REG:S], key_class[:, REG:S], query_class[:], MASKED,
                                  ALU.not_equal, ALU.mult).then_inc(mask_done, 1)

            def masked_logits(b):
                step = Tally(logit_step, b * LOGIT_STEPS)
                dve.wait_ge(scored, b + 1)
                dve.wait_ge(mask_done, b + 1)
                step.done(dve.tensor_tensor(
                    logits[:], scores[0:QR, :, 0:KT * S].rearrange("p a (m s) -> p a m s", m=KT),
                    repeated(repeated(mask[:].unsqueeze(1).unsqueeze(1), 1, HPT), 2, KT), ALU.add))
                step.wait(dve)
                by_head = logits[:].rearrange("p a m s -> p (a m) s")
                step.done(dve.tensor_reduce(top[:], by_head, AX.X, ALU.max))
                step.wait(dve)
                step.done(dve.tensor_tensor(by_head, by_head, repeated(top[:].unsqueeze(2), 2, S), ALU.subtract))

            def sums(b):
                dve.wait_ge(exp_done, b + 1)
                dve.tensor_reduce(total[:], prob[:].rearrange("p a m s -> p (a m) s"), AX.X, ALU.add
                                  ).then_inc(inv_done, 1)
                dve.wait_ge(inv_done, 2 * b + 1)
                dve.reciprocal(inv[:], total[:]).then_inc(inv_done, 1)

            def turn_back(b):
                for n in (1, 3):
                    dve.wait_ge(p_turned, b * HPT + n + 1)
                    dve.tensor_copy(pt[:, n * HPT:(n + 1) * HPT, :],
                                    turned[n % 2][0:S, 0:HPT * QR].rearrange("p (j q) -> p j q", j=HPT)
                                    ).then_inc(pt_dve, 1)

            def weigh(b):
                dve.wait_ge(mix_full, b + 1)
                dve.wait_ge(inv_done, 2 * b + 2)
                dve.tensor_tensor(mixed[:].rearrange("p (m a d) -> p m a d", a=HPT, d=HD),
                                  mix_bank[0:QR, :].rearrange("p (m a d) -> p m a d", a=HPT, d=HD),
                                  repeated(inv[:].rearrange("p (a m) -> p m a", m=KT).unsqueeze(3), 3, HD),
                                  ALU.mult).then_inc(mixed_done, 1)

            def mix_parts(b):
                dve.wait_ge(ot_hi_done, b + 1)
                dve.tensor_tensor(ot_lo[:], turned[0][:, 0:KT * S].rearrange("p (k s) -> p k s", k=KT), ot_hi[:],
                                  ALU.subtract).then_inc(ot_lo_done, 1)

            def result(b, stored_before):
                dve.wait_ge(proj_full, b + 1)
                dve.wait_ge(x1_in, 16 * b + 16)
                if stored_before:
                    dve.wait_ge(stored, 16 * b)
                dve.scalar_tensor_tensor(y[:], proj_bank[0:S, :], gate[0:S, :], x1[:], ALU.mult, ALU.add
                                         ).then_inc(y_step, 1)
                dve.wait_ge(y_step, b + 1)
                dve.tensor_tensor(y[:], y[:], gate_bias[:], ALU.add).then_inc(y_ready, 1)

            def body(b, stored_before):
                turn_back(b)
                keys(b + 1)
                make_mask(b + 1)
                weigh(b)
                masked_logits(b + 1)
                mix_parts(b)
                sums(b + 1)
                result(b, stored_before)

            keys(0)
            make_mask(0)
            masked_logits(0)
            sums(0)
            body(0, False)
            with dve.Fori(1, B - 1) as b:
                body(b, True)
            turn_back(B - 1)
            weigh(B - 1)
            mix_parts(B - 1)
            result(B - 1, True)

        @block.tensor
        def _(pe):
            pe.wait_ge(consts_in, 80)
            pe.wait_ge(ends_step, 3)
            pe.transpose(mix_bank[0:1, 0:B], ends[:, 0:1], ident[0:B, 0:B])
            pe.transpose(mix_bank[0:1, B:2 * B], ends[:, 1:2], ident[0:B, 0:B]).then_inc(ends_turned, 1)
            pe.wait_ge(ends_step, 5)
            pe.matmul(proj_bank[0:B, 0:2], ones[:], low_high[:], start=True, stop=True).then_inc(ends_turned, 1)
            pe.wait_ge(ends_step, 6)
            pe.wait_ge(w_split, 2)

            def turn_qk(b):
                pe.wait_ge(qk_in, 32 * b + 32)
                for k in range(KT):
                    last = pe.transpose(turned[0][:, k * QR:(k + 1) * QR], qk[:, 0, k * P:(k + 1) * P],
                                        ident[0:QR, 0:QR])
                last.then_inc(q_turned, 1)
                for k in range(KT):
                    last = pe.transpose(turned[1][:, k * S:(k + 1) * S], qk[0:S, 1, k * P:(k + 1) * P],
                                        ident[0:S, 0:S])
                last.then_inc(k_turned, 1)

            def score(b, follows):
                pe.wait_ge(qt_done, b + 1)
                pe.wait_ge(kt_done, b + 1)
                if follows:
                    pe.wait_ge(logit_step, (b - 1) * LOGIT_STEPS + 1)
                for k in range(KT):
                    for j in range(HPT):
                        part = slice(j * HD, (j + 1) * HD)
                        last = pe.matmul(scores[0:QR, j, k * S:(k + 1) * S], qt[part, k, :], kt[part, k, :],
                                         start=True, stop=True)
                last.then_inc(scored, 1)

            def turn_probs(b):
                pe.wait_ge(exp_done, b + 1)
                for n in range(HPT):
                    if n == 2:
                        pe.wait_ge(pt_act, 2 * b + 1)
                    if n == 3:
                        pe.wait_ge(pt_dve, 2 * b + 1)
                    for k in range(KT):
                        last = pe.transpose(turned[n % 2][0:S, k * QR:(k + 1) * QR], prob[:, n, k, :],
                                            ident[0:QR, 0:QR])
                    last.then_inc(p_turned, 1)

            def mix(b):
                pe.wait_ge(v_in, 16 * b + 16)
                pe.wait_ge(pt_act, 2 * b + 2)
                pe.wait_ge(pt_dve, 2 * b + 2)
                for n in range(HPT):
                    for k in range(KT):
                        cols = slice((k * HPT + n) * HD, (k * HPT + n + 1) * HD)
                        last = pe.matmul(mix_bank[0:QR, cols], pt[:, n * KT + k, :], values[:, cols],
                                         start=True, stop=True)
                last.then_inc(mix_full, 1)

            def fold_mix(b):
                pe.wait_ge(mixed_done, b + 1)
                for k in range(KT):
                    last = pe.matmul(turned[0][:, k * S:(k + 1) * S], mixed[:, k * P:(k + 1) * P], fold[:],
                                     start=True, stop=True)
                last.then_inc(o_turned, 1)

            def project(b, follows):
                pe.wait_ge(ot_lo_done, b + 1)
                if follows:
                    pe.wait_ge(y_step, b)
                for k in range(KT):
                    last = three_products(pe, proj_bank[0:S, :], ot_hi[:, k, :], ot_lo[:, k, :], w_hi[:, k, :],
                                          w_lo[:, k, :], k == 0, k == KT - 1)
                last.then_inc(proj_full, 1)

            def body(b, follows):
                if follows:
                    pe.wait_ge(ot_lo_done, b)
                turn_probs(b)
                mix(b)
                turn_qk(b + 1)
                score(b + 1, True)
                fold_mix(b)
                project(b, follows)

            turn_qk(0)
            score(0, False)
            body(0, False)
            with pe.Fori(1, B - 1) as b:
                body(b, True)
            pe.wait_ge(ot_lo_done, B - 1)
            turn_probs(B - 1)
            mix(B - 1)
            fold_mix(B - 1)
            project(B - 1, True)


def flamingo_block(nc, x, ctx_1024, g_xattn, g_ffn, wq, bq, wk, bk, wv, bv, wo, bo, g_info, w_qkv, w_proj, b_proj,
                   ident, neg_ident, fold, out):
    q_parts = nc.dram_tensor("q_parts", [2, D, ROWS], F32).ap()
    attn = nc.dram_tensor("attn", [ROWS, D], F32).ap()
    x1 = nc.dram_tensor("x1", [ROWS, D], F32).ap()
    qkv = nc.dram_tensor("qkv", [ROWS, 3 * D], F32).ap()
    sim = nc.dram_tensor("sim", [ROWS, 1], F32).ap()
    classes = nc.dram_tensor("classes", [B, QR], F32).ap()
    x_rows = x.rearrange("b s d -> (b s) d")
    stage_queries(nc, x, wq, bq, ident, q_parts)
    stage_cross(nc, ctx_1024, wk, bk, wv, bv, ident, neg_ident, q_parts, attn)
    stage_rows(nc, x_rows, attn, g_xattn, wo, bo, g_info, w_qkv, ident, x1, qkv, sim)
    stage_self(nc, qkv, sim, x1, classes, g_ffn, w_proj, b_proj, ident, fold, out.rearrange("b s d -> (b s) d"))


INPUTS = ["x", "ctx_1024", "g_xattn", "g_ffn", "L0_xattn_wq", "L0_xattn_bq", "L0_xattn_wk", "L0_xattn_bk",
          "L0_xattn_wv", "L0_xattn_bv", "L0_xattn_wo", "L0_xattn_bo", "L0_ffn_g_info", "L0_ffn_W_qkv",
          "L0_ffn_W_proj", "L0_ffn_b_proj"]


def kernel(**inputs):
    import concourse.bacc as bacc
    from concourse.bass_utils import run_bass_kernel_spmd

    fold = np.zeros((QR, S), np.float32)
    for q in range(S):
        fold[q, q] = 0.5 if q < REG else 1.0
    for q in range(REG):
        fold[S + q, q] = 0.5
    arrays = {name: np.ascontiguousarray(inputs[name]) for name in INPUTS}
    arrays |= {"ident": np.eye(P, dtype=np.float32), "neg_ident": -np.eye(HPT, dtype=np.float32),
               "fold": fold}
    nc = bacc.Bacc("TRN2", target_bir_lowering=False, num_devices=1)
    args = [nc.dram_tensor(f"in_{name}", a.shape, mybir.dt.from_np(a.dtype), kind="ExternalInput").ap()
            for name, a in arrays.items()]
    out = nc.dram_tensor("out", (B, S, D), F32, kind="ExternalOutput").ap()
    flamingo_block(nc, *args, out)
    result = run_bass_kernel_spmd(nc, [{f"in_{name}": a for name, a in arrays.items()}], core_ids=[0])
    return result.results[0]["out"]
```

```python
from contextlib import ExitStack

import numpy as np

import concourse.bass as bass
from concourse import mybir

F32 = mybir.dt.float32
F32R = mybir.dt.float32r
BF16 = mybir.dt.bfloat16
ALU = mybir.AluOpType
ACT = mybir.ActivationFunctionType
AX = mybir.AxisListType

P = 128
B, S, D = 32, 100, 512
C = 722
H, HD = 16, 32
KT = D // P
HPT = P // HD
REG = 5
ROWS = B * S
EPS = 1e-5
LOGIT_SCALE = HD ** -0.5
THRESHOLD = 0.9
MASKED = 2.0 ** 100


class Tally:

    def __init__(self, sem, base=0):
        self.sem, self.base, self.n = sem, base, 0

    def done(self, instruction):
        instruction.then_inc(self.sem, 1)
        self.n += 1

    def wait(self, engine, back=0):
        engine.wait_ge(self.sem, self.base + (self.n - back))


class Memory:
    def __init__(self, nc, ctx, prefix):
        self.nc, self.ctx, self.prefix = nc, ctx, prefix

    def sb(self, name, shape, dt=F32):
        return self.ctx.enter_context(self.nc.sbuf_tensor(self.prefix + name, shape, dt))

    def ps(self, name, shape):
        return self.ctx.enter_context(self.nc.psum_tensor(self.prefix + name, shape, F32))

    def sem(self, name):
        return self.ctx.enter_context(self.nc.semaphore(self.prefix + name))


def f32(ap):
    return ap.bitcast(F32)


def repeated(ap, dim, times):
    shape = list(ap.shape)
    shape[dim] = times
    return ap.broadcast_to(shape)


def row_of(vector, partitions):
    return repeated(vector.rearrange("(a n) -> a n", a=1), 0, partitions)


def three_products(pe, out, left_hi, left_lo, right_hi, right_lo, first, last):
    pe.matmul(out, left_hi, right_hi, start=first, stop=False)
    pe.matmul(out, left_hi, right_lo, start=False, stop=False)
    return pe.matmul(out, left_lo, right_hi, start=False, stop=last)


GB = 4
GROUPS = B // GB
GS = GB * S


def stage_queries(nc, x, wq, bq, ident_dram, q_parts):
    with ExitStack() as ctx:
        m = Memory(nc, ctx, "q_")
        ident = m.sb("ident", [P, P])
        w_raw = m.sb("w_raw", [P, KT, D])
        w_hi, w_lo = m.sb("w_hi", [P, KT, D], F32R), m.sb("w_lo", [P, KT, D], F32R)
        bias = m.sb("bias", [P, KT])
        eps = m.sb("eps", [P, 1])
        rows = m.sb("rows", [S, GB, D])
        stats, moments = m.sb("stats", [S, GB, 6]), m.sb("moments", [S, GB, 2])
        std, rstd = m.sb("std", [S, GB]), m.sb("rstd", [S, GB])
        normed = m.sb("normed", [S, GB, D])
        xt_hi, xt_lo = m.sb("xt_hi", [P, KT, GS], F32R), m.sb("xt_lo", [P, KT, GS], F32R)
        q_hi, q_lo = m.sb("q_hi", [P, KT, GS], F32R), m.sb("q_lo", [P, KT, GS], F32R)
        bank = [m.ps(f"bank{i}", [P, 512]) for i in range(8)]
        turned, product = bank[:4], bank[4:]

        loaded, w_split, rows_in = m.sem("loaded"), m.sem("w_split"), m.sem("rows_in")
        eps_set, stats_seen = m.sem("eps_set"), m.sem("stats_seen")
        dve_step, act_std = m.sem("dve_step"), m.sem("act_std")
        normed_ready, turned_ready = m.sem("normed_ready"), m.sem("turned_ready")
        xt_hi_ready, xt_lo_ready = m.sem("xt_hi_ready"), m.sem("xt_lo_ready")
        product_ready = m.sem("product_ready")
        q_hi_ready, q_lo_ready, stored = m.sem("q_hi_ready"), m.sem("q_lo_ready"), m.sem("stored")

        block = ctx.enter_context(nc.Block())
        x_groups = x.rearrange("(g r) s d -> g s r d", r=GB)

        @block.sync
        def _(sp):
            sp.dma_start(rows[:], x_groups[0]).then_inc(rows_in, 16)
            sp.dma_start(w_raw[:], wq.rearrange("(k p) n -> p k n", p=P)).then_inc(loaded, 16)
            sp.dma_start(bias[:], bq.rearrange("(k p) -> p k", p=P), allow_slow_non_contiguous=True).then_inc(loaded, 16)
            sp.dma_start(ident[:], ident_dram).then_inc(loaded, 16)

            def store(g):
                sp.wait_ge(q_hi_ready, g * KT + KT)
                sp.wait_ge(q_lo_ready, g * KT + KT)
                for part, t in enumerate((q_hi, q_lo)):
                    dst = q_parts[part].rearrange("(k p) n -> p k n", p=P)
                    sp.dma_start(dst[:, :, bass.ds(g * GS, GS)], f32(t[:])).then_inc(stored, 16)

            with sp.Fori(0, GROUPS - 1) as g:
                sp.wait_ge(normed_ready, g + 1)
                sp.dma_start(rows[:], x_groups[g + 1]).then_inc(rows_in, 16)
                store(g)
            store(GROUPS - 1)
            sp.wait_ge(stored, 32 * GROUPS)

        @block.vector
        def _(dve):
            dve.memset(eps[:], EPS).then_inc(eps_set, 1)
            dve.wait_ge(loaded, 48)
            dve.wait_ge(w_split, 1)
            dve.tensor_tensor(w_lo[:], w_raw[:], w_hi[:], ALU.subtract).then_inc(w_split, 1)
            STEPS = GB + GB + 1

            def normalise(g):
                step = Tally(dve_step, g * STEPS)
                dve.wait_ge(rows_in, g * 16 + 16)
                for r in range(GB):
                    step.done(dve.bn_stats(stats[:, r, :], rows[:, r, :]))
                step.wait(dve)
                dve.sem_inc(stats_seen, 1)
                for r in range(GB):
                    step.done(dve.bn_aggr(moments[:, r, :], stats[:, r, :]))
                dve.wait_ge(act_std, g + 1)
                step.done(dve.reciprocal(rstd[:], std[:]))
                step.wait(dve)
                for r in range(GB):
                    last = dve.tensor_scalar(normed[:, r, :], rows[:, r, :], moments[:, r, 0:1],
                                             rstd[:, r:r + 1], ALU.subtract, ALU.mult)
                last.then_inc(normed_ready, 1)

            def split_rows(g):
                for k in range(KT):
                    dve.wait_ge(xt_hi_ready, g * KT + k + 1)
                    dve.tensor_tensor(xt_lo[:, k, :], turned[k][:, 0:GS], xt_hi[:, k, :],
                                      ALU.subtract).then_inc(xt_lo_ready, 1)

            def split_queries(g):
                for k in range(KT):
                    dve.wait_ge(q_hi_ready, g * KT + k + 1)
                    dve.scalar_tensor_tensor(q_lo[:, k, :], product[k][:, 0:GS], bias[:, k:k + 1],
                                             q_hi[:, k, :], ALU.add, ALU.subtract).then_inc(q_lo_ready, 1)

            normalise(0)
            split_rows(0)
            with dve.Fori(0, GROUPS - 1) as g:
                normalise(g + 1)
                split_queries(g)
                split_rows(g + 1)
            split_queries(GROUPS - 1)

        @block.scalar
        def _(act):
            act.wait_ge(loaded, 48)
            act.activation(w_hi[:], w_raw[:], ACT.Copy).then_inc(w_split, 1)
            act.wait_ge(eps_set, 1)

            def roots(g):
                act.wait_ge(dve_step, g * (2 * GB + 1) + 2 * GB)
                act.activation(std[:], moments[:, :, 1], ACT.Sqrt, bias=eps[0:S, :]).then_inc(act_std, 1)

            def split_rows(g):
                for k in range(KT):
                    act.wait_ge(turned_ready, g * KT + k + 1)
                    act.activation(xt_hi[:, k, :], turned[k][:, 0:GS], ACT.Copy).then_inc(xt_hi_ready, 1)

            def split_queries(g, stores_before):
                for k in range(KT):
                    act.wait_ge(product_ready, g * KT + k + 1)
                    if k == 0 and stores_before:
                        act.wait_ge(stored, g * 32)
                    act.activation(q_hi[:, k, :], product[k][:, 0:GS], ACT.Identity,
                                   bias=bias[:, k:k + 1]).then_inc(q_hi_ready, 1)

            roots(0)
            split_rows(0)
            roots(1)
            split_queries(0, False)
            split_rows(1)
            with act.Fori(1, GROUPS - 1) as g:
                roots(g + 1)
                split_queries(g, True)
                split_rows(g + 1)
            split_queries(GROUPS - 1, True)

        @block.tensor
        def _(pe):
            pe.wait_ge(loaded, 48)

            def turn(g):
                pe.wait_ge(normed_ready, g + 1)
                for k in range(KT):
                    for r in range(GB):
                        last = pe.transpose(turned[k][:, r * S:(r + 1) * S],
                                            normed[:, r, k * P:(k + 1) * P], ident[0:S, 0:S])
                    last.then_inc(turned_ready, 1)

            def project(g):
                pe.wait_ge(xt_lo_ready, g * KT + KT)
                for n in range(KT):
                    for k in range(KT):
                        cols = slice(n * P, (n + 1) * P)
                        last = three_products(pe, product[n][:, 0:GS], w_hi[:, k, cols], w_lo[:, k, cols],
                                              xt_hi[:, k, :], xt_lo[:, k, :], k == 0, k == KT - 1)
                    last.then_inc(product_ready, 1)

            turn(0)
            pe.wait_ge(w_split, 2)
            project(0)
            turn(1)
            with pe.Fori(1, GROUPS - 1) as g:
                pe.wait_ge(q_lo_ready, g * KT)
                project(g)
                turn(g + 1)
            pe.wait_ge(q_lo_ready, (GROUPS - 1) * KT)
            project(GROUPS - 1)


CT = -(-C // P)
CPAD = CT * P
C_LAST = C - (CT - 1) * P
HALF = (C // 2 + 1) // 2 * 2
HALVES = (slice(0, HALF), slice(HALF, C))
MAX_HALVES = (slice(0, HALF), slice(C - HALF, C))
STACK = 3 * HD
SROWS = STACK + HPT
VW = 2 * HD + 2
HG = 2
PR = 4

V_PARTS, K_PARTS = 4, 2
V_HELD = 4
PARTS = {"values": V_PARTS, "keys": K_PARTS}


def front_plan():
    plan, peaks = [], 0
    parts = [(t, p) for t in range(CT) for p in range(V_PARTS)]
    spread = len(parts) - V_HELD
    for n, (t, p) in enumerate(parts[:spread]):
        plan.append(("values", t, p))
        while peaks < H and peaks * spread < n * H:
            plan.append(("peak", peaks, 0))
            peaks += 1
            if peaks % HPT == 2 and peaks > HPT:
                plan.append(("shift", peaks // HPT - 1, 0))
    plan += [("peak", n, 0) for n in range(peaks, H)]
    held = [("values", t, p) for t, p in parts[spread:]]
    return plan + held[:2] + [("scores", 0, 0)] + held[2:3] + [("shift", KT - 1, 0)] + held[3:]


WORK = [("turn", t) for t in range(CT)] + [("keys", n) for n in range(2 * KT)]
FIRST_WORK = [(kind, i, p) for kind, i in WORK for p in range(PARTS.get(kind, 1))]
WORK_AFTER = (1, 1, 2, 1, 1, 1, 1, 2, 1, 1, 2, 1, 1, 2, 1, 1, 1, 1)


def batch_plan(with_next):
    plan = front_plan()
    for h in range(H + 2):
        if 0 < h < H:
            plan.append(("scores", h, 0))
        if with_next:
            at = sum(WORK_AFTER[:h])
            plan += FIRST_WORK[at:at + WORK_AFTER[h]]
        if h >= 2:
            plan.append(("mix", h - 2, 0))
    return plan


A_USES = CT + CT + 2 * KT
A_FIRST = CT + 2 * KT


def work_use(kind, index, b):
    if kind == "values":
        return index, A_FIRST + b * A_USES + index
    at = WORK.index((kind, index))
    return (at, at) if b is None else (CT + at, A_FIRST + b * A_USES + CT + at)


def stage_cross(nc, context, wk, bk, wv, ident_dram, neg_ident_dram, q_parts, mix_parts, prob_sums):
    with ExitStack() as ctx:
        m = Memory(nc, ctx, "c_")
        ident = m.sb("ident", [P, P])
        neg_ident = m.sb("neg_ident", [HPT, HPT])
        rows = m.sb("rows", [P, CT, D])
        wk_hi, wk_lo = m.sb("wk_hi", [P, KT, D], F32R), m.sb("wk_lo", [P, KT, D], F32R)
        wv_hi, wv_lo = m.sb("wv_hi", [P, KT, D], F32R), m.sb("wv_lo", [P, KT, D], F32R)
        key_bias = m.sb("key_bias", [P, KT])
        ct_hi, ct_lo = m.sb("ct_hi", [P, KT, C], F32R), m.sb("ct_lo", [P, KT, C], F32R)
        k_hi = [m.sb(f"k_hi{i}", [P, C], F32R) for i in range(2)]
        k_lo = [m.sb(f"k_lo{i}", [P, C], F32R) for i in range(2)]
        k_stack = m.sb("k_stack", [SROWS, H, CPAD], F32R)
        q_stack = m.sb("q_stack", [SROWS, H, S], F32R)
        v = m.sb("v", [P, CT, H, VW], F32R)
        peak = m.sb("peak", [S, H])
        prob = [m.sb(f"prob{i}", [P, CT, S]) for i in range(2)]
        parted = [m.sb(f"parted{i}", [P, CT, 2, S], F32R) for i in range(PR)]
        mixed = m.sb("mixed", [VW, H, S])
        raw_w = [m.sb(f"raw_w{n}", [P, KT, D]) for n in range(2)]

        work = [m.ps(f"work{i}", [P, 512]) for i in range(2)]
        pair = [m.ps(f"pair{i}", [P, 2, 512]) for i in range(2)]
        mix = [m.ps(f"mix{i}", [P, 512]) for i in range(2)]
        shift_bank = mix[0][:, HG * 2 * S:HG * 2 * S + S]

        consts_in, w_hi_done, w_lo_done = m.sem("consts_in"), m.sem("w_hi_done"), m.sem("w_lo_done")
        w_in = [m.sem(f"w_in{n}") for n in range(2)]
        cleared = m.sem("cleared")
        rows_in = m.sem("rows_in")
        q_in = [m.sem(f"q_in{half}") for half in range(2)]
        k_in = [m.sem(f"k_in{n}") for n in range(KT)]
        work_full, work_hi, work_lo = m.sem("work_full"), m.sem("work_hi"), m.sem("work_lo")
        peak_full, peak_done = m.sem("peak_full"), m.sem("peak_done")
        shift_full, shift_done = m.sem("shift_full"), m.sem("shift_done")
        scores_full, exp_hi_done, exp_done = m.sem("scores_full"), m.sem("exp_hi_done"), m.sem("exp_done")
        p_lo_done, mix_done = m.sem("p_lo_done"), m.sem("mix_done")
        mixed_done, stored = m.sem("mixed_done"), m.sem("stored")

        block = ctx.enter_context(nc.Block())

        def c_rows(t):
            return P if t < CT - 1 else C_LAST

        def stack_queries(engine, b, half):
            heads = slice(half * H // 2, (half + 1) * H // 2)
            for n, part in enumerate((0, 0, 1)):
                src = q_parts[part].rearrange("(h d) n -> d h n", d=HD)[:, heads, bass.ds(b * S, S)]
                engine.dma_start(f32(q_stack[n * HD:(n + 1) * HD, heads, :]), src).then_inc(q_in[half], 16)

        @block.sync
        def _(sp):
            for n, (raw, w) in enumerate(zip(raw_w, (wk, wv))):
                sp.dma_start(raw[:], w.rearrange("(k p) n -> p k n", p=P)).then_inc(w_in[n], 16)
            sp.dma_start(ident[:], ident_dram).then_inc(consts_in, 16)
            sp.dma_start(neg_ident[:], neg_ident_dram).then_inc(consts_in, 16)
            sp.dma_start(key_bias[:], bk.rearrange("(k p) -> p k", p=P), allow_slow_non_contiguous=True).then_inc(consts_in, 16)

            def load_rows(b):
                whole = (CT - 1) * P
                sp.dma_start(rows[:, 0:CT - 1, :], context[b, 0:whole, :].rearrange("(t p) d -> p t d", p=P)
                             ).then_inc(rows_in, 16)
                sp.dma_start(rows[0:C_LAST, CT - 1, :], context[b, whole:C, :]).then_inc(rows_in, 16)

            def stack_keys(n):
                for j in range(HPT):
                    for place, part in enumerate((k_hi, k_lo, k_hi)):
                        sp.dma_start(f32(k_stack[place * HD:(place + 1) * HD, n * HPT + j, 0:C]),
                                     f32(part[n % 2][j * HD:(j + 1) * HD, :])).then_inc(k_in[n], 16)

            def store_mix(b):
                sp.wait_ge(mixed_done, (b + 1) * (H // HG))
                for n in range(2):
                    dst = mix_parts[n].rearrange("(h d) n -> d h n", d=HD)[:, :, bass.ds(b * S, S)]
                    sp.dma_start(dst, mixed[n * HD:(n + 1) * HD, :, :]).then_inc(stored, 16)
                sp.dma_start(prob_sums.rearrange("(a h) n -> a h n", a=1)[:, :, bass.ds(b * S, S)],
                             mixed[2 * HD:2 * HD + 1, :, :]).then_inc(stored, 16)

            load_rows(0)
            sp.wait_ge(cleared, 2)
            for half in range(2):
                stack_queries(sp, 0, half)
            for n in range(KT):
                sp.wait_ge(work_lo, CT + 2 * n + 2)
                stack_keys(n)

            with sp.Fori(0, B - 1) as b:
                sp.wait_ge(work_full, b * A_USES + WORK.index(("turn", CT - 1)) + 1)
                load_rows(b + 1)
                for n in range(KT):
                    use = work_use("keys", 2 * n + 1, b)[1]
                    sp.wait_ge(work_lo, use + 1)
                    stack_keys(n)
                store_mix(b)
            store_mix(B - 1)
            sp.wait_ge(stored, 48 * B)

        @block.gpsimd
        def _(pool):
            fills = [(k_stack[:, :, C:CPAD], 0.0), (k_stack[STACK:SROWS, :, 0:C], 1.0),
                     (v[:, CT - 1, :, :], 0.0), (v[0:C_LAST, CT - 1, :, 2 * HD:2 * HD + 1], 1.0),
                     (v[:, 0:CT - 1, :, 2 * HD + 1:VW], 0.0), (v[:, 0:CT - 1, :, 2 * HD:2 * HD + 1], 1.0)]
            for n, (part, value) in enumerate(fills):
                if n:
                    pool.wait_ge(cleared, n)
                pool.memset(f32(part), value).then_inc(cleared, 1)

        @block.scalar
        def _(act):
            for n, w in enumerate((wk_hi, wv_hi)):
                act.wait_ge(w_in[n], 16)
                act.activation(w[:], raw_w[n][:], ACT.Copy).then_inc(w_hi_done, 1)
            act.wait_ge(consts_in, 48)
            act.wait_ge(cleared, 6)

            def emit(kind, i, part, b, with_next=False):
                if part < PARTS.get(kind, 1) - 1:
                    return
                if kind in ("values", "turn", "keys"):
                    local, use = work_use(kind, i, b)
                    bank = work[local % 2]
                    act.wait_ge(work_full, use + 1)
                    if kind == "values":
                        r = c_rows(i)
                        ins = act.activation(v[0:r, i, :, 0:HD],
                                             bank[0:r, :].rearrange("p (h d) -> p h d", d=HD), ACT.Copy)
                    elif kind == "turn":
                        r = c_rows(i)
                        ins = act.activation(ct_hi[:, :, i * P:i * P + r],
                                             bank[:, 0:KT * r].rearrange("p (k c) -> p k c", k=KT), ACT.Copy)
                    else:
                        n, half = divmod(i, 2)
                        if half == 0 and not (b is None and n < 2):
                            before = (n + 2) % KT
                            times = 0 if b is None else b + 1
                            act.wait_ge(k_in[before], (times + (1 if n >= 2 else 0)) * 16 * 3 * HPT)
                        cols = HALVES[half]
                        ins = act.activation(k_hi[n % 2][:, cols], bank[:, 0:cols.stop - cols.start],
                                             ACT.Identity, bias=key_bias[:, n:n + 1])
                    ins.then_inc(work_hi, 1)
                elif kind == "scores":
                    act.wait_ge(scores_full, b * H + i + 1)
                    logits = pair[i % 2][:, :, 0:CT // 2 * S].rearrange("p a (t s) -> p a t s", s=S)
                    if i >= PR:
                        act.wait_ge(mix_done, b * H + i - PR + 1)
                    act.activation(parted[i % PR][:, :, 0, :].rearrange("p (a t) s -> p a t s", a=2), logits,
                                   ACT.Exp).then_inc(exp_hi_done, 1)
                    if i >= 2:
                        act.wait_ge(p_lo_done, b * H + i - 1)
                    act.activation(prob[i % 2][:, :, :].rearrange("p (a t) s -> p a t s", a=2), logits,
                                   ACT.Exp).then_inc(exp_done, 1)
                    if with_next and i % (H // 2) == H // 2 - 1:
                        stack_queries(act, b + 1, i // (H // 2))

            for kind, i, part in FIRST_WORK:
                emit(kind, i, part, None)
            with act.Fori(0, B - 1) as b:
                for kind, i, part in batch_plan(True):
                    emit(kind, i, part, b, True)
            for kind, i, part in batch_plan(False):
                emit(kind, i, part, B - 1)

        @block.vector
        def _(dve):
            for n, (hi, lo) in enumerate(((wk_hi, wk_lo), (wv_hi, wv_lo))):
                dve.wait_ge(w_hi_done, n + 1)
                dve.tensor_tensor(lo[:], raw_w[n][:], hi[:], ALU.subtract).then_inc(w_lo_done, 1)
            dve.wait_ge(consts_in, 48)
            dve.wait_ge(cleared, 6)

            def emit(kind, i, part, b, stored_before=True):
                if part < PARTS.get(kind, 1) - 1:
                    return
                if kind in ("values", "turn", "keys"):
                    local, use = work_use(kind, i, b)
                    bank = work[local % 2]
                    dve.wait_ge(work_hi, use + 1)
                    if kind == "values":
                        r = c_rows(i)
                        ins = dve.tensor_tensor(v[0:r, i, :, HD:2 * HD],
                                                bank[0:r, :].rearrange("p (h d) -> p h d", d=HD),
                                                v[0:r, i, :, 0:HD], ALU.subtract)
                    elif kind == "turn":
                        r = c_rows(i)
                        cols = slice(i * P, i * P + r)
                        ins = dve.tensor_tensor(ct_lo[:, :, cols],
                                                bank[:, 0:KT * r].rearrange("p (k c) -> p k c", k=KT),
                                                ct_hi[:, :, cols], ALU.subtract)
                    else:
                        n, half = divmod(i, 2)
                        cols = HALVES[half]
                        ins = dve.scalar_tensor_tensor(k_lo[n % 2][:, cols], bank[:, 0:cols.stop - cols.start],
                                                       key_bias[:, n:n + 1], k_hi[n % 2][:, cols],
                                                       ALU.add, ALU.subtract)
                    ins.then_inc(work_lo, 1)
                elif kind == "peak":
                    dve.wait_ge(peak_full, b * H + i + 1)
                    dve.tensor_reduce(peak[:, i:i + 1], pair[i % 2][0:S, :, 0:HALF], AX.XY, ALU.max
                                      ).then_inc(peak_done, 1)
                elif kind == "shift":
                    dve.wait_ge(shift_full, b * KT + i + 1)
                    dve.tensor_tensor(q_stack[STACK:SROWS, i * HPT:(i + 1) * HPT, :],
                                      repeated(shift_bank[0:HPT, :].unsqueeze(1), 1, HPT),
                                      repeated(neg_ident[:].unsqueeze(2), 2, S), ALU.mult
                                      ).then_inc(shift_done, 1)
                elif kind == "scores":
                    dve.wait_ge(exp_done, b * H + i + 1)
                    if i >= PR:
                        dve.wait_ge(mix_done, b * H + i - PR + 1)
                    p = parted[i % PR]
                    dve.tensor_tensor(p[:, :, 1, :], prob[i % 2][:], p[:, :, 0, :], ALU.subtract
                                      ).then_inc(p_lo_done, 1)
                elif kind == "mix" and i % HG == HG - 1:
                    g = i // HG
                    dve.wait_ge(mix_done, b * H + i + 1)
                    if g == 0 and stored_before:
                        dve.wait_ge(stored, b * 48)
                    dve.tensor_reduce(mixed[:, g * HG:(g + 1) * HG, :],
                                      mix[g % 2][0:VW, 0:HG * 2 * S].rearrange("p (h a s) -> p h s a", a=2, s=S),
                                      AX.X, ALU.add).then_inc(mixed_done, 1)

            for kind, i, part in FIRST_WORK:
                emit(kind, i, part, None)
            for kind, i, part in batch_plan(True):
                emit(kind, i, part, 0, False)
            with dve.Fori(1, B - 1) as b:
                for kind, i, part in batch_plan(True):
                    emit(kind, i, part, b)
            for kind, i, part in batch_plan(False):
                emit(kind, i, part, B - 1)

        @block.tensor
        def _(pe):
            pe.wait_ge(consts_in, 48)

            def emit(kind, i, part, b):
                if kind in ("values", "turn", "keys"):
                    local, use = work_use(kind, i, b)
                    bank = work[local % 2]
                    if part == 0 and not (b is None and local < 2):
                        pe.wait_ge(work_lo, use - 1)
                        pe.wait_ge(work_hi, use - 1)
                    if kind == "turn":
                        if i == 0:
                            pe.wait_ge(rows_in, 32 if b is None else b * 32 + 64)
                        r = c_rows(i)
                        for k in range(KT):
                            last = pe.transpose(bank[:, k * r:(k + 1) * r], rows[0:r, i, k * P:(k + 1) * P],
                                                ident[0:r, 0:r])
                    elif kind == "keys":
                        n, half = divmod(i, 2)
                        cols = HALVES[half]
                        if n == 0 and part == 0:
                            tile_end = -(-cols.stop // P)
                            pe.wait_ge(work_lo, work_use("turn", tile_end - 1, b)[1] + 1)
                        for k in range(part * KT // K_PARTS, (part + 1) * KT // K_PARTS):
                            wcols = slice(n * P, (n + 1) * P)
                            last = three_products(pe, bank[:, 0:cols.stop - cols.start], wk_hi[:, k, wcols],
                                                  wk_lo[:, k, wcols], ct_hi[:, k, cols], ct_lo[:, k, cols],
                                                  k == 0, k == KT - 1)
                    else:
                        r = c_rows(i)
                        cols = slice(i * P, i * P + r)
                        for k in range(part * KT // V_PARTS, (part + 1) * KT // V_PARTS):
                            last = three_products(pe, bank[0:r, :], ct_hi[:, k, cols], ct_lo[:, k, cols],
                                                  wv_hi[:, k, :], wv_lo[:, k, :], k == 0, k == KT - 1)
                    if part == PARTS.get(kind, 1) - 1:
                        last.then_inc(work_full, 1)
                elif kind == "peak":
                    if i % (H // 2) == 0:
                        pe.wait_ge(q_in[i // (H // 2)], b * 48 + 48)
                    if i % HPT == 0:
                        pe.wait_ge(k_in[i // HPT], (b + 1) * 16 * 3 * HPT)
                    if i >= 2:
                        pe.wait_ge(peak_done, b * H + i - 1)
                    for bank, cols in enumerate(MAX_HALVES):
                        last = pe.matmul(pair[i % 2][0:S, bank, 0:HALF], q_stack[0:STACK, i, :],
                                         k_stack[0:STACK, i, cols], start=True, stop=True)
                    last.then_inc(peak_full, 1)
                elif kind == "shift":
                    pe.wait_ge(peak_done, b * H + (i + 1) * HPT)
                    if i >= 1:
                        pe.wait_ge(shift_done, b * KT + i)
                    pe.transpose(shift_bank[0:HPT, :], peak[:, i * HPT:(i + 1) * HPT], ident[0:S, 0:S]
                                 ).then_inc(shift_full, 1)
                elif kind == "scores":
                    if i % HPT == 0:
                        pe.wait_ge(shift_done, b * KT + i // HPT + 1)
                    if i < 2:
                        pe.wait_ge(peak_done, b * H + H - 1 + i)
                    else:
                        pe.wait_ge(exp_done, b * H + i - 1)
                    for t in range(CT):
                        col = t % (CT // 2) * S
                        last = pe.matmul(pair[i % 2][:, t // (CT // 2), col:col + S],
                                         k_stack[:, i, t * P:(t + 1) * P], q_stack[:, i, :],
                                         start=True, stop=True)
                    last.then_inc(scores_full, 1)
                elif kind == "mix":
                    g, at = divmod(i, HG)
                    if i == 0:
                        pe.wait_ge(shift_done, b * KT + KT)
                        pe.wait_ge(work_lo, work_use("values", CT - 1, b)[1] + 1)
                    if at == 0 and g >= 2:
                        pe.wait_ge(mixed_done, b * (H // HG) + g - 1)
                    pe.wait_ge(p_lo_done, b * H + i + 1)
                    for t in range(CT):
                        last = pe.matmul(mix[g % 2][0:VW, at * 2 * S:(at + 1) * 2 * S], v[:, t, i, :],
                                         parted[i % PR][:, t, :, :].rearrange("p a s -> p (a s)"),
                                         start=(t == 0), stop=(t == CT - 1))
                    last.then_inc(mix_done, 1)

            for kind, i, part in FIRST_WORK:
                if (kind, i, part) == ("keys", 0, 0):
                    pe.wait_ge(w_lo_done, 2)
                    pe.wait_ge(cleared, 6)
                emit(kind, i, part, None)
            with pe.Fori(0, B - 1) as b:
                for kind, i, part in batch_plan(True):
                    emit(kind, i, part, b)
            for kind, i, part in batch_plan(False):
                emit(kind, i, part, B - 1)


TILES = ROWS // P
A_LOADS = 2 + HPT
A_STEPS = 2
X1_STEPS = 4
SIM_STEPS = 6


def stage_rows(nc, x, mix_parts, prob_sums, inverses, bv, g_xattn, wo, bo, g_info, w_qkv, ident_dram, x1_dram, qkv_dram, sim_dram):
    with ExitStack() as ctx:
        m = Memory(nc, ctx, "r_")
        ident = m.sb("ident", [P, P])
        raw = [m.sb(f"raw{i}", [P, KT, D]) for i in range(4)]
        w_hi = [m.sb(f"w_hi{i}", [P, KT, D], F32R) for i in range(4)]
        w_lo = [m.sb(f"w_lo{i}", [P, KT, D], F32R) for i in range(4)]
        gate, gate_bias = m.sb("gate", [P, 1]), m.sb("gate_bias", [P, D])
        guide, guide_sq = m.sb("guide", [P, D]), m.sb("guide_sq", [P, D])
        guide_norm = m.sb("guide_norm", [P, 3, H])
        eps = m.sb("eps", [P, 1])
        value_bias = m.sb("value_bias", [P, KT])
        parts = m.sb("parts", [P, 3, KT, P])
        sums = m.sb("sums", [P, H * ROWS // P])
        attn = m.sb("attn", [P, KT, P])
        x_rows = m.sb("x_rows", [P, D])
        at_hi, at_lo = m.sb("at_hi", [P, KT, P], F32R), m.sb("at_lo", [P, KT, P], F32R)
        x1, normed = m.sb("x1", [P, D]), m.sb("normed", [P, D])
        nt_hi, nt_lo = m.sb("nt_hi", [P, KT, P], F32R), m.sb("nt_lo", [P, KT, P], F32R)
        stats, moments, std, rstd = m.sb("stats", [P, 6]), m.sb("moments", [P, 2]), m.sb("std", [P, 1]), m.sb("rstd", [P, 1])
        qkv = m.sb("qkv", [P, 3, D])
        q_sq, q_dot = m.sb("q_sq", [P, D]), m.sb("q_dot", [P, D])
        sq_sum, dot_sum = m.sb("sq_sum", [P, H]), m.sb("dot_sum", [P, H])
        q_norm, cosine = m.sb("q_norm", [P, 2, H]), m.sb("cosine", [P, H])
        sim = m.sb("sim", [P, 1])
        turned_x, mixed = m.ps("turned_x", [P, KT, P]), m.ps("mixed", [P, D])
        product = [m.ps(f"product{i}", [P, D]) for i in range(3)]

        consts_in, w_hi_done, w_lo_done = m.sem("consts_in"), m.sem("w_hi_done"), m.sem("w_lo_done")
        w_in = [m.sem(f"w_in{i}") for i in range(4)]
        sums_in, sums_done, inv_stored = m.sem("sums_in"), m.sem("sums_done"), m.sem("inv_stored")
        set_up, act_setup, stats_seen = m.sem("set_up"), m.sem("act_setup"), m.sem("stats_seen")
        a_in, x_in = m.sem("a_in"), m.sem("x_in")
        a_step, a_joined, a_hi, a_lo, a_mixed = m.sem("a_step"), m.sem("a_joined"), m.sem("a_hi"), m.sem("a_lo"), m.sem("a_mixed")
        x1_ready, x1_step, act_std, normed_ready = m.sem("x1_ready"), m.sem("x1_step"), m.sem("act_std"), m.sem("normed_ready")
        n_turned, n_hi, n_lo = m.sem("n_turned"), m.sem("n_hi"), m.sem("n_lo")
        q_full, kv_full, q_out, kv_out = m.sem("q_full"), m.sem("kv_full"), m.sem("q_out"), m.sem("kv_out")
        q_sq_done, q_root, sim_step, sim_ready = m.sem("q_sq_done"), m.sem("q_root"), m.sem("sim_step"), m.sem("sim_ready")
        x1_stored, q_stored, kv_stored, sim_stored = (
            m.sem("x1_stored"), m.sem("q_stored"), m.sem("kv_stored"), m.sem("sim_stored"))

        block = ctx.enter_context(nc.Block())

        @block.sync
        def _(sp):
            by_row = lambda dram: dram.rearrange("h (a n) -> (h a) n", a=P // H)
            sp.dma_start(sums[:], by_row(prob_sums)).then_inc(sums_in, 16)
            for n in range(4):
                src = wo if n == 0 else w_qkv[:, (n - 1) * D:n * D]
                sp.dma_start(raw[n][:], src.rearrange("(k p) n -> p k n", p=P)).then_inc(w_in[n], 16)
                if n == 0:
                    sp.wait_ge(sums_done, 1)
                    sp.dma_start(by_row(inverses), sums[:]).then_inc(inv_stored, 16)
            sp.dma_start(x_rows[:], x[0:P, :]).then_inc(x_in, 16)
            sp.dma_start(ident[:], ident_dram).then_inc(consts_in, 16)
            sp.dma_start(gate[:], row_of(g_xattn, P)).then_inc(consts_in, 16)
            sp.dma_start(gate_bias[:], row_of(bo, P)).then_inc(consts_in, 16)
            sp.dma_start(guide[:], repeated(g_info[0, 0:1, :], 0, P)).then_inc(consts_in, 16)
            sp.dma_start(value_bias[:], bv.rearrange("(k p) -> p k", p=P), allow_slow_non_contiguous=True
                         ).then_inc(consts_in, 16)
            sp.wait_ge(inv_stored, 16)

            def load_parts(t):
                for n in range(2):
                    src = mix_parts[n].rearrange("(k p) n -> p k n", p=P)[:, :, bass.ds(t * P, P)]
                    sp.dma_start(parts[:, n, :, :], src).then_inc(a_in, 16)
                for j in range(HPT):
                    src = inverses.rearrange("(k a) n -> a k n", a=HPT)[j:j + 1, :, bass.ds(t * P, P)]
                    sp.dma_start(parts[j * HD:(j + 1) * HD, 2, :, :], repeated(src, 0, HD)).then_inc(a_in, 16)

            def load_x(t):
                sp.wait_ge(x1_ready, t)
                sp.dma_start(x_rows[:], x[bass.ds(t * P, P), :]).then_inc(x_in, 16)

            def store_x1(t):
                sp.wait_ge(x1_ready, t + 1)
                sp.dma_start(x1_dram[bass.ds(t * P, P), :], x1[:]).then_inc(x1_stored, 16)

            def store_qkv(t):
                dst = qkv_dram[bass.ds(t * P, P), :].rearrange("p (a n) -> p a n", n=D)
                sp.wait_ge(q_out, t + 1)
                sp.dma_start(dst[:, 0, :], qkv[:, 0, :]).then_inc(q_stored, 16)
                sp.wait_ge(sim_ready, t + 1)
                sp.wait_ge(kv_out, 2 * t + 2)
                sp.dma_start(dst[:, 1:3, :], qkv[:, 1:3, :]).then_inc(kv_stored, 16)
                sp.dma_start(sim_dram[bass.ds(t * P, P), :], sim[:]).then_inc(sim_stored, 16)

            load_parts(0)
            sp.wait_ge(a_joined, 1)
            load_parts(1)
            store_x1(0)
            load_x(1)
            with sp.Fori(0, TILES - 2) as t:
                sp.wait_ge(a_joined, t + 2)
                load_parts(t + 2)
                store_x1(t + 1)
                load_x(t + 2)
                store_qkv(t)
            store_x1(TILES - 1)
            store_qkv(TILES - 2)
            store_qkv(TILES - 1)
            sp.wait_ge(x1_stored, 16 * TILES)
            sp.wait_ge(q_stored, 16 * TILES)
            sp.wait_ge(kv_stored, 16 * TILES)
            sp.wait_ge(sim_stored, 16 * TILES)

        @block.gpsimd
        def _(pool):
            pool.wait_ge(consts_in, 80)

            def join_attn(t, follows):
                step = Tally(a_step, t * A_STEPS)
                pool.wait_ge(a_in, (t + 1) * 16 * A_LOADS)
                if follows:
                    pool.wait_ge(a_hi, t)
                    pool.wait_ge(a_lo, t)
                step.done(pool.tensor_tensor(attn[:], parts[:, 0, :, :], parts[:, 1, :, :], ALU.add))
                step.wait(pool)
                pool.tensor_tensor(attn[:], attn[:], parts[:, 2, :, :], ALU.mult).then_inc(a_joined, 1)
                pool.wait_ge(a_joined, t + 1)
                step.done(pool.tensor_tensor(attn[:], attn[:], repeated(value_bias[:].unsqueeze(2), 2, P), ALU.add))

            join_attn(0, False)
            with pool.Fori(1, TILES) as t:
                join_attn(t, True)

        @block.scalar
        def _(act):
            for n in range(4):
                act.wait_ge(w_in[n], 16)
                act.activation(w_hi[n][:], raw[n][:], ACT.Copy).then_inc(w_hi_done, 1)
            act.wait_ge(consts_in, 80)
            act.activation(gate[:], gate[:], ACT.Tanh).then_inc(act_setup, 1)
            act.wait_ge(set_up, 2)
            act.activation(guide_norm[:, 1, :], guide_norm[:, 0, :], ACT.Sqrt).then_inc(act_setup, 1)

            def split_attn(t, follows=True):
                act.wait_ge(a_step, t * A_STEPS + A_STEPS)
                if follows:
                    act.wait_ge(a_mixed, t)
                act.activation(at_hi[:], attn[:], ACT.Copy).then_inc(a_hi, 1)

            def root(t):
                act.wait_ge(x1_step, t * X1_STEPS + X1_STEPS - 1)
                act.activation(std[:], moments[:, 1:2], ACT.Sqrt, bias=eps[:]).then_inc(act_std, 1)

            def split_normed(t):
                act.wait_ge(n_turned, t + 1)
                act.activation(nt_hi[:], turned_x[:], ACT.Copy).then_inc(n_hi, 1)

            def queries(t, stored_before):
                act.wait_ge(q_full, t + 1)
                if stored_before:
                    act.wait_ge(q_stored, 16 * t)
                    act.wait_ge(sim_ready, t)
                act.activation(q_sq[:], product[0][:], ACT.Square).then_inc(q_sq_done, 1)
                act.activation(qkv[:, 0, :], product[0][:], ACT.Copy).then_inc(q_out, 1)

            def keys_values(t, stored_before):
                if stored_before:
                    act.wait_ge(kv_stored, 16 * t)
                for n in (1, 2):
                    act.wait_ge(kv_full, 2 * t + n)
                    act.activation(qkv[:, n, :], product[n][:], ACT.Copy).then_inc(kv_out, 1)

            def query_root(t):
                act.wait_ge(sim_step, t * SIM_STEPS + 2)
                act.activation(q_norm[:, 0, :], sq_sum[:], ACT.Sqrt).then_inc(q_root, 1)

            def body(t, stored_before, more_attn=True):
                split_normed(t)
                root(t + 1)
                queries(t, stored_before)
                query_root(t)
                keys_values(t, stored_before)
                if more_attn:
                    split_attn(t + 2)

            split_attn(0, False)
            root(0)
            split_attn(1)
            body(0, False)
            with act.Fori(1, TILES - 2) as t:
                body(t, True)
            body(TILES - 2, True, False)
            split_normed(TILES - 1)
            queries(TILES - 1, True)
            query_root(TILES - 1)
            keys_values(TILES - 1, True)

        @block.vector
        def _(dve):
            dve.wait_ge(sums_in, 16)
            dve.reciprocal(sums[:], sums[:]).then_inc(sums_done, 1)
            for n in range(4):
                dve.wait_ge(w_hi_done, n + 1)
                dve.tensor_tensor(w_lo[n][:], raw[n][:], w_hi[n][:], ALU.subtract).then_inc(w_lo_done, 1)
            dve.wait_ge(consts_in, 80)
            by_head = guide[:].rearrange("p (h d) -> p h d", d=HD)
            step = Tally(set_up)
            step.done(dve.memset(eps[:], EPS))
            dve.tensor_tensor(guide_sq[:], guide[:], guide[:], ALU.mult).then_inc(sim_step, 1)
            dve.wait_ge(sim_step, 1)
            step.done(dve.tensor_reduce(guide_norm[:, 0, :], guide_sq[:].rearrange("p (h d) -> p h d", d=HD),
                                        AX.X, ALU.add))
            dve.wait_ge(act_setup, 2)
            step.done(dve.reciprocal(guide_norm[:, 2, :], guide_norm[:, 1, :]))
            step.wait(dve)
            step.done(dve.tensor_tensor(by_head, by_head, repeated(guide_norm[:, 2, :].unsqueeze(2), 2, HD), ALU.mult))
            step.done(dve.tensor_scalar(gate_bias[:], gate_bias[:], gate[:], None, ALU.mult))
            step.wait(dve)

            def split_attn(t):
                dve.wait_ge(a_hi, t + 1)
                dve.tensor_tensor(at_lo[:], attn[:], at_hi[:], ALU.subtract).then_inc(a_lo, 1)

            def residual(t, stored_before):
                step = Tally(x1_step, t * X1_STEPS)
                dve.wait_ge(a_mixed, t + 1)
                dve.wait_ge(x_in, t * 16 + 16)
                if stored_before:
                    dve.wait_ge(x1_stored, 16 * t)
                step.done(dve.scalar_tensor_tensor(x1[:], mixed[:], gate[:], x_rows[:], ALU.mult, ALU.add))
                step.wait(dve)
                dve.tensor_tensor(x1[:], x1[:], gate_bias[:], ALU.add).then_inc(x1_ready, 1)
                dve.wait_ge(x1_ready, t + 1)
                step.done(dve.bn_stats(stats[:], x1[:]))
                step.wait(dve)
                dve.sem_inc(stats_seen, 1)
                step.done(dve.bn_aggr(moments[:], stats[:]))
                dve.wait_ge(act_std, t + 1)
                step.done(dve.reciprocal(rstd[:], std[:]))
                step.wait(dve)
                if stored_before:
                    dve.wait_ge(n_turned, t)
                dve.tensor_scalar(normed[:], x1[:], moments[:, 0:1], rstd[:], ALU.subtract, ALU.mult
                                  ).then_inc(normed_ready, 1)

            def split_normed(t):
                dve.wait_ge(n_hi, t + 1)
                dve.tensor_tensor(nt_lo[:], turned_x[:], nt_hi[:], ALU.subtract).then_inc(n_lo, 1)

            def query_sums(t):
                step = Tally(sim_step, t * SIM_STEPS + 1)
                dve.wait_ge(q_sq_done, t + 1)
                step.done(dve.tensor_reduce(sq_sum[:], q_sq[:].rearrange("p (h d) -> p h d", d=HD), AX.X, ALU.add))
                dve.wait_ge(q_out, t + 1)
                step.done(dve.tensor_tensor(q_dot[:], qkv[:, 0, :], guide[:], ALU.mult))
                step.wait(dve)
                step.done(dve.tensor_reduce(dot_sum[:], q_dot[:].rearrange("p (h d) -> p h d", d=HD), AX.X, ALU.add))
                return step

            def similarity(t, step, stored_before):
                dve.wait_ge(q_root, t + 1)
                step.done(dve.reciprocal(q_norm[:, 1, :], q_norm[:, 0, :]))
                step.wait(dve)
                step.done(dve.tensor_tensor(cosine[:], dot_sum[:], q_norm[:, 1, :], ALU.mult))
                step.wait(dve)
                step.done(dve.tensor_scalar(cosine[:], cosine[:], 1.0 / H, None, ALU.mult))
                step.wait(dve)
                if stored_before:
                    dve.wait_ge(sim_stored, 16 * t)
                dve.tensor_reduce(sim[:], cosine[:], AX.X, ALU.add).then_inc(sim_ready, 1)

            def body(t, more_attn=True):
                split_normed(t)
                residual(t + 1, True)
                similarity(t, query_sums(t), True)
                if more_attn:
                    split_attn(t + 2)

            split_attn(0)
            residual(0, False)
            split_attn(1)
            split_normed(0)
            residual(1, True)
            similarity(0, query_sums(0), False)
            split_attn(2)
            with dve.Fori(1, TILES - 2) as t:
                body(t)
            body(TILES - 2, False)
            split_normed(TILES - 1)
            similarity(TILES - 1, query_sums(TILES - 1), True)

        @block.tensor
        def _(pe):
            pe.wait_ge(consts_in, 80)

            def mix_attn(t):
                pe.wait_ge(a_lo, t + 1)
                for k in range(KT):
                    last = three_products(pe, mixed[:], at_hi[:, k, :], at_lo[:, k, :], w_hi[0][:, k, :],
                                          w_lo[0][:, k, :], k == 0, k == KT - 1)
                last.then_inc(a_mixed, 1)

            def turn_normed(t):
                pe.wait_ge(normed_ready, t + 1)
                for k in range(KT):
                    last = pe.transpose(turned_x[:, k, :], normed[:, k * P:(k + 1) * P], ident[:])
                last.then_inc(n_turned, 1)

            def project(n):
                for k in range(KT):
                    last = three_products(pe, product[n][:], nt_hi[:, k, :], nt_lo[:, k, :], w_hi[n + 1][:, k, :],
                                          w_lo[n + 1][:, k, :], k == 0, k == KT - 1)
                last.then_inc(q_full if n == 0 else kv_full, 1)

            def project_all(t, follows):
                pe.wait_ge(n_lo, t + 1)
                if follows:
                    pe.wait_ge(q_out, t)
                project(0)
                if follows:
                    pe.wait_ge(kv_out, 2 * t)
                project(1)
                project(2)

            def body(t, follows):
                turn_normed(t)
                mix_attn(t + 1)
                project_all(t, follows)

            pe.wait_ge(w_lo_done, 1)
            mix_attn(0)
            pe.wait_ge(w_lo_done, 4)
            body(0, False)
            with pe.Fori(1, TILES - 1) as t:
                body(t, True)
            turn_normed(TILES - 1)
            project_all(TILES - 1, True)


QR = S + REG
TW = S + QR


def stage_self(nc, qkv_dram, sim_dram, x1_dram, table_dram, g_ffn, w_proj, b_proj, ident_dram, fold_dram, out):
    with ExitStack() as ctx:
        m = Memory(nc, ctx, "s_")
        ident, fold = m.sb("ident", [P, P]), m.sb("fold", [QR, S])
        raw = m.sb("raw", [P, KT, D])
        w_hi, w_lo = m.sb("w_hi", [P, KT, D], F32R), m.sb("w_lo", [P, KT, D], F32R)
        gate, gate_bias = m.sb("gate", [P, 1]), m.sb("gate_bias", [S, D])
        sim = m.sb("sim", [B, S])
        ends, ends_all = m.sb("ends", [B, 2]), m.sb("ends_all", [B, 2])
        low_high = m.sb("low_high", [1, 2])
        ones = m.sb("ones", [1, B])
        spread = m.sb("spread", [B, 2])
        classes = m.sb("classes", [B, 2, QR])
        tables = m.sb("tables", [B, 2, TW], BF16)
        table = m.sb("table", [P, TW], BF16)
        qk = m.sb("qk", [QR, 2, D])
        values = m.sb("values", [S, D])
        x1 = m.sb("x1", [S, D])
        qt, kt = m.sb("qt", [P, KT, QR]), m.sb("kt", [P, KT, S])
        prob = m.sb("prob", [QR, HPT, KT, S])
        shift, total, inv = m.sb("shift", [QR, H]), m.sb("total", [QR, H]), m.sb("inv", [QR, H])
        pt = m.sb("pt", [S, H, QR])
        mixed = m.sb("mixed", [QR, D])
        ot_hi, ot_lo = m.sb("ot_hi", [P, KT, S], F32R), m.sb("ot_lo", [P, KT, S], F32R)
        y = m.sb("y", [S, D])
        scores = m.ps("scores", [P, HPT, 512])
        turned = [m.ps(f"turned{i}", [P, 512]) for i in range(2)]
        mix_bank, proj_bank = m.ps("mix_bank", [P, 512]), m.ps("proj_bank", [P, 512])

        ident_in, consts_in, w_in = m.sem("ident_in"), m.sem("consts_in"), m.sem("w_in")
        w_split, gate_ready, bias_ready = m.sem("w_split"), m.sem("gate_ready"), m.sem("bias_ready")
        sim_in, ends_step, ends_turned = m.sem("sim_in"), m.sem("ends_step"), m.sem("ends_turned")
        tables_ready, tables_stored = m.sem("tables_ready"), m.sem("tables_stored")
        qk_in, v_in, table_in, x1_in = m.sem("qk_in"), m.sem("v_in"), m.sem("table_in"), m.sem("x1_in")
        q_turned, k_turned, qt_done, kt_done = m.sem("q_turned"), m.sem("k_turned"), m.sem("qt_done"), m.sem("kt_done")
        scored, shift_done, exp_done, inv_done = m.sem("scored"), m.sem("shift_done"), m.sem("exp_done"), m.sem("inv_done")
        p_turned, pt_act, pt_dve = m.sem("p_turned"), m.sem("pt_act"), m.sem("pt_dve")
        mix_full, mixed_done = m.sem("mix_full"), m.sem("mixed_done")
        o_turned, ot_hi_done, ot_lo_done = m.sem("o_turned"), m.sem("ot_hi_done"), m.sem("ot_lo_done")
        biased, proj_full, y_ready, stored = m.sem("biased"), m.sem("proj_full"), m.sem("y_ready"), m.sem("stored")

        block = ctx.enter_context(nc.Block())

        @block.sync
        def _(sp):
            sp.dma_start(sim[:], sim_dram.rearrange("(b s) a -> b (s a)", s=S)).then_inc(sim_in, 16)
            sp.dma_start(ident[:], ident_dram).then_inc(ident_in, 16)

            def load_qk(b):
                src = qkv_dram[bass.ds(b * S, S), 0:2 * D].rearrange("s (a n) -> s a n", a=2)
                sp.dma_start(qk[0:S, :, :], src).then_inc(qk_in, 16)
                sp.dma_start(qk[S:QR, 0, :], qkv_dram[bass.ds(b * S, REG), 0:D]).then_inc(qk_in, 16)

            def load_table(b):
                for j in range(HPT):
                    sp.dma_start(table[j * HD:j * HD + 2, :], table_dram[bass.ds(b, 1)].rearrange("a r n -> (a r) n")
                                 ).then_inc(table_in, 16)

            def load_values(b):
                sp.dma_start(values[:], qkv_dram[bass.ds(b * S, S), 2 * D:3 * D]).then_inc(v_in, 16)

            def load_x1(b):
                sp.dma_start(x1[:], x1_dram[bass.ds(b * S, S), :]).then_inc(x1_in, 16)

            load_qk(0)
            load_values(0)
            sp.dma_start(gate[:], row_of(g_ffn, P)).then_inc(consts_in, 16)
            sp.dma_start(gate_bias[:], row_of(b_proj, S)).then_inc(consts_in, 16)
            sp.dma_start(fold[:], fold_dram).then_inc(consts_in, 16)
            sp.wait_ge(tables_ready, 1)
            sp.dma_start(table_dram, tables[:]).then_inc(tables_stored, 16)
            sp.dma_start(raw[:], w_proj.rearrange("(k p) n -> p k n", p=P)).then_inc(w_in, 16)
            sp.wait_ge(tables_stored, 16)
            load_table(0)
            load_x1(0)
            sp.wait_ge(k_turned, 1)
            load_qk(1)
            sp.wait_ge(scored, HPT)
            load_table(1)
            sp.wait_ge(k_turned, 2)
            load_qk(2)

            def store(b):
                sp.wait_ge(y_ready, b + 1)
                sp.dma_start(out[bass.ds(b * S, S), :], y[:]).then_inc(stored, 16)

            def body(b, follows=True, more_turns=True):
                if follows:
                    store(b - 1)
                    load_x1(b)
                sp.wait_ge(mix_full, b + 1)
                load_values(b + 1)
                if more_turns:
                    sp.wait_ge(scored, (b + 2) * HPT)
                    load_table(b + 2)

            def next_qk(b):
                sp.wait_ge(k_turned, b + 3)
                load_qk(b + 3)

            body(0, False)
            next_qk(0)
            with sp.Fori(1, B - 3) as b:
                body(b)
                next_qk(b)
            body(B - 3)
            body(B - 2, more_turns=False)
            store(B - 2)
            load_x1(B - 1)
            store(B - 1)
            sp.wait_ge(stored, 16 * B)

        @block.gpsimd
        def _(pool):
            pool.wait_ge(bias_ready, 1)
            with pool.Fori(0, B) as b:
                pool.wait_ge(x1_in, 16 * b + 16)
                pool.tensor_tensor(x1[:], x1[:], gate_bias[:], ALU.add).then_inc(biased, 1)

        @block.scalar
        def _(act):
            def queries(b):
                act.wait_ge(q_turned, b + 1)
                act.activation(qt[:], turned[1][:, 0:KT * QR].rearrange("p (k s) -> p k s", k=KT), ACT.Copy,
                               scale=-LOGIT_SCALE).then_inc(qt_done, 1)

            def exponentials(b, j, follows=True):
                if j == 0 and follows:
                    act.wait_ge(inv_done, b)
                act.wait_ge(shift_done, b * HPT + j + 1)
                for k in range(KT):
                    at = j * KT + k
                    last = act.activation(prob[:, j, k, :], scores[0:QR, j, k * S:(k + 1) * S], ACT.Exp,
                                          bias=shift[:, at:at + 1], scale=-1.0, accum_out=total[:, at:at + 1])
                last.then_inc(exp_done, 1)

            def turn_back(b):
                for n in (0, 2):
                    act.wait_ge(p_turned, b * HPT + n + 1)
                    act.activation(pt[:, n * HPT:(n + 1) * HPT, :],
                                   turned[0][0:S, 0:HPT * QR].rearrange("p (j q) -> p j q", j=HPT), ACT.Copy
                                   ).then_inc(pt_act, 1)

            def split_mix(b):
                act.wait_ge(o_turned, b + 1)
                act.activation(ot_hi[:], turned[0][:, 0:KT * S].rearrange("p (k s) -> p k s", k=KT), ACT.Copy
                               ).then_inc(ot_hi_done, 1)

            def body(b, more_scores=True, more_turns=True):
                turn_back(b)
                if more_scores:
                    for j in range(HPT - 1):
                        exponentials(b + 1, j)
                split_mix(b)
                if more_scores:
                    exponentials(b + 1, HPT - 1)
                if more_turns:
                    queries(b + 2)

            act.wait_ge(consts_in, 48)
            act.activation(gate[:], gate[:], ACT.Tanh).then_inc(gate_ready, 1)
            queries(0)
            act.wait_ge(w_in, 16)
            act.activation(w_hi[:], raw[:], ACT.Copy).then_inc(w_split, 1)
            for j in range(HPT):
                exponentials(0, j, False)
            queries(1)
            with act.Fori(0, B - 2) as b:
                body(b)
            body(B - 2, more_turns=False)
            body(B - 1, False, False)

        @block.vector
        def _(dve):
            step = Tally(ends_step)
            dve.wait_ge(sim_in, 16)
            step.done(dve.memset(ones[:], 1.0))
            step.done(dve.tensor_reduce(ends[:, 0:1], sim[:, REG:S], AX.X, ALU.min))
            step.done(dve.tensor_reduce(ends[:, 1:2], sim[:, REG:S], AX.X, ALU.max))
            dve.wait_ge(ends_turned, 1)
            step.done(dve.tensor_reduce(low_high[:, 0:1], mix_bank[0:1, 0:B], AX.X, ALU.min))
            step.done(dve.tensor_reduce(low_high[:, 1:2], mix_bank[0:1, B:2 * B], AX.X, ALU.max))
            dve.wait_ge(ends_turned, 2)
            step.done(dve.tensor_copy(ends_all[:], proj_bank[0:B, 0:2]))
            step.wait(dve)
            step.done(dve.tensor_tensor(spread[:, 0:1], ends_all[:, 1:2], ends_all[:, 0:1], ALU.subtract))
            step.wait(dve)
            step.done(dve.reciprocal(spread[:, 1:2], spread[:, 0:1]))
            step.wait(dve)
            step.done(dve.tensor_scalar(sim[:], sim[:], ends_all[:, 0:1], spread[:, 1:2], ALU.subtract, ALU.mult))
            step.wait(dve)
            step.done(dve.tensor_scalar(classes[:, 0, 0:S], sim[:], THRESHOLD, None, ALU.is_gt))
            step.done(dve.memset(classes[:, 0, S:QR], 0.0))
            step.wait(dve)
            step.done(dve.memset(classes[:, 0, 0:REG], 1.0))
            step.wait(dve)
            step.done(dve.tensor_scalar(classes[:, 1, :], classes[:, 0, :], -1.0, 1.0, ALU.mult, ALU.add))
            step.wait(dve)
            step.done(dve.tensor_copy(tables[:, :, S:TW], classes[:]))
            step.done(dve.tensor_scalar(tables[:, 0, 0:S], classes[:, 1, 0:S], MASKED, None, ALU.mult))
            step.done(dve.tensor_scalar(tables[:, 1, 0:S], classes[:, 0, 0:S], MASKED, None, ALU.mult))
            step.wait(dve)
            dve.memset(tables[:, :, 0:REG], 0.0).then_inc(tables_ready, 1)
            dve.wait_ge(gate_ready, 1)
            dve.tensor_scalar(gate_bias[:], gate_bias[:], gate[0:S, :], None, ALU.mult).then_inc(bias_ready, 1)

            def keys(b):
                dve.wait_ge(k_turned, b + 1)
                dve.tensor_copy(kt[:], mix_bank[:, 0:KT * S].rearrange("p (k s) -> p k s", k=KT)
                                ).then_inc(kt_done, 1)

            def shifts(b):
                for j in range(HPT):
                    dve.wait_ge(scored, b * HPT + j + 1)
                    dve.tensor_reduce(shift[:, j * KT:(j + 1) * KT],
                                      scores[0:QR, j, 0:KT * S].rearrange("p (k s) -> p k s", k=KT), AX.X, ALU.min
                                      ).then_inc(shift_done, 1)

            def invert(b):
                dve.wait_ge(exp_done, b * HPT + HPT)
                dve.reciprocal(inv[:], total[:]).then_inc(inv_done, 1)

            def turn_back(b):
                for n in (1, 3):
                    dve.wait_ge(p_turned, b * HPT + n + 1)
                    dve.tensor_copy(pt[:, n * HPT:(n + 1) * HPT, :],
                                    turned[1][0:S, 0:HPT * QR].rearrange("p (j q) -> p j q", j=HPT)
                                    ).then_inc(pt_dve, 1)

            def weigh(b):
                dve.wait_ge(mix_full, b + 1)
                dve.wait_ge(inv_done, b + 1)
                dve.tensor_tensor(mixed[:].rearrange("p (m a d) -> p m a d", a=HPT, d=HD),
                                  mix_bank[0:QR, :].rearrange("p (m a d) -> p m a d", a=HPT, d=HD),
                                  repeated(inv[:].rearrange("p (a m) -> p m a", m=KT).unsqueeze(3), 3, HD),
                                  ALU.mult).then_inc(mixed_done, 1)

            def split_mix(b):
                dve.wait_ge(ot_hi_done, b + 1)
                dve.tensor_tensor(ot_lo[:], turned[0][:, 0:KT * S].rearrange("p (k s) -> p k s", k=KT), ot_hi[:],
                                  ALU.subtract).then_inc(ot_lo_done, 1)

            def result(b, stored_before=True):
                dve.wait_ge(proj_full, b + 1)
                dve.wait_ge(biased, b + 1)
                if stored_before:
                    dve.wait_ge(stored, 16 * b)
                dve.scalar_tensor_tensor(y[:], proj_bank[0:S, :], gate[0:S, :], x1[:], ALU.mult, ALU.add
                                         ).then_inc(y_ready, 1)

            def body(b, before=2, more_scores=True, more_turns=True):
                turn_back(b)
                if before:
                    result(b - 1, before > 1)
                weigh(b)
                if more_scores:
                    shifts(b + 1)
                split_mix(b)
                if more_turns:
                    keys(b + 2)
                if more_scores:
                    invert(b + 1)

            keys(0)
            dve.wait_ge(w_split, 1)
            dve.tensor_tensor(w_lo[:], raw[:], w_hi[:], ALU.subtract).then_inc(w_split, 1)
            shifts(0)
            keys(1)
            invert(0)
            body(0, 0)
            body(1, 1)
            with dve.Fori(2, B - 2) as b:
                body(b)
            body(B - 2, more_turns=False)
            body(B - 1, more_scores=False, more_turns=False)
            result(B - 1)

        @block.tensor
        def _(pe):
            pe.wait_ge(ident_in, 16)
            pe.wait_ge(ends_step, 3)
            pe.transpose(mix_bank[0:1, 0:B], ends[:, 0:1], ident[0:B, 0:B])
            pe.transpose(mix_bank[0:1, B:2 * B], ends[:, 1:2], ident[0:B, 0:B]).then_inc(ends_turned, 1)
            pe.wait_ge(ends_step, 5)
            pe.matmul(proj_bank[0:B, 0:2], ones[:], low_high[:], start=True, stop=True).then_inc(ends_turned, 1)
            pe.wait_ge(ends_step, 6)
            pe.wait_ge(consts_in, 48)

            def turn_qk(b):
                pe.wait_ge(qk_in, 32 * b + 32)
                for k in range(KT):
                    last = pe.transpose(turned[1][:, k * QR:(k + 1) * QR], qk[:, 0, k * P:(k + 1) * P],
                                        ident[0:QR, 0:QR])
                last.then_inc(q_turned, 1)
                for k in range(KT):
                    last = pe.transpose(mix_bank[:, k * S:(k + 1) * S], qk[0:S, 1, k * P:(k + 1) * P],
                                        ident[0:S, 0:S])
                last.then_inc(k_turned, 1)

            def score(b):
                pe.wait_ge(table_in, HPT * (16 * b + 16))
                pe.wait_ge(qt_done, b + 1)
                pe.wait_ge(kt_done, b + 1)
                for j in range(HPT):
                    rows = slice(j * HD, j * HD + 2)
                    pe.matmul(scores[0:QR, j, 0:KT * S].rearrange("p (k s) -> p k s", k=KT), table[rows, S:TW],
                              repeated(table[rows, 0:S].unsqueeze(1), 1, KT), start=True, stop=False)
                    for k in range(KT):
                        part = slice(j * HD, (j + 1) * HD)
                        last = pe.matmul(scores[0:QR, j, k * S:(k + 1) * S], qt[part, k, :], kt[part, k, :],
                                         start=False, stop=(k == KT - 1))
                    last.then_inc(scored, 1)

            def turn_probs(b, n):
                pe.wait_ge(exp_done, b * HPT + n + 1)
                for k in range(KT):
                    last = pe.transpose(turned[n % 2][0:S, k * QR:(k + 1) * QR], prob[:, n, k, :],
                                        ident[0:QR, 0:QR])
                last.then_inc(p_turned, 1)

            def mix(b, n):
                for k in range(KT):
                    cols = slice((k * HPT + n) * HD, (k * HPT + n + 1) * HD)
                    last = pe.matmul(mix_bank[0:QR, cols], pt[:, n * KT + k, :], values[:, cols],
                                     start=True, stop=True)
                if n == HPT - 1:
                    last.then_inc(mix_full, 1)

            def fold_mix(b):
                pe.wait_ge(mixed_done, b + 1)
                for k in range(KT):
                    last = pe.matmul(turned[0][:, k * S:(k + 1) * S], mixed[:, k * P:(k + 1) * P], fold[:],
                                     start=True, stop=True)
                last.then_inc(o_turned, 1)

            def project(b, follows):
                pe.wait_ge(ot_lo_done, b + 1)
                if follows:
                    pe.wait_ge(y_ready, b)
                for k in range(KT):
                    last = three_products(pe, proj_bank[0:S, :], ot_hi[:, k, :], ot_lo[:, k, :], w_hi[:, k, :],
                                          w_lo[:, k, :], k == 0, k == KT - 1)
                last.then_inc(proj_full, 1)

            def body(b, follows=True, more_scores=True, more_turns=True):
                if follows:
                    pe.wait_ge(ot_lo_done, b)
                turn_probs(b, 0)
                if more_scores:
                    pe.wait_ge(qt_done, b + 2)
                    pe.wait_ge(kt_done, b + 2)
                turn_probs(b, 1)
                pe.wait_ge(pt_act, 2 * b + 1)
                turn_probs(b, 2)
                pe.wait_ge(v_in, 16 * b + 16)
                mix(b, 0)
                pe.wait_ge(pt_dve, 2 * b + 1)
                turn_probs(b, 3)
                mix(b, 1)
                pe.wait_ge(pt_act, 2 * b + 2)
                mix(b, 2)
                pe.wait_ge(pt_dve, 2 * b + 2)
                mix(b, 3)
                if more_scores:
                    score(b + 1)
                fold_mix(b)
                if more_turns:
                    turn_qk(b + 2)
                project(b, follows)

            turn_qk(0)
            score(0)
            turn_qk(1)
            pe.wait_ge(w_split, 2)
            body(0, False)
            with pe.Fori(1, B - 2) as b:
                body(b)
            body(B - 2, more_turns=False)
            body(B - 1, more_scores=False, more_turns=False)


def flamingo_block(nc, x, ctx_1024, g_xattn, g_ffn, wq, bq, wk, bk, wv, bv, wo, bo, g_info, w_qkv, w_proj, b_proj,
                   ident, neg_ident, fold, out):
    q_parts = nc.dram_tensor("q_parts", [2, D, ROWS], F32).ap()
    mix_parts = nc.dram_tensor("mix_parts", [2, D, ROWS], F32).ap()
    prob_sums = nc.dram_tensor("prob_sums", [H, ROWS], F32).ap()
    inverses = nc.dram_tensor("inverses", [H, ROWS], F32).ap()
    x1 = nc.dram_tensor("x1", [ROWS, D], F32).ap()
    qkv = nc.dram_tensor("qkv", [ROWS, 3 * D], F32).ap()
    sim = nc.dram_tensor("sim", [ROWS, 1], F32).ap()
    tables = nc.dram_tensor("tables", [B, 2, TW], BF16).ap()
    x_rows = x.rearrange("b s d -> (b s) d")
    stage_queries(nc, x, wq, bq, ident, q_parts)
    stage_cross(nc, ctx_1024, wk, bk, wv, ident, neg_ident, q_parts, mix_parts, prob_sums)
    stage_rows(nc, x_rows, mix_parts, prob_sums, inverses, bv, g_xattn, wo, bo, g_info, w_qkv, ident, x1, qkv, sim)
    stage_self(nc, qkv, sim, x1, tables, g_ffn, w_proj, b_proj, ident, fold, out.rearrange("b s d -> (b s) d"))


INPUTS = ["x", "ctx_1024", "g_xattn", "g_ffn", "L0_xattn_wq", "L0_xattn_bq", "L0_xattn_wk", "L0_xattn_bk",
          "L0_xattn_wv", "L0_xattn_bv", "L0_xattn_wo", "L0_xattn_bo", "L0_ffn_g_info", "L0_ffn_W_qkv",
          "L0_ffn_W_proj", "L0_ffn_b_proj"]


def kernel(**inputs):
    import concourse.bacc as bacc
    from concourse.bass_utils import run_bass_kernel_spmd

    fold = np.zeros((QR, S), np.float32)
    for q in range(S):
        fold[q, q] = 0.5 if q < REG else 1.0
    for q in range(REG):
        fold[S + q, q] = 0.5
    arrays = {name: np.ascontiguousarray(inputs[name]) for name in INPUTS}
    arrays |= {"ident": np.eye(P, dtype=np.float32), "neg_ident": -np.eye(HPT, dtype=np.float32),
               "fold": fold}
    nc = bacc.Bacc("TRN2", target_bir_lowering=False, num_devices=1)
    args = [nc.dram_tensor(f"in_{name}", a.shape, mybir.dt.from_np(a.dtype), kind="ExternalInput").ap()
            for name, a in arrays.items()]
    out = nc.dram_tensor("out", (B, S, D), F32, kind="ExternalOutput").ap()
    flamingo_block(nc, *args, out)
    result = run_bass_kernel_spmd(nc, [{f"in_{name}": a for name, a in arrays.items()}], core_ids=[0])
    return result.results[0]["out"]
```

```python
from contextlib import ExitStack

import numpy as np

import concourse.bass as bass
from concourse import mybir

F32 = mybir.dt.float32
F32R = mybir.dt.float32r
ALU = mybir.AluOpType
ACT = mybir.ActivationFunctionType
AX = mybir.AxisListType

P = 128
B, S, D = 32, 100, 512
C = 722
H, HD = 16, 32
KT = D // P
HPT = P // HD
REG = 5
ROWS = B * S
EPS = 1e-5
LOGIT_SCALE = HD ** -0.5
THRESHOLD = 0.9
MASKED = 2.0 ** 100


class Tally:

    def __init__(self, sem, base=0):
        self.sem, self.base, self.n = sem, base, 0

    def done(self, instruction):
        instruction.then_inc(self.sem, 1)
        self.n += 1

    def wait(self, engine, back=0):
        engine.wait_ge(self.sem, self.base + (self.n - back))


class Memory:
    def __init__(self, nc, ctx, prefix):
        self.nc, self.ctx, self.prefix = nc, ctx, prefix

    def sb(self, name, shape, dt=F32):
        return self.ctx.enter_context(self.nc.sbuf_tensor(self.prefix + name, shape, dt))

    def ps(self, name, shape):
        return self.ctx.enter_context(self.nc.psum_tensor(self.prefix + name, shape, F32))

    def sem(self, name):
        return self.ctx.enter_context(self.nc.semaphore(self.prefix + name))


def f32(ap):
    return ap.bitcast(F32)


def repeated(ap, dim, times):
    shape = list(ap.shape)
    shape[dim] = times
    return ap.broadcast_to(shape)


def row_of(vector, partitions):
    return repeated(vector.rearrange("(a n) -> a n", a=1), 0, partitions)


def three_products(pe, out, left_hi, left_lo, right_hi, right_lo, first, last):
    pe.matmul(out, left_hi, right_hi, start=first, stop=False)
    pe.matmul(out, left_hi, right_lo, start=False, stop=False)
    return pe.matmul(out, left_lo, right_hi, start=False, stop=last)


class Shared:

    def __init__(self, nc, ctx):
        m = Memory(nc, ctx, "e_")
        self.ident = m.sb("ident", [P, P])
        self.rows = m.sb("rows", [P, CT, D])
        self.raw_w = [m.sb(f"raw_w{n}", [P, KT, D]) for n in range(2)]
        self.ident_in, self.rows_in = m.sem("ident_in"), m.sem("rows_in")
        self.w_in = [m.sem(f"w_in{n}") for n in range(2)]

    def load_rows(self, engine, context, b):
        whole = (CT - 1) * P
        engine.dma_start(self.rows[:, 0:CT - 1, :], context[b, 0:whole, :].rearrange("(t p) d -> p t d", p=P)
                         ).then_inc(self.rows_in, 16)
        engine.dma_start(self.rows[0:C_LAST, CT - 1, :], context[b, whole:C, :]).then_inc(self.rows_in, 16)

    def load_weights(self, engine, weights):
        for n, w in enumerate(weights):
            engine.dma_start(self.raw_w[n][:], w.rearrange("(k p) n -> p k n", p=P)).then_inc(self.w_in[n], 16)


GB = 4
GROUPS = B // GB
GS = GB * S


def stage_queries(nc, shared, x, wq, bq, ident_dram, q_parts, context, wk, wv):
    with ExitStack() as ctx:
        m = Memory(nc, ctx, "q_")
        ident = shared.ident
        w_raw = m.sb("w_raw", [P, KT, D])
        w_hi, w_lo = m.sb("w_hi", [P, KT, D], F32R), m.sb("w_lo", [P, KT, D], F32R)
        bias = m.sb("bias", [P, KT])
        eps = m.sb("eps", [P, 1])
        rows = m.sb("rows", [S, GB, D])
        stats, moments = m.sb("stats", [S, GB, 6]), m.sb("moments", [S, GB, 2])
        std, rstd = m.sb("std", [S, GB]), m.sb("rstd", [S, GB])
        normed = m.sb("normed", [S, GB, D])
        xt_hi = [m.sb(f"xt_hi{i}", [P, KT, GS], F32R) for i in range(2)]
        xt_lo = [m.sb(f"xt_lo{i}", [P, KT, GS], F32R) for i in range(2)]
        q_hi = [m.sb(f"q_hi{i}", [P, KT, GS], F32R) for i in range(2)]
        q_lo = [m.sb(f"q_lo{i}", [P, KT, GS], F32R) for i in range(2)]
        bank = [m.ps(f"bank{i}", [P, 512]) for i in range(8)]
        turned, product = bank[:4], bank[4:]

        loaded, w_split, rows_in = m.sem("loaded"), m.sem("w_split"), m.sem("rows_in")
        eps_set, stats_seen = m.sem("eps_set"), m.sem("stats_seen")
        dve_step, act_std = m.sem("dve_step"), m.sem("act_std")
        normed_ready, turned_ready = m.sem("normed_ready"), m.sem("turned_ready")
        xt_hi_ready, xt_lo_ready = m.sem("xt_hi_ready"), m.sem("xt_lo_ready")
        product_ready = m.sem("product_ready")
        q_hi_ready, q_lo_ready = m.sem("q_hi_ready"), m.sem("q_lo_ready")
        stored = [m.sem(f"stored{i}") for i in range(2)]

        block = ctx.enter_context(nc.Block())
        x_groups = x.rearrange("(g r) s d -> g s r d", r=GB)

        def all_groups(engine, body):
            body(0, 0)
            with engine.Fori(0, (GROUPS - 4) // 2) as u:
                body(u * 2 + 1, 1)
                body(u * 2 + 2, 0)
            for g in range(GROUPS - 3, GROUPS):
                body(g, g % 2, g + 1 < GROUPS, g + 2 < GROUPS)

        @block.sync
        def _(sp):
            sp.dma_start(rows[:], x_groups[0]).then_inc(rows_in, 16)
            sp.dma_start(w_raw[:], wq.rearrange("(k p) n -> p k n", p=P)).then_inc(loaded, 16)
            sp.dma_start(bias[:], bq.rearrange("(k p) -> p k", p=P), allow_slow_non_contiguous=True).then_inc(loaded, 16)
            sp.dma_start(ident[:], ident_dram).then_inc(shared.ident_in, 16)

            def load(g):
                sp.wait_ge(normed_ready, g)
                sp.dma_start(rows[:], x_groups[g]).then_inc(rows_in, 16)

            def store(g, odd):
                sp.wait_ge(q_hi_ready, g * KT + KT)
                sp.wait_ge(q_lo_ready, g * KT + KT)
                for part, tile in enumerate((q_hi[odd], q_lo[odd])):
                    dst = q_parts[part].rearrange("(k p) n -> p k n", p=P)
                    sp.dma_start(dst[:, :, bass.ds(g * GS, GS)], f32(tile[:])).then_inc(stored[odd], 16)

            def body(g, odd, *at_the_end):
                if not at_the_end:
                    load(g + 3)
                store(g, odd)

            load(1)
            shared.load_rows(sp, context, 0)
            load(2)
            shared.load_weights(sp, (wk, wv))
            all_groups(sp, body)
            for odd in range(2):
                sp.wait_ge(stored[odd], 16 * GROUPS)

        @block.vector
        def _(dve):
            dve.memset(eps[:], EPS).then_inc(eps_set, 1)
            STEPS = GB + GB + 1

            def normalise(g, follows=True):
                step = Tally(dve_step, g * STEPS)
                dve.wait_ge(rows_in, g * 16 + 16)
                for r in range(GB):
                    step.done(dve.bn_stats(stats[:, r, :], rows[:, r, :]))
                step.wait(dve)
                dve.sem_inc(stats_seen, 1)
                for r in range(GB):
                    step.done(dve.bn_aggr(moments[:, r, :], stats[:, r, :]))
                dve.wait_ge(act_std, g + 1)
                step.done(dve.reciprocal(rstd[:], std[:]))
                step.wait(dve)
                if follows:
                    dve.wait_ge(turned_ready, g * KT)
                for r in range(GB):
                    last = dve.tensor_scalar(normed[:, r, :], rows[:, r, :], moments[:, r, 0:1],
                                             rstd[:, r:r + 1], ALU.subtract, ALU.mult)
                last.then_inc(normed_ready, 1)

            def split_rows(g, odd):
                for k in range(KT):
                    dve.wait_ge(xt_hi_ready, g * KT + k + 1)
                    dve.tensor_tensor(xt_lo[odd][:, k, :], turned[k][:, 0:GS], xt_hi[odd][:, k, :],
                                      ALU.subtract).then_inc(xt_lo_ready, 1)

            def split_queries(g, odd):
                for k in range(KT):
                    dve.wait_ge(q_hi_ready, g * KT + k + 1)
                    dve.scalar_tensor_tensor(q_lo[odd][:, k, :], product[k][:, 0:GS], bias[:, k:k + 1],
                                             q_hi[odd][:, k, :], ALU.add, ALU.subtract).then_inc(q_lo_ready, 1)

            def body(g, odd, more_turns=True, more_rows=True):
                if more_turns:
                    split_rows(g + 1, 1 - odd)
                if more_rows:
                    normalise(g + 2)
                split_queries(g, odd)

            normalise(0, False)
            dve.wait_ge(loaded, 32)
            dve.wait_ge(w_split, 1)
            dve.tensor_tensor(w_lo[:], w_raw[:], w_hi[:], ALU.subtract).then_inc(w_split, 1)
            split_rows(0, 0)
            normalise(1)
            all_groups(dve, body)

        @block.scalar
        def _(act):
            act.wait_ge(eps_set, 1)

            def roots(g):
                act.wait_ge(dve_step, g * (2 * GB + 1) + 2 * GB)
                act.activation(std[:], moments[:, :, 1], ACT.Sqrt, bias=eps[0:S, :]).then_inc(act_std, 1)

            def split_rows(g, odd):
                for k in range(KT):
                    act.wait_ge(turned_ready, g * KT + k + 1)
                    act.activation(xt_hi[odd][:, k, :], turned[k][:, 0:GS], ACT.Copy).then_inc(xt_hi_ready, 1)

            def split_queries(g, odd):
                for k in range(KT):
                    act.wait_ge(product_ready, g * KT + k + 1)
                    if k == 0 and not (isinstance(g, int) and g < 2):
                        act.wait_ge(stored[odd], (g - odd) * 16)
                    act.activation(q_hi[odd][:, k, :], product[k][:, 0:GS], ACT.Identity,
                                   bias=bias[:, k:k + 1]).then_inc(q_hi_ready, 1)

            def body(g, odd, more_turns=True, more_rows=True):
                if more_turns:
                    split_rows(g + 1, 1 - odd)
                if more_rows:
                    roots(g + 2)
                split_queries(g, odd)

            roots(0)
            act.wait_ge(loaded, 32)
            act.activation(w_hi[:], w_raw[:], ACT.Copy).then_inc(w_split, 1)
            split_rows(0, 0)
            roots(1)
            all_groups(act, body)

        @block.tensor
        def _(pe):
            pe.wait_ge(shared.ident_in, 16)

            def turn(g):
                pe.wait_ge(normed_ready, g + 1)
                for k in range(KT):
                    for r in range(GB):
                        last = pe.transpose(turned[k][:, r * S:(r + 1) * S],
                                            normed[:, r, k * P:(k + 1) * P], ident[0:S, 0:S])
                    last.then_inc(turned_ready, 1)

            def project(g, odd, follows):
                pe.wait_ge(xt_lo_ready, g * KT + KT)
                for n in range(KT):
                    if follows:
                        pe.wait_ge(q_lo_ready, (g - 1) * KT + n + 1)
                    for k in range(KT):
                        cols = slice(n * P, (n + 1) * P)
                        last = three_products(pe, product[n][:, 0:GS], w_hi[:, k, cols], w_lo[:, k, cols],
                                              xt_hi[odd][:, k, :], xt_lo[odd][:, k, :], k == 0, k == KT - 1)
                    last.then_inc(product_ready, 1)

            def body(g, odd, more_turns=True, more_rows=True):
                if more_turns:
                    pe.wait_ge(xt_lo_ready, g * KT + KT)
                    turn(g + 1)
                project(g, odd, not (isinstance(g, int) and g == 0))

            turn(0)
            pe.wait_ge(w_split, 2)
            all_groups(pe, body)


CT = -(-C // P)
CPAD = CT * P
C_LAST = C - (CT - 1) * P
HALF = (C // 2 + 1) // 2 * 2
HALVES = (slice(0, HALF), slice(HALF, C))
MAX_HALVES = (slice(0, HALF), slice(C - HALF, C))
STACK = 3 * HD
SROWS = STACK + HPT
VW = 2 * HD + 2
HG = 2
PR = 4

V_PARTS, K_PARTS = 4, 2
V_HELD = 4
PARTS = {"values": V_PARTS, "keys": K_PARTS}


def front_plan():
    plan, peaks = [], 0
    parts = [(t, p) for t in range(CT) for p in range(V_PARTS)]
    spread = len(parts) - V_HELD
    for n, (t, p) in enumerate(parts[:spread]):
        plan.append(("values", t, p))
        while peaks < H and peaks * spread < n * H:
            plan.append(("peak", peaks, 0))
            peaks += 1
            if peaks % HPT == 2 and peaks > HPT:
                plan.append(("shift", peaks // HPT - 1, 0))
    plan += [("peak", n, 0) for n in range(peaks, H)]
    held = [("values", t, p) for t, p in parts[spread:]]
    return plan + held[:2] + [("scores", 0, 0)] + held[2:]


WORK = [("turn", t) for t in range(CT)] + [("keys", n) for n in range(2 * KT)]
FIRST_WORK = [(kind, i, p) for kind, i in WORK for p in range(PARTS.get(kind, 1))]
WORK_AFTER = (1, 1, 2, 1, 1, 1, 1, 2, 1, 1, 2, 1, 1, 2, 1, 1, 1, 1)


def batch_plan(with_next):
    plan = front_plan()
    for h in range(H + 2):
        if 0 < h < H:
            plan.append(("scores", h, 0))
        if with_next:
            at = sum(WORK_AFTER[:h])
            plan += FIRST_WORK[at:at + WORK_AFTER[h]]
        if h == 1:
            plan.append(("shift", KT - 1, 0))
        if h >= 2:
            plan.append(("mix", h - 2, 0))
    return plan


A_USES = CT + CT + 2 * KT
A_FIRST = CT + 2 * KT


def work_use(kind, index, b):
    if kind == "values":
        return index, A_FIRST + b * A_USES + index
    at = WORK.index((kind, index))
    return (at, at) if b is None else (CT + at, A_FIRST + b * A_USES + CT + at)


def stage_cross(nc, shared, context, bk, neg_ident_dram, q_parts, mix_parts, prob_sums, next_weights):
    with ExitStack() as ctx:
        m = Memory(nc, ctx, "c_")
        ident, rows, raw_w = shared.ident, shared.rows, shared.raw_w
        rows_in, w_in = shared.rows_in, shared.w_in
        neg_ident = m.sb("neg_ident", [HPT, HPT])
        wk_hi, wk_lo = m.sb("wk_hi", [P, KT, D], F32R), m.sb("wk_lo", [P, KT, D], F32R)
        wv_hi, wv_lo = m.sb("wv_hi", [P, KT, D], F32R), m.sb("wv_lo", [P, KT, D], F32R)
        key_bias = m.sb("key_bias", [P, KT])
        ct_hi, ct_lo = m.sb("ct_hi", [P, KT, C], F32R), m.sb("ct_lo", [P, KT, C], F32R)
        k_hi = [m.sb(f"k_hi{i}", [P, C], F32R) for i in range(2)]
        k_lo = [m.sb(f"k_lo{i}", [P, C], F32R) for i in range(2)]
        k_stack = m.sb("k_stack", [SROWS, H, CPAD], F32R)
        q_stack = m.sb("q_stack", [SROWS, H, S], F32R)
        v = m.sb("v", [P, CT, H, VW], F32R)
        peak = m.sb("peak", [S, H])
        prob = [m.sb(f"prob{i}", [P, CT, S]) for i in range(2)]
        parted = [m.sb(f"parted{i}", [P, CT, 2, S], F32R) for i in range(PR)]
        mixed = m.sb("mixed", [VW, H, S])

        work = [m.ps(f"work{i}", [P, 512]) for i in range(2)]
        pair = [m.ps(f"pair{i}", [P, 2, 512]) for i in range(2)]
        mix = [m.ps(f"mix{i}", [P, 512]) for i in range(2)]
        shift_bank = mix[0][:, HG * 2 * S:HG * 2 * S + S]

        consts_in, w_hi_done, w_lo_done = m.sem("consts_in"), m.sem("w_hi_done"), m.sem("w_lo_done")
        cleared = m.sem("cleared")
        q_in = [m.sem(f"q_in{half}") for half in range(2)]
        k_in = [m.sem(f"k_in{n}") for n in range(KT)]
        work_full, work_hi, work_lo = m.sem("work_full"), m.sem("work_hi"), m.sem("work_lo")
        peak_full, peak_done = m.sem("peak_full"), m.sem("peak_done")
        shift_full, shift_done = m.sem("shift_full"), m.sem("shift_done")
        scores_full, exp_hi_done, exp_done = m.sem("scores_full"), m.sem("exp_hi_done"), m.sem("exp_done")
        p_lo_done, mix_done = m.sem("p_lo_done"), m.sem("mix_done")
        mixed_done, stored = m.sem("mixed_done"), m.sem("stored")

        block = ctx.enter_context(nc.Block())

        def c_rows(t):
            return P if t < CT - 1 else C_LAST

        def stack_queries(engine, b, half):
            heads = slice(half * H // 2, (half + 1) * H // 2)
            for n, part in enumerate((0, 0, 1)):
                src = q_parts[part].rearrange("(h d) n -> d h n", d=HD)[:, heads, bass.ds(b * S, S)]
                engine.dma_start(f32(q_stack[n * HD:(n + 1) * HD, heads, :]), src).then_inc(q_in[half], 16)

        @block.sync
        def _(sp):
            sp.dma_start(neg_ident[:], neg_ident_dram).then_inc(consts_in, 16)
            sp.dma_start(key_bias[:], bk.rearrange("(k p) -> p k", p=P), allow_slow_non_contiguous=True).then_inc(consts_in, 16)

            def stack_keys(n):
                for j in range(HPT):
                    for place, part in enumerate((k_hi, k_lo, k_hi)):
                        sp.dma_start(f32(k_stack[place * HD:(place + 1) * HD, n * HPT + j, 0:C]),
                                     f32(part[n % 2][j * HD:(j + 1) * HD, :])).then_inc(k_in[n], 16)

            def store_mix(b):
                sp.wait_ge(mixed_done, (b + 1) * (H // HG))
                for n in range(2):
                    dst = mix_parts[n].rearrange("(h d) n -> d h n", d=HD)[:, :, bass.ds(b * S, S)]
                    sp.dma_start(dst, mixed[n * HD:(n + 1) * HD, :, :]).then_inc(stored, 16)
                sp.dma_start(prob_sums.rearrange("(a h) n -> a h n", a=1)[:, :, bass.ds(b * S, S)],
                             mixed[2 * HD:2 * HD + 1, :, :]).then_inc(stored, 16)

            sp.wait_ge(cleared, 2)
            for half in range(2):
                stack_queries(sp, 0, half)
            for n in range(KT):
                sp.wait_ge(work_lo, CT + 2 * n + 2)
                stack_keys(n)

            with sp.Fori(0, B - 1) as b:
                sp.wait_ge(work_full, b * A_USES + WORK.index(("turn", CT - 1)) + 1)
                shared.load_rows(sp, context, b + 1)
                for n in range(KT):
                    use = work_use("keys", 2 * n + 1, b)[1]
                    sp.wait_ge(work_lo, use + 1)
                    stack_keys(n)
                store_mix(b)
            shared.load_weights(sp, next_weights)
            store_mix(B - 1)
            sp.wait_ge(stored, 48 * B)

        @block.gpsimd
        def _(pool):
            fills = [(k_stack[:, :, C:CPAD], 0.0), (k_stack[STACK:SROWS, :, 0:C], 1.0),
                     (v[:, CT - 1, :, :], 0.0), (v[0:C_LAST, CT - 1, :, 2 * HD:2 * HD + 1], 1.0),
                     (v[:, 0:CT - 1, :, 2 * HD + 1:VW], 0.0), (v[:, 0:CT - 1, :, 2 * HD:2 * HD + 1], 1.0)]
            for n, (part, value) in enumerate(fills):
                if n:
                    pool.wait_ge(cleared, n)
                pool.memset(f32(part), value).then_inc(cleared, 1)

        @block.scalar
        def _(act):
            def split_weights(n, hi):
                act.wait_ge(w_in[n], 16)
                act.activation(hi[:], raw_w[n][:], ACT.Copy).then_inc(w_hi_done, 1)

            split_weights(0, wk_hi)
            act.wait_ge(consts_in, 32)

            def emit(kind, i, part, b, with_next=False):
                if part < PARTS.get(kind, 1) - 1:
                    return
                if kind in ("values", "turn", "keys"):
                    local, use = work_use(kind, i, b)
                    bank = work[local % 2]
                    act.wait_ge(work_full, use + 1)
                    if kind == "values":
                        r = c_rows(i)
                        ins = act.activation(v[0:r, i, :, 0:HD],
                                             bank[0:r, :].rearrange("p (h d) -> p h d", d=HD), ACT.Copy)
                    elif kind == "turn":
                        r = c_rows(i)
                        ins = act.activation(ct_hi[:, :, i * P:i * P + r],
                                             bank[:, 0:KT * r].rearrange("p (k c) -> p k c", k=KT), ACT.Copy)
                    else:
                        n, half = divmod(i, 2)
                        if half == 0 and not (b is None and n < 2):
                            before = (n + 2) % KT
                            times = 0 if b is None else b + 1
                            act.wait_ge(k_in[before], (times + (1 if n >= 2 else 0)) * 16 * 3 * HPT)
                        cols = HALVES[half]
                        ins = act.activation(k_hi[n % 2][:, cols], bank[:, 0:cols.stop - cols.start],
                                             ACT.Identity, bias=key_bias[:, n:n + 1])
                    ins.then_inc(work_hi, 1)
                elif kind == "scores":
                    act.wait_ge(scores_full, b * H + i + 1)
                    logits = pair[i % 2][:, :, 0:CT // 2 * S].rearrange("p a (t s) -> p a t s", s=S)
                    if i >= PR:
                        act.wait_ge(mix_done, b * H + i - PR + 1)
                    act.activation(parted[i % PR][:, :, 0, :].rearrange("p (a t) s -> p a t s", a=2), logits,
                                   ACT.Exp).then_inc(exp_hi_done, 1)
                    if i >= 2:
                        act.wait_ge(p_lo_done, b * H + i - 1)
                    act.activation(prob[i % 2][:, :, :].rearrange("p (a t) s -> p a t s", a=2), logits,
                                   ACT.Exp).then_inc(exp_done, 1)
                    if with_next and i % (H // 2) == H // 2 - 1:
                        stack_queries(act, b + 1, i // (H // 2))

            for kind, i, part in FIRST_WORK:
                if (kind, i, part) == ("keys", 0, 0):
                    split_weights(1, wv_hi)
                emit(kind, i, part, None)
            act.wait_ge(cleared, 6)
            with act.Fori(0, B - 1) as b:
                for kind, i, part in batch_plan(True):
                    emit(kind, i, part, b, True)
            for kind, i, part in batch_plan(False):
                emit(kind, i, part, B - 1)

        @block.vector
        def _(dve):
            def split_weights(n, hi, lo):
                dve.wait_ge(w_hi_done, n + 1)
                dve.tensor_tensor(lo[:], raw_w[n][:], hi[:], ALU.subtract).then_inc(w_lo_done, 1)

            split_weights(0, wk_hi, wk_lo)
            dve.wait_ge(consts_in, 32)

            def emit(kind, i, part, b, stored_before=True):
                if part < PARTS.get(kind, 1) - 1:
                    return
                if kind in ("values", "turn", "keys"):
                    local, use = work_use(kind, i, b)
                    bank = work[local % 2]
                    dve.wait_ge(work_hi, use + 1)
                    if kind == "values":
                        r = c_rows(i)
                        ins = dve.tensor_tensor(v[0:r, i, :, HD:2 * HD],
                                                bank[0:r, :].rearrange("p (h d) -> p h d", d=HD),
                                                v[0:r, i, :, 0:HD], ALU.subtract)
                    elif kind == "turn":
                        r = c_rows(i)
                        cols = slice(i * P, i * P + r)
                        ins = dve.tensor_tensor(ct_lo[:, :, cols],
                                                bank[:, 0:KT * r].rearrange("p (k c) -> p k c", k=KT),
                                                ct_hi[:, :, cols], ALU.subtract)
                    else:
                        n, half = divmod(i, 2)
                        cols = HALVES[half]
                        ins = dve.scalar_tensor_tensor(k_lo[n % 2][:, cols], bank[:, 0:cols.stop - cols.start],
                                                       key_bias[:, n:n + 1], k_hi[n % 2][:, cols],
                                                       ALU.add, ALU.subtract)
                    ins.then_inc(work_lo, 1)
                elif kind == "peak":
                    dve.wait_ge(peak_full, b * H + i + 1)
                    dve.tensor_reduce(peak[:, i:i + 1], pair[i % 2][0:S, :, 0:HALF], AX.XY, ALU.max
                                      ).then_inc(peak_done, 1)
                elif kind == "shift":
                    dve.wait_ge(shift_full, b * KT + i + 1)
                    dve.tensor_tensor(q_stack[STACK:SROWS, i * HPT:(i + 1) * HPT, :],
                                      repeated(shift_bank[0:HPT, :].unsqueeze(1), 1, HPT),
                                      repeated(neg_ident[:].unsqueeze(2), 2, S), ALU.mult
                                      ).then_inc(shift_done, 1)
                elif kind == "scores":
                    dve.wait_ge(exp_done, b * H + i + 1)
                    if i >= PR:
                        dve.wait_ge(mix_done, b * H + i - PR + 1)
                    p = parted[i % PR]
                    dve.tensor_tensor(p[:, :, 1, :], prob[i % 2][:], p[:, :, 0, :], ALU.subtract
                                      ).then_inc(p_lo_done, 1)
                elif kind == "mix" and i % HG == HG - 1:
                    g = i // HG
                    dve.wait_ge(mix_done, b * H + i + 1)
                    if g == 0 and stored_before:
                        dve.wait_ge(stored, b * 48)
                    dve.tensor_reduce(mixed[:, g * HG:(g + 1) * HG, :],
                                      mix[g % 2][0:VW, 0:HG * 2 * S].rearrange("p (h a s) -> p h s a", a=2, s=S),
                                      AX.X, ALU.add).then_inc(mixed_done, 1)

            for kind, i, part in FIRST_WORK:
                if (kind, i, part) == ("keys", 0, 0):
                    split_weights(1, wv_hi, wv_lo)
                emit(kind, i, part, None)
            dve.wait_ge(cleared, 6)
            for kind, i, part in batch_plan(True):
                emit(kind, i, part, 0, False)
            with dve.Fori(1, B - 1) as b:
                for kind, i, part in batch_plan(True):
                    emit(kind, i, part, b)
            for kind, i, part in batch_plan(False):
                emit(kind, i, part, B - 1)

        @block.tensor
        def _(pe):
            pe.wait_ge(consts_in, 32)

            def emit(kind, i, part, b):
                if kind in ("values", "turn", "keys"):
                    local, use = work_use(kind, i, b)
                    bank = work[local % 2]
                    if part == 0 and not (b is None and local < 2):
                        pe.wait_ge(work_lo, use - 1)
                        pe.wait_ge(work_hi, use - 1)
                    if kind == "turn":
                        if i == 0:
                            pe.wait_ge(rows_in, 32 if b is None else b * 32 + 64)
                        r = c_rows(i)
                        for k in range(KT):
                            last = pe.transpose(bank[:, k * r:(k + 1) * r], rows[0:r, i, k * P:(k + 1) * P],
                                                ident[0:r, 0:r])
                    elif kind == "keys":
                        n, half = divmod(i, 2)
                        cols = HALVES[half]
                        if n == 0 and part == 0:
                            tile_end = -(-cols.stop // P)
                            pe.wait_ge(work_lo, work_use("turn", tile_end - 1, b)[1] + 1)
                        for k in range(part * KT // K_PARTS, (part + 1) * KT // K_PARTS):
                            wcols = slice(n * P, (n + 1) * P)
                            last = three_products(pe, bank[:, 0:cols.stop - cols.start], wk_hi[:, k, wcols],
                                                  wk_lo[:, k, wcols], ct_hi[:, k, cols], ct_lo[:, k, cols],
                                                  k == 0, k == KT - 1)
                    else:
                        r = c_rows(i)
                        cols = slice(i * P, i * P + r)
                        for k in range(part * KT // V_PARTS, (part + 1) * KT // V_PARTS):
                            last = three_products(pe, bank[0:r, :], ct_hi[:, k, cols], ct_lo[:, k, cols],
                                                  wv_hi[:, k, :], wv_lo[:, k, :], k == 0, k == KT - 1)
                    if part == PARTS.get(kind, 1) - 1:
                        last.then_inc(work_full, 1)
                elif kind == "peak":
                    if i % (H // 2) == 0:
                        pe.wait_ge(q_in[i // (H // 2)], b * 48 + 48)
                    if i % HPT == 0:
                        pe.wait_ge(k_in[i // HPT], (b + 1) * 16 * 3 * HPT)
                    if i >= 2:
                        pe.wait_ge(peak_done, b * H + i - 1)
                    for bank, cols in enumerate(MAX_HALVES):
                        last = pe.matmul(pair[i % 2][0:S, bank, 0:HALF], q_stack[0:STACK, i, :],
                                         k_stack[0:STACK, i, cols], start=True, stop=True)
                    last.then_inc(peak_full, 1)
                elif kind == "shift":
                    pe.wait_ge(peak_done, b * H + (i + 1) * HPT)
                    if i >= 1:
                        pe.wait_ge(shift_done, b * KT + i)
                    pe.transpose(shift_bank[0:HPT, :], peak[:, i * HPT:(i + 1) * HPT], ident[0:S, 0:S]
                                 ).then_inc(shift_full, 1)
                elif kind == "scores":
                    if i % HPT == 0:
                        pe.wait_ge(shift_done, b * KT + i // HPT + 1)
                    if i < 2:
                        pe.wait_ge(peak_done, b * H + H - 1 + i)
                    else:
                        pe.wait_ge(exp_done, b * H + i - 1)
                    for t in range(CT):
                        col = t % (CT // 2) * S
                        last = pe.matmul(pair[i % 2][:, t // (CT // 2), col:col + S],
                                         k_stack[:, i, t * P:(t + 1) * P], q_stack[:, i, :],
                                         start=True, stop=True)
                    last.then_inc(scores_full, 1)
                elif kind == "mix":
                    g, at = divmod(i, HG)
                    if i == 0:
                        pe.wait_ge(shift_done, b * KT + KT)
                        pe.wait_ge(work_lo, work_use("values", CT - 1, b)[1] + 1)
                    if at == 0 and g >= 2:
                        pe.wait_ge(mixed_done, b * (H // HG) + g - 1)
                    pe.wait_ge(p_lo_done, b * H + i + 1)
                    for t in range(CT):
                        last = pe.matmul(mix[g % 2][0:VW, at * 2 * S:(at + 1) * 2 * S], v[:, t, i, :],
                                         parted[i % PR][:, t, :, :].rearrange("p a s -> p (a s)"),
                                         start=(t == 0), stop=(t == CT - 1))
                    last.then_inc(mix_done, 1)

            for kind, i, part in FIRST_WORK:
                if (kind, i, part) == ("keys", 0, 0):
                    pe.wait_ge(w_lo_done, 1)
                emit(kind, i, part, None)
            pe.wait_ge(w_lo_done, 2)
            pe.wait_ge(cleared, 6)
            with pe.Fori(0, B - 1) as b:
                for kind, i, part in batch_plan(True):
                    emit(kind, i, part, b)
            for kind, i, part in batch_plan(False):
                emit(kind, i, part, B - 1)


TILES = ROWS // P
A_LOADS = 2 + HPT
A_STEPS = 2
X1_STEPS = 4
SIM_STEPS = 6


def stage_rows(nc, shared, x, mix_parts, prob_sums, inverses, bv, g_xattn, bo, g_info, w_qkv, x1_dram, qk_parts, values_dram,
               sim_dram):
    with ExitStack() as ctx:
        m = Memory(nc, ctx, "r_")
        ident = shared.ident
        raw = shared.raw_w + [m.sb(f"raw{i}", [P, KT, D]) for i in range(2, 4)]
        w_hi = [m.sb(f"w_hi{i}", [P, KT, D], F32R) for i in range(4)]
        w_lo = [m.sb(f"w_lo{i}", [P, KT, D], F32R) for i in range(4)]
        gate, gate_bias = m.sb("gate", [P, 1]), m.sb("gate_bias", [P, D])
        guide, guide_sq = m.sb("guide", [P, D]), m.sb("guide_sq", [P, D])
        guide_norm = m.sb("guide_norm", [P, 3, H])
        eps = m.sb("eps", [P, 1])
        value_bias = m.sb("value_bias", [P, KT])
        parts = m.sb("parts", [P, 3, KT, P])
        sums = m.sb("sums", [P, H * ROWS // P])
        attn = m.sb("attn", [P, KT, P])
        x_rows = m.sb("x_rows", [P, D])
        at_hi, at_lo = m.sb("at_hi", [P, KT, P], F32R), m.sb("at_lo", [P, KT, P], F32R)
        x1, normed = m.sb("x1", [P, D]), m.sb("normed", [P, D])
        nt_hi, nt_lo = m.sb("nt_hi", [P, KT, P], F32R), m.sb("nt_lo", [P, KT, P], F32R)
        stats, moments, std, rstd = m.sb("stats", [P, 6]), m.sb("moments", [P, 2]), m.sb("std", [P, 1]), m.sb("rstd", [P, 1])
        qkv = m.sb("qkv", [P, 3, D])
        q_sq, q_dot = m.sb("q_sq", [P, D]), m.sb("q_dot", [P, D])
        sq_sum, dot_sum = m.sb("sq_sum", [P, H]), m.sb("dot_sum", [P, H])
        q_norm, cosine = m.sb("q_norm", [P, 2, H]), m.sb("cosine", [P, H])
        sim = m.sb("sim", [P, 1])
        qk_hi = [m.sb(f"{name}_hi", [P, KT, P], F32R) for name in ("q", "k")]
        qk_lo = [m.sb(f"{name}_lo", [P, KT, P], F32R) for name in ("q", "k")]
        turned_x, mixed = m.ps("turned_x", [P, KT, P]), m.ps("mixed", [P, D])
        turned_qk = [m.ps(f"turned_{name}", [P, KT, P]) for name in ("q", "k")]
        product = [m.ps(f"product{i}", [P, D]) for i in range(3)]

        consts_in, w_hi_done, w_lo_done = m.sem("consts_in"), m.sem("w_hi_done"), m.sem("w_lo_done")
        w_in = [m.sem(f"w_in{i}") for i in range(2, 4)]
        sums_in, sums_done, inv_stored = m.sem("sums_in"), m.sem("sums_done"), m.sem("inv_stored")
        set_up, act_setup, stats_seen = m.sem("set_up"), m.sem("act_setup"), m.sem("stats_seen")
        a_in, x_in = m.sem("a_in"), m.sem("x_in")
        a_step, a_joined, a_hi, a_lo, a_mixed = m.sem("a_step"), m.sem("a_joined"), m.sem("a_hi"), m.sem("a_lo"), m.sem("a_mixed")
        x1_ready, x1_step, act_std, normed_ready = m.sem("x1_ready"), m.sem("x1_step"), m.sem("act_std"), m.sem("normed_ready")
        n_turned, n_hi, n_lo = m.sem("n_turned"), m.sem("n_hi"), m.sem("n_lo")
        q_full, kv_full, q_out, kv_out = m.sem("q_full"), m.sem("kv_full"), m.sem("q_out"), m.sem("kv_out")
        q_sq_done, q_root, sim_step, sim_ready = m.sem("q_sq_done"), m.sem("q_root"), m.sem("sim_step"), m.sem("sim_ready")
        qk_turned, qk_hi_done, qk_lo_done = m.sem("qk_turned"), m.sem("qk_hi_done"), m.sem("qk_lo_done")
        x1_stored, qk_stored, v_stored, sim_stored = (
            m.sem("x1_stored"), m.sem("qk_stored"), m.sem("v_stored"), m.sem("sim_stored"))

        block = ctx.enter_context(nc.Block())

        @block.sync
        def _(sp):
            by_row = lambda dram: dram.rearrange("h (a n) -> (h a) n", a=P // H)
            sp.dma_start(sums[:], by_row(prob_sums)).then_inc(sums_in, 16)

            def load_weights(n):
                src = w_qkv[:, (n - 1) * D:n * D]
                sp.dma_start(raw[n][:], src.rearrange("(k p) n -> p k n", p=P)).then_inc(w_in[n - 2], 16)

            def load_mix(t):
                for n in range(2):
                    src = mix_parts[n].rearrange("(k p) n -> p k n", p=P)[:, :, bass.ds(t * P, P)]
                    sp.dma_start(parts[:, n, :, :], src).then_inc(a_in, 16)

            def load_inverses(t):
                for j in range(HPT):
                    src = inverses.rearrange("(k a) n -> a k n", a=HPT)[j:j + 1, :, bass.ds(t * P, P)]
                    sp.dma_start(parts[j * HD:(j + 1) * HD, 2, :, :], repeated(src, 0, HD)).then_inc(a_in, 16)

            def load_parts(t):
                load_mix(t)
                load_inverses(t)

            load_mix(0)
            sp.dma_start(value_bias[:], bv.rearrange("(k p) -> p k", p=P), allow_slow_non_contiguous=True
                         ).then_inc(consts_in, 16)
            sp.wait_ge(sums_done, 1)
            sp.dma_start(by_row(inverses), sums[:]).then_inc(inv_stored, 16)
            sp.wait_ge(inv_stored, 16)
            load_inverses(0)
            sp.dma_start(gate[:], row_of(g_xattn, P)).then_inc(consts_in, 16)
            sp.dma_start(gate_bias[:], row_of(bo, P)).then_inc(consts_in, 16)
            sp.dma_start(guide[:], repeated(g_info[0, 0:1, :], 0, P)).then_inc(consts_in, 16)
            sp.dma_start(x_rows[:], x[0:P, :]).then_inc(x_in, 16)
            load_weights(2)
            load_weights(3)

            def load_x(t):
                sp.wait_ge(x1_ready, t)
                sp.dma_start(x_rows[:], x[bass.ds(t * P, P), :]).then_inc(x_in, 16)

            def store_x1(t):
                sp.wait_ge(x1_ready, t + 1)
                sp.dma_start(x1_dram[bass.ds(t * P, P), :], x1[:]).then_inc(x1_stored, 16)

            def store_qk(t):
                sp.wait_ge(qk_hi_done, 2 * t + 2)
                sp.wait_ge(qk_lo_done, 2 * t + 2)
                for n in range(2):
                    for part, tile in enumerate((qk_hi[n], qk_lo[n])):
                        dst = qk_parts[2 * n + part].rearrange("(k p) n -> p k n", p=P)
                        sp.dma_start(dst[:, :, bass.ds(t * P, P)], f32(tile[:])).then_inc(qk_stored, 16)

            def store_values(t):
                sp.wait_ge(sim_ready, t + 1)
                sp.wait_ge(kv_out, 2 * t + 2)
                sp.dma_start(values_dram[bass.ds(t * P, P), :], qkv[:, 2, :]).then_inc(v_stored, 16)
                sp.dma_start(sim_dram[bass.ds(t * P, P), :], sim[:]).then_inc(sim_stored, 16)

            sp.wait_ge(a_joined, 1)
            load_parts(1)
            store_x1(0)
            load_x(1)
            sp.wait_ge(a_joined, 2)
            load_parts(2)

            def body(t, follows=True, more_parts=True):
                if follows:
                    store_qk(t - 1)
                store_x1(t + 1)
                load_x(t + 2)
                if more_parts:
                    sp.wait_ge(a_joined, t + 3)
                    load_parts(t + 3)
                store_values(t)

            body(0, False)
            with sp.Fori(1, TILES - 3) as t:
                body(t)
            body(TILES - 3, more_parts=False)
            store_x1(TILES - 1)
            store_qk(TILES - 3)
            store_values(TILES - 2)
            store_qk(TILES - 2)
            store_values(TILES - 1)
            store_qk(TILES - 1)
            sp.wait_ge(x1_stored, 16 * TILES)
            sp.wait_ge(qk_stored, 64 * TILES)
            sp.wait_ge(v_stored, 16 * TILES)
            sp.wait_ge(sim_stored, 16 * TILES)

        @block.gpsimd
        def _(pool):
            pool.wait_ge(consts_in, 64)

            def join_attn(t, follows):
                step = Tally(a_step, t * A_STEPS)
                pool.wait_ge(a_in, (t + 1) * 16 * A_LOADS)
                if follows:
                    pool.wait_ge(a_hi, t)
                    pool.wait_ge(a_lo, t)
                step.done(pool.tensor_tensor(attn[:], parts[:, 0, :, :], parts[:, 1, :, :], ALU.add))
                step.wait(pool)
                pool.tensor_tensor(attn[:], attn[:], parts[:, 2, :, :], ALU.mult).then_inc(a_joined, 1)
                pool.wait_ge(a_joined, t + 1)
                step.done(pool.tensor_tensor(attn[:], attn[:], repeated(value_bias[:].unsqueeze(2), 2, P), ALU.add))

            join_attn(0, False)
            with pool.Fori(1, TILES) as t:
                join_attn(t, True)

        @block.scalar
        def _(act):
            def split_weights(n):
                if n < 2:
                    act.wait_ge(shared.w_in[n], 32)
                else:
                    act.wait_ge(w_in[n - 2], 16)
                act.activation(w_hi[n][:], raw[n][:], ACT.Copy).then_inc(w_hi_done, 1)

            split_weights(0)
            split_weights(1)
            act.wait_ge(consts_in, 64)
            act.activation(gate[:], gate[:], ACT.Tanh).then_inc(act_setup, 1)
            act.wait_ge(set_up, 2)
            act.activation(guide_norm[:, 1, :], guide_norm[:, 0, :], ACT.Sqrt).then_inc(act_setup, 1)

            def split_attn(t, follows=True):
                act.wait_ge(a_step, t * A_STEPS + A_STEPS)
                if follows:
                    act.wait_ge(a_mixed, t)
                act.activation(at_hi[:], attn[:], ACT.Copy).then_inc(a_hi, 1)

            def root(t):
                act.wait_ge(x1_step, t * X1_STEPS + X1_STEPS - 1)
                act.activation(std[:], moments[:, 1:2], ACT.Sqrt, bias=eps[:]).then_inc(act_std, 1)

            def split_normed(t):
                act.wait_ge(n_turned, t + 1)
                act.activation(nt_hi[:], turned_x[:], ACT.Copy).then_inc(n_hi, 1)

            def queries(t, stored_before):
                act.wait_ge(q_full, t + 1)
                if stored_before:
                    act.wait_ge(sim_ready, t)
                act.activation(q_sq[:], product[0][:], ACT.Square).then_inc(q_sq_done, 1)
                act.activation(qkv[:, 0, :], product[0][:], ACT.Copy).then_inc(q_out, 1)

            def keys(t):
                act.wait_ge(kv_full, 2 * t + 1)
                act.activation(qkv[:, 1, :], product[1][:], ACT.Copy).then_inc(kv_out, 1)

            def values(t, stored_before):
                if stored_before:
                    act.wait_ge(v_stored, 16 * t)
                act.wait_ge(kv_full, 2 * t + 2)
                act.activation(qkv[:, 2, :], product[2][:], ACT.Copy).then_inc(kv_out, 1)

            def query_root(t):
                act.wait_ge(sim_step, t * SIM_STEPS + 2)
                act.activation(q_norm[:, 0, :], sq_sum[:], ACT.Sqrt).then_inc(q_root, 1)

            def split_qk(t, stored_before=True):
                if stored_before:
                    act.wait_ge(qk_stored, 64 * t)
                for n, scale in enumerate((-LOGIT_SCALE, 1.0)):
                    act.wait_ge(qk_turned, 2 * t + n + 1)
                    act.activation(qk_hi[n][:], turned_qk[n][:], ACT.Copy, scale=scale).then_inc(qk_hi_done, 1)

            def body(t, before=2, more_attn=True):
                split_normed(t)
                if before:
                    split_qk(t - 1, before > 1)
                root(t + 1)
                queries(t, before > 0)
                if more_attn:
                    split_attn(t + 2)
                query_root(t)
                keys(t)
                values(t, before > 0)

            split_attn(0, False)
            split_weights(2)
            root(0)
            split_weights(3)
            split_attn(1)
            body(0, 0)
            body(1, 1)
            with act.Fori(2, TILES - 2) as t:
                body(t)
            body(TILES - 2, more_attn=False)
            split_normed(TILES - 1)
            split_qk(TILES - 2)
            queries(TILES - 1, True)
            query_root(TILES - 1)
            keys(TILES - 1)
            values(TILES - 1, True)
            split_qk(TILES - 1)

        @block.vector
        def _(dve):
            dve.wait_ge(sums_in, 16)
            dve.reciprocal(sums[:], sums[:]).then_inc(sums_done, 1)

            def split_weights(n):
                dve.wait_ge(w_hi_done, n + 1)
                dve.tensor_tensor(w_lo[n][:], raw[n][:], w_hi[n][:], ALU.subtract).then_inc(w_lo_done, 1)

            split_weights(0)
            split_weights(1)
            dve.wait_ge(consts_in, 64)
            by_head = guide[:].rearrange("p (h d) -> p h d", d=HD)
            step = Tally(set_up)
            step.done(dve.memset(eps[:], EPS))
            dve.tensor_tensor(guide_sq[:], guide[:], guide[:], ALU.mult).then_inc(sim_step, 1)
            dve.wait_ge(sim_step, 1)
            step.done(dve.tensor_reduce(guide_norm[:, 0, :], guide_sq[:].rearrange("p (h d) -> p h d", d=HD),
                                        AX.X, ALU.add))
            dve.wait_ge(act_setup, 2)
            step.done(dve.reciprocal(guide_norm[:, 2, :], guide_norm[:, 1, :]))
            step.wait(dve)
            step.done(dve.tensor_tensor(by_head, by_head, repeated(guide_norm[:, 2, :].unsqueeze(2), 2, HD), ALU.mult))
            step.done(dve.tensor_scalar(gate_bias[:], gate_bias[:], gate[:], None, ALU.mult))
            step.wait(dve)

            def split_attn(t):
                dve.wait_ge(a_hi, t + 1)
                dve.tensor_tensor(at_lo[:], attn[:], at_hi[:], ALU.subtract).then_inc(a_lo, 1)

            def residual(t, stored_before):
                step = Tally(x1_step, t * X1_STEPS)
                dve.wait_ge(a_mixed, t + 1)
                dve.wait_ge(x_in, t * 16 + 16)
                if stored_before:
                    dve.wait_ge(x1_stored, 16 * t)
                step.done(dve.scalar_tensor_tensor(x1[:], mixed[:], gate[:], x_rows[:], ALU.mult, ALU.add))
                step.wait(dve)
                dve.tensor_tensor(x1[:], x1[:], gate_bias[:], ALU.add).then_inc(x1_ready, 1)
                dve.wait_ge(x1_ready, t + 1)
                step.done(dve.bn_stats(stats[:], x1[:]))
                step.wait(dve)
                dve.sem_inc(stats_seen, 1)
                step.done(dve.bn_aggr(moments[:], stats[:]))
                dve.wait_ge(act_std, t + 1)
                step.done(dve.reciprocal(rstd[:], std[:]))
                step.wait(dve)
                if stored_before:
                    dve.wait_ge(n_turned, t)
                dve.tensor_scalar(normed[:], x1[:], moments[:, 0:1], rstd[:], ALU.subtract, ALU.mult
                                  ).then_inc(normed_ready, 1)

            def split_normed(t):
                dve.wait_ge(n_hi, t + 1)
                dve.tensor_tensor(nt_lo[:], turned_x[:], nt_hi[:], ALU.subtract).then_inc(n_lo, 1)

            def query_sums(t):
                step = Tally(sim_step, t * SIM_STEPS + 1)
                dve.wait_ge(q_sq_done, t + 1)
                step.done(dve.tensor_reduce(sq_sum[:], q_sq[:].rearrange("p (h d) -> p h d", d=HD), AX.X, ALU.add))
                dve.wait_ge(q_out, t + 1)
                step.done(dve.tensor_tensor(q_dot[:], qkv[:, 0, :], guide[:], ALU.mult))
                step.wait(dve)
                step.done(dve.tensor_reduce(dot_sum[:], q_dot[:].rearrange("p (h d) -> p h d", d=HD), AX.X, ALU.add))
                return step

            def similarity(t, step, stored_before):
                dve.wait_ge(q_root, t + 1)
                step.done(dve.reciprocal(q_norm[:, 1, :], q_norm[:, 0, :]))
                step.wait(dve)
                step.done(dve.tensor_tensor(cosine[:], dot_sum[:], q_norm[:, 1, :], ALU.mult))
                step.wait(dve)
                step.done(dve.tensor_scalar(cosine[:], cosine[:], 1.0 / H, None, ALU.mult))
                step.wait(dve)
                if stored_before:
                    dve.wait_ge(sim_stored, 16 * t)
                dve.tensor_reduce(sim[:], cosine[:], AX.X, ALU.add).then_inc(sim_ready, 1)

            def split_qk(t, stored_before=True):
                if stored_before:
                    dve.wait_ge(qk_stored, 64 * t)
                for n, scale in enumerate((-LOGIT_SCALE, 1.0)):
                    dve.wait_ge(qk_hi_done, 2 * t + n + 1)
                    dve.scalar_tensor_tensor(qk_lo[n][:], turned_qk[n][:], scale, qk_hi[n][:], ALU.mult,
                                             ALU.subtract).then_inc(qk_lo_done, 1)

            def body(t, before=2, more_attn=True):
                split_normed(t)
                if before:
                    split_qk(t - 1, before > 1)
                residual(t + 1, True)
                if more_attn:
                    split_attn(t + 2)
                similarity(t, query_sums(t), before > 0)

            split_attn(0)
            split_weights(2)
            residual(0, False)
            split_weights(3)
            split_attn(1)
            body(0, 0)
            body(1, 1)
            with dve.Fori(2, TILES - 2) as t:
                body(t)
            body(TILES - 2, more_attn=False)
            split_normed(TILES - 1)
            split_qk(TILES - 2)
            similarity(TILES - 1, query_sums(TILES - 1), True)
            split_qk(TILES - 1)

        @block.tensor
        def _(pe):
            pe.wait_ge(consts_in, 64)

            def mix_attn(t):
                pe.wait_ge(a_lo, t + 1)
                for k in range(KT):
                    last = three_products(pe, mixed[:], at_hi[:, k, :], at_lo[:, k, :], w_hi[0][:, k, :],
                                          w_lo[0][:, k, :], k == 0, k == KT - 1)
                last.then_inc(a_mixed, 1)

            def turn_normed(t):
                pe.wait_ge(normed_ready, t + 1)
                for k in range(KT):
                    last = pe.transpose(turned_x[:, k, :], normed[:, k * P:(k + 1) * P], ident[:])
                last.then_inc(n_turned, 1)

            def project(n):
                for k in range(KT):
                    last = three_products(pe, product[n][:], nt_hi[:, k, :], nt_lo[:, k, :], w_hi[n + 1][:, k, :],
                                          w_lo[n + 1][:, k, :], k == 0, k == KT - 1)
                last.then_inc(q_full if n == 0 else kv_full, 1)

            def project_all(t, follows):
                pe.wait_ge(n_lo, t + 1)
                if follows:
                    pe.wait_ge(q_out, t)
                project(0)
                if follows:
                    pe.wait_ge(kv_out, 2 * t)
                project(1)
                project(2)

            def turn_qk(t, follows=True):
                pe.wait_ge(q_out, t + 1)
                pe.wait_ge(kv_out, 2 * t + 1)
                if follows:
                    pe.wait_ge(qk_lo_done, 2 * t)
                for n in range(2):
                    for k in range(KT):
                        last = pe.transpose(turned_qk[n][:, k, :], qkv[:, n, k * P:(k + 1) * P], ident[:])
                    last.then_inc(qk_turned, 1)

            def body(t, before=2):
                turn_normed(t)
                if before:
                    turn_qk(t - 1, before > 1)
                mix_attn(t + 1)
                project_all(t, before > 0)

            pe.wait_ge(w_lo_done, 1)
            mix_attn(0)
            pe.wait_ge(w_lo_done, 4)
            body(0, 0)
            body(1, 1)
            with pe.Fori(2, TILES - 1) as t:
                body(t)
            turn_normed(TILES - 1)
            turn_qk(TILES - 2)
            project_all(TILES - 1, True)
            turn_qk(TILES - 1)


SIDE = REG + 1
QR = S + SIDE
PAIRS = B // 2
QUAD = 4
QUADS = B // QUAD
SCORE_ROWS = STACK + 2
QUERIES_AT = S
TW = QUERIES_AT + S + 2 * SIDE
A_PAIR_LOADS = 10


def stage_self(nc, shared, qk_parts, values_dram, sim_dram, x1_dram, table_dram, g_ffn, w_proj, b_proj, fold_dram,
               out):
    with ExitStack() as ctx:
        m = Memory(nc, ctx, "s_")
        ident = shared.ident
        fold = m.sb("fold", [QR, 2, S])
        raw = m.sb("raw", [P, KT, D])
        w_hi, w_lo = m.sb("w_hi", [P, KT, D], F32R), m.sb("w_lo", [P, KT, D], F32R)
        gate, gate_bias = m.sb("gate", [P, 1]), m.sb("gate_bias", [S, D])
        sim = m.sb("sim", [B, S])
        ends, ends_all = m.sb("ends", [B, 2]), m.sb("ends_all", [B, 2])
        low_high = m.sb("low_high", [1, 2])
        ones = m.sb("ones", [1, B])
        spread = m.sb("spread", [B, 2])
        classes = m.sb("classes", [B, 2, S + 2 * SIDE])
        tables = m.sb("tables", [B, 2, TW], F32R)
        q_stack = [m.sb(f"q_stack{i}", [SCORE_ROWS, H, 2 * QR], F32R) for i in range(2)]
        k_stack = [m.sb(f"k_stack{i}", [SCORE_ROWS, H, 2 * S], F32R) for i in range(2)]
        unit_column = m.sb("unit_column", [STACK, 1])
        values = m.sb("values", [S, D])
        x1 = m.sb("x1", [S, D])
        prob = m.sb("prob", [QR, HPT, KT, S])
        shift, total, inv = m.sb("shift", [QR, H]), m.sb("total", [QR, H]), m.sb("inv", [QR, H])
        pt = m.sb("pt", [S, H, QR])
        mixed = m.sb("mixed", [QR, D])
        ot_hi, ot_lo = m.sb("ot_hi", [P, KT, S], F32R), m.sb("ot_lo", [P, KT, S], F32R)
        y = m.sb("y", [S, D])
        scores = m.ps("scores", [P, HPT, 512])
        turned = [m.ps(f"turned{i}", [P, 512]) for i in range(2)]
        mix_bank, proj_bank = m.ps("mix_bank", [P, 512]), m.ps("proj_bank", [P, 512])

        consts_in, w_in = m.sem("consts_in"), m.sem("w_in")
        w_split, gate_ready, bias_ready = m.sem("w_split"), m.sem("gate_ready"), m.sem("bias_ready")
        sim_in, ends_step, ends_turned = m.sem("sim_in"), m.sem("ends_step"), m.sem("ends_turned")
        tables_ready, tables_stored = m.sem("tables_ready"), m.sem("tables_stored")
        pair_in, copies_done = [m.sem(f"pair_in{i}") for i in range(2)], m.sem("copies_done")
        v_in, x1_in = m.sem("v_in"), m.sem("x1_in")
        scored, shift_done, exp_done, inv_done = m.sem("scored"), m.sem("shift_done"), m.sem("exp_done"), m.sem("inv_done")
        p_turned, pt_act, pt_dve = m.sem("p_turned"), m.sem("pt_act"), m.sem("pt_dve")
        mix_full, mixed_done = m.sem("mix_full"), m.sem("mixed_done")
        o_turned, ot_hi_done, ot_lo_done = m.sem("o_turned"), m.sem("ot_hi_done"), m.sem("ot_lo_done")
        biased, proj_full, y_ready, stored = m.sem("biased"), m.sem("proj_full"), m.sem("y_ready"), m.sem("stored")
        cleared = m.sem("cleared")

        block = ctx.enter_context(nc.Block())

        def all_batches(engine, body):
            for i in range(QUAD):
                body(i, min(i, 2), False)
            with engine.Fori(1, QUADS - 1) as u:
                for i in range(QUAD):
                    body(u * QUAD + i, 2, False)
            for i in range(QUAD):
                body(B - QUAD + i, 2, i == QUAD - 1)

        @block.sync
        def _(sp):
            sp.dma_start(sim[:], sim_dram.rearrange("(b s) a -> b (s a)", s=S)).then_inc(sim_in, 16)

            def load_pair(first, buf):
                load_stacks(first, buf)
                load_tables(first, buf)

            def load_stacks(first, buf):
                for stack, parts, at in ((q_stack, (0, 0, 1), SIDE), (k_stack, (2, 3, 2), 0)):
                    for n, part in enumerate(parts):
                        src = qk_parts[part].rearrange("(h d) n -> d h n", d=HD)[:, :, bass.ds(first * S, 2 * S)]
                        sp.dma_start(f32(stack[buf][n * HD:(n + 1) * HD, :, at:at + 2 * S]), src
                                     ).then_inc(pair_in[buf], 16)

            def load_tables(first, buf):
                for odd in range(2):
                    of_batch = table_dram[bass.ds(first + odd, 1)].rearrange("a r n -> r a n")
                    at = QUERIES_AT + odd * SIDE
                    sp.dma_start(f32(k_stack[buf][STACK:SCORE_ROWS, :, odd * S:(odd + 1) * S]),
                                 repeated(of_batch[:, :, 0:S], 1, H)).then_inc(pair_in[buf], 16)
                    sp.dma_start(f32(q_stack[buf][STACK:SCORE_ROWS, :, odd * QR:(odd + 1) * QR]),
                                 repeated(of_batch[:, :, at:at + QR], 1, H)).then_inc(pair_in[buf], 16)

            def load_values(b):
                sp.dma_start(values[:], values_dram[bass.ds(b * S, S), :]).then_inc(v_in, 16)

            def load_x1(b):
                sp.dma_start(x1[:], x1_dram[bass.ds(b * S, S), :]).then_inc(x1_in, 16)

            sp.dma_start(gate[:], row_of(g_ffn, P)).then_inc(consts_in, 16)
            sp.dma_start(gate_bias[:], row_of(b_proj, S)).then_inc(consts_in, 16)
            load_stacks(0, 0)
            sp.wait_ge(tables_ready, 1)
            sp.dma_start(table_dram, f32(tables[:])).then_inc(tables_stored, 16)
            sp.dma_start(fold[:], fold_dram.rearrange("e q s -> q e s")).then_inc(consts_in, 16)
            load_values(0)
            sp.wait_ge(tables_stored, 16)
            load_tables(0, 0)
            sp.dma_start(raw[:], w_proj.rearrange("(k p) n -> p k n", p=P)).then_inc(w_in, 16)
            load_x1(0)
            load_pair(2, 1)

            def store(b):
                sp.wait_ge(y_ready, b + 1)
                sp.dma_start(out[bass.ds(b * S, S), :], y[:]).then_inc(stored, 16)

            def body(b, i, follows=True, more_pairs=True):
                sp.wait_ge(mix_full, b + 1)
                load_values(b + 1)
                if follows:
                    store(b - 1)
                    load_x1(b)
                if i % 2 == 0 and more_pairs:
                    sp.wait_ge(scored, (b + 2) * HPT)
                    load_pair(b + QUAD, (i // 2) % 2)

            for i in range(QUAD):
                body(i, i, i > 0)
            with sp.Fori(1, QUADS - 1) as u:
                for i in range(QUAD):
                    body(u * QUAD + i, i)
            for i in range(QUAD - 1):
                body(B - QUAD + i, i, more_pairs=False)
            store(B - 2)
            load_x1(B - 1)
            store(B - 1)
            sp.wait_ge(stored, 16 * B)

        @block.gpsimd
        def _(pool):
            unit = repeated(repeated(unit_column[:].unsqueeze(2), 1, H), 2, REG)
            for n, (buf, at) in enumerate(((0, REG), (0, 2 * QR - 1), (1, REG), (1, 2 * QR - 1))):
                if n:
                    pool.wait_ge(cleared, n)
                pool.memset(f32(q_stack[buf][0:STACK, :, at:at + 1]), 0.0).then_inc(cleared, 1)
            pool.wait_ge(cleared, 4)
            pool.memset(unit_column[:], 1.0).then_inc(cleared, 1)
            pool.wait_ge(cleared, 5)

            def copy_registers(buf, pairs_before):
                pool.wait_ge(pair_in[buf], (pairs_before + 1) * 16 * A_PAIR_LOADS)
                for to, at in ((0, SIDE), (2 * QR - SIDE, SIDE + S)):
                    rows = q_stack[buf][0:STACK, :, at:at + REG]
                    pool.tensor_tensor(q_stack[buf][0:STACK, :, to:to + REG], rows, unit, ALU.mult
                                       ).then_inc(copies_done, 1)

            pool.wait_ge(bias_ready, 1)
            copy_registers(0, 0)
            copy_registers(1, 0)

            def bias(b):
                pool.wait_ge(x1_in, 16 * b + 16)
                pool.tensor_tensor(x1[:], x1[:], gate_bias[:], ALU.add).then_inc(biased, 1)

            with pool.Fori(0, QUADS - 1) as u:
                for i in range(QUAD):
                    bias(u * QUAD + i)
                    if i % 2 == 0:
                        copy_registers((i // 2) % 2, u + 1)
            for i in range(QUAD):
                bias(B - QUAD + i)

        @block.scalar
        def _(act):
            def exponentials(b, j, follows=True):
                if j == 0 and follows:
                    act.wait_ge(inv_done, b)
                act.wait_ge(shift_done, b * HPT + j + 1)
                for k in range(KT):
                    at = j * KT + k
                    last = act.activation(prob[:, j, k, :], scores[0:QR, j, k * S:(k + 1) * S], ACT.Exp,
                                          bias=shift[:, at:at + 1], scale=-1.0, accum_out=total[:, at:at + 1])
                last.then_inc(exp_done, 1)

            def turn_back(b, n):
                act.wait_ge(p_turned, b * HPT + n + 1)
                act.activation(pt[:, n * HPT:(n + 1) * HPT, :],
                               turned[0][0:S, 0:HPT * QR].rearrange("p (j q) -> p j q", j=HPT), ACT.Copy
                               ).then_inc(pt_act, 1)

            def body(b, before, last):
                turn_back(b, 2)
                if not last:
                    for j in range(HPT):
                        exponentials(b + 1, j)

            act.wait_ge(consts_in, 48)
            act.activation(gate[:], gate[:], ACT.Tanh).then_inc(gate_ready, 1)
            act.wait_ge(w_in, 16)
            act.activation(w_hi[:], raw[:], ACT.Copy).then_inc(w_split, 1)
            for j in range(HPT):
                exponentials(0, j, False)
            all_batches(act, body)

        @block.vector
        def _(dve):
            step = Tally(ends_step)
            dve.wait_ge(sim_in, 16)
            step.done(dve.memset(ones[:], 1.0))
            step.done(dve.tensor_reduce(ends[:, 0:1], sim[:, REG:S], AX.X, ALU.min))
            step.done(dve.tensor_reduce(ends[:, 1:2], sim[:, REG:S], AX.X, ALU.max))
            dve.wait_ge(ends_turned, 1)
            step.done(dve.tensor_reduce(low_high[:, 0:1], mix_bank[0:1, 0:B], AX.X, ALU.min))
            step.done(dve.tensor_reduce(low_high[:, 1:2], mix_bank[0:1, B:2 * B], AX.X, ALU.max))
            dve.wait_ge(ends_turned, 2)
            step.done(dve.tensor_copy(ends_all[:], proj_bank[0:B, 0:2]))
            step.wait(dve)
            step.done(dve.tensor_tensor(spread[:, 0:1], ends_all[:, 1:2], ends_all[:, 0:1], ALU.subtract))
            step.done(dve.memset(classes[:, 0, :], 0.0))
            step.wait(dve)
            step.done(dve.reciprocal(spread[:, 1:2], spread[:, 0:1]))
            step.wait(dve)
            step.done(dve.tensor_scalar(sim[:], sim[:], ends_all[:, 0:1], spread[:, 1:2], ALU.subtract, ALU.mult))
            step.wait(dve)
            step.done(dve.tensor_scalar(classes[:, 0, SIDE:SIDE + S], sim[:], THRESHOLD, None, ALU.is_gt))
            step.wait(dve)
            step.done(dve.memset(classes[:, 0, SIDE:SIDE + REG], 1.0))
            step.wait(dve)
            step.done(dve.tensor_scalar(classes[:, 1, :], classes[:, 0, :], -1.0, 1.0, ALU.mult, ALU.add))
            step.wait(dve)
            step.done(dve.tensor_copy(tables[:, :, QUERIES_AT:TW], classes[:]))
            step.done(dve.tensor_scalar(tables[:, 0, 0:S], classes[:, 1, SIDE:SIDE + S], MASKED, None, ALU.mult))
            step.done(dve.tensor_scalar(tables[:, 1, 0:S], classes[:, 0, SIDE:SIDE + S], MASKED, None, ALU.mult))
            step.wait(dve)
            dve.memset(f32(tables[:, :, 0:REG]), 0.0).then_inc(tables_ready, 1)
            dve.wait_ge(gate_ready, 1)
            dve.tensor_scalar(gate_bias[:], gate_bias[:], gate[0:S, :], None, ALU.mult).then_inc(bias_ready, 1)

            def shifts(b):
                for j in range(HPT):
                    dve.wait_ge(scored, b * HPT + j + 1)
                    dve.tensor_reduce(shift[:, j * KT:(j + 1) * KT],
                                      scores[0:QR, j, 0:KT * S].rearrange("p (k s) -> p k s", k=KT), AX.X, ALU.min
                                      ).then_inc(shift_done, 1)

            def invert(b):
                dve.wait_ge(exp_done, b * HPT + HPT)
                dve.reciprocal(inv[:], total[:]).then_inc(inv_done, 1)

            def turn_back(b, n):
                dve.wait_ge(p_turned, b * HPT + n + 1)
                dve.tensor_copy(pt[:, n * HPT:(n + 1) * HPT, :],
                                turned[n % 2][0:S, 0:HPT * QR].rearrange("p (j q) -> p j q", j=HPT)
                                ).then_inc(pt_dve, 1)

            def weigh(b):
                dve.wait_ge(mix_full, b + 1)
                dve.wait_ge(inv_done, b + 1)
                dve.tensor_tensor(mixed[:].rearrange("p (m a d) -> p m a d", a=HPT, d=HD),
                                  mix_bank[0:QR, :].rearrange("p (m a d) -> p m a d", a=HPT, d=HD),
                                  repeated(inv[:].rearrange("p (a m) -> p m a", m=KT).unsqueeze(3), 3, HD),
                                  ALU.mult).then_inc(mixed_done, 1)

            def split_mix(b):
                dve.wait_ge(o_turned, b + 1)
                dve.tensor_copy(ot_hi[:], turned[1][:, 0:KT * S].rearrange("p (k s) -> p k s", k=KT)
                                ).then_inc(ot_hi_done, 1)
                dve.wait_ge(ot_hi_done, b + 1)
                dve.tensor_tensor(ot_lo[:], turned[1][:, 0:KT * S].rearrange("p (k s) -> p k s", k=KT), ot_hi[:],
                                  ALU.subtract).then_inc(ot_lo_done, 1)

            def result(b, stored_before=True):
                dve.wait_ge(proj_full, b + 1)
                dve.wait_ge(biased, b + 1)
                if stored_before:
                    dve.wait_ge(stored, 16 * b)
                dve.scalar_tensor_tensor(y[:], proj_bank[0:S, :], gate[0:S, :], x1[:], ALU.mult, ALU.add
                                         ).then_inc(y_ready, 1)

            def body(b, before, last):
                turn_back(b, 1)
                turn_back(b, 3)
                invert(b)
                weigh(b)
                if before:
                    result(b - 1, before > 1)
                if not last:
                    shifts(b + 1)
                split_mix(b)
                if not last:
                    turn_back(b + 1, 0)

            dve.wait_ge(w_split, 1)
            dve.tensor_tensor(w_lo[:], raw[:], w_hi[:], ALU.subtract).then_inc(w_split, 1)
            shifts(0)
            turn_back(0, 0)
            all_batches(dve, body)
            result(B - 1)

        @block.tensor
        def _(pe):
            pe.wait_ge(ends_step, 3)
            pe.transpose(mix_bank[0:1, 0:B], ends[:, 0:1], ident[0:B, 0:B])
            pe.transpose(mix_bank[0:1, B:2 * B], ends[:, 1:2], ident[0:B, 0:B]).then_inc(ends_turned, 1)
            pe.wait_ge(ends_step, 5)
            pe.matmul(proj_bank[0:B, 0:2], ones[:], low_high[:], start=True, stop=True).then_inc(ends_turned, 1)
            pe.wait_ge(ends_step, 6)
            pe.wait_ge(consts_in, 48)
            pe.wait_ge(cleared, 4)

            def score(b, i, pairs_before):
                buf, odd = i // 2, i % 2
                if not odd:
                    pe.wait_ge(pair_in[buf], (pairs_before + 1) * 16 * A_PAIR_LOADS)
                    pe.wait_ge(copies_done, 4 * pairs_before + 2 * buf + 2)
                for j in range(HPT):
                    for k in range(KT):
                        h = k * HPT + j
                        last = pe.matmul(scores[0:QR, j, k * S:(k + 1) * S], q_stack[buf][:, h, odd * QR:(odd + 1) * QR],
                                         k_stack[buf][:, h, odd * S:(odd + 1) * S], start=True, stop=True)
                    last.then_inc(scored, 1)

            def turn_probs(b, n):
                pe.wait_ge(exp_done, b * HPT + n + 1)
                for k in range(KT):
                    last = pe.transpose(turned[n % 2][0:S, k * QR:(k + 1) * QR], prob[:, n, k, :],
                                        ident[0:QR, 0:QR])
                last.then_inc(p_turned, 1)

            def mix(b, n):
                for k in range(KT):
                    cols = slice((k * HPT + n) * HD, (k * HPT + n + 1) * HD)
                    last = pe.matmul(mix_bank[0:QR, cols], pt[:, n * KT + k, :], values[:, cols],
                                     start=True, stop=True)
                if n == HPT - 1:
                    last.then_inc(mix_full, 1)

            def fold_mix(b, i):
                pe.wait_ge(mixed_done, b + 1)
                for k in range(KT):
                    last = pe.matmul(turned[1][:, k * S:(k + 1) * S], mixed[:, k * P:(k + 1) * P], fold[:, i % 2, :],
                                     start=True, stop=True)
                last.then_inc(o_turned, 1)

            def project(b, half, follows=True):
                if half == 0:
                    pe.wait_ge(ot_lo_done, b + 1)
                    if follows:
                        pe.wait_ge(y_ready, b)
                for k in range(half * KT // 2, (half + 1) * KT // 2):
                    last = three_products(pe, proj_bank[0:S, :], ot_hi[:, k, :], ot_lo[:, k, :], w_hi[:, k, :],
                                          w_lo[:, k, :], k == 0, k == KT - 1)
                if half:
                    last.then_inc(proj_full, 1)

            def body(b, i, follows, last, step):
                turn_probs(b, 1)
                pe.wait_ge(pt_dve, 3 * b + 1)
                turn_probs(b, 2)
                pe.wait_ge(v_in, 16 * b + 16)
                mix(b, 0)
                pe.wait_ge(pt_dve, 3 * b + 2)
                turn_probs(b, 3)
                mix(b, 1)
                pe.wait_ge(pt_act, b + 1)
                mix(b, 2)
                pe.wait_ge(pt_dve, 3 * b + 3)
                mix(b, 3)
                if follows:
                    project(b - 1, 1)
                if not last:
                    at = (i + 1) % QUAD
                    score(b + 1, at, step + (i + 1) // QUAD)
                fold_mix(b, i)
                if not last:
                    turn_probs(b + 1, 0)
                project(b, 0, follows)
                if last:
                    project(b, 1)

            score(0, 0, 0)
            pe.wait_ge(w_split, 2)
            turn_probs(0, 0)
            for i in range(QUAD):
                body(i, i, i > 0, False, 0)
            with pe.Fori(1, QUADS - 1) as u:
                for i in range(QUAD):
                    body(u * QUAD + i, i, True, False, u)
            for i in range(QUAD):
                body(B - QUAD + i, i, True, i == QUAD - 1, QUADS - 1)


def flamingo_block(nc, x, ctx_1024, g_xattn, g_ffn, wq, bq, wk, bk, wv, bv, wo, bo, g_info, w_qkv, w_proj, b_proj,
                   ident, neg_ident, fold, out):
    q_parts = nc.dram_tensor("q_parts", [2, D, ROWS], F32).ap()
    mix_parts = nc.dram_tensor("mix_parts", [2, D, ROWS], F32).ap()
    prob_sums = nc.dram_tensor("prob_sums", [H, ROWS], F32).ap()
    inverses = nc.dram_tensor("inverses", [H, ROWS], F32).ap()
    x1 = nc.dram_tensor("x1", [ROWS, D], F32).ap()
    qk_parts = nc.dram_tensor("qk_parts", [4, D, ROWS], F32).ap()
    values = nc.dram_tensor("values", [ROWS, D], F32).ap()
    sim = nc.dram_tensor("sim", [ROWS, 1], F32).ap()
    tables = nc.dram_tensor("tables", [B, 2, TW], F32).ap()
    x_rows = x.rearrange("b s d -> (b s) d")
    with ExitStack() as ctx:
        shared = Shared(nc, ctx)
        stage_queries(nc, shared, x, wq, bq, ident, q_parts, ctx_1024, wk, wv)
        stage_cross(nc, shared, ctx_1024, bk, neg_ident, q_parts, mix_parts, prob_sums, (wo, w_qkv[:, 0:D]))
        stage_rows(nc, shared, x_rows, mix_parts, prob_sums, inverses, bv, g_xattn, bo, g_info, w_qkv, x1, qk_parts,
                   values, sim)
        stage_self(nc, shared, qk_parts, values, sim, x1, tables, g_ffn, w_proj, b_proj, fold,
                   out.rearrange("b s d -> (b s) d"))


INPUTS = ["x", "ctx_1024", "g_xattn", "g_ffn", "L0_xattn_wq", "L0_xattn_bq", "L0_xattn_wk", "L0_xattn_bk",
          "L0_xattn_wv", "L0_xattn_bv", "L0_xattn_wo", "L0_xattn_bo", "L0_ffn_g_info", "L0_ffn_W_qkv",
          "L0_ffn_W_proj", "L0_ffn_b_proj"]


def kernel(**inputs):
    import concourse.bacc as bacc
    from concourse.bass_utils import run_bass_kernel_spmd

    fold = np.zeros((2, QR, S), np.float32)
    for odd in range(2):
        rows, copies = (0, S) if odd else (SIDE, 0)
        for q in range(S):
            fold[odd, rows + q, q] = 0.5 if q < REG else 1.0
        for q in range(REG):
            fold[odd, copies + q, q] = 0.5
    arrays = {name: np.ascontiguousarray(inputs[name]) for name in INPUTS}
    arrays |= {"ident": np.eye(P, dtype=np.float32), "neg_ident": -np.eye(HPT, dtype=np.float32),
               "fold": fold}
    nc = bacc.Bacc("TRN2", target_bir_lowering=False, num_devices=1)
    args = [nc.dram_tensor(f"in_{name}", a.shape, mybir.dt.from_np(a.dtype), kind="ExternalInput").ap()
            for name, a in arrays.items()]
    out = nc.dram_tensor("out", (B, S, D), F32, kind="ExternalOutput").ap()
    flamingo_block(nc, *args, out)
    result = run_bass_kernel_spmd(nc, [{f"in_{name}": a for name, a in arrays.items()}], core_ids=[0])
    return result.results[0]["out"]
```
